# Optimizing a Trainium2 kernel written in Bass

```python
import numpy as np
import jax
import jax.numpy as jnp

def _softmax(x, axis=-1):
    return jax.nn.softmax(x, axis=axis)

def _gelu(x):
    return jax.nn.gelu(x, approximate=True)

def _silu(x):
    return jax.nn.silu(x)

def _sigmoid(x):
    return jax.nn.sigmoid(x)

def _layernorm(x, axis=-1, eps=1e-05):
    m = jnp.mean(x, axis=axis, keepdims=True)
    v = jnp.var(x, axis=axis, keepdims=True)
    return (x - m) / jnp.sqrt(v + eps)

def _scatter_add(tgt, idx, src, axis=0):
    return tgt.at[idx].add(src)

def _segment_sum(src, seg, n):
    return jax.ops.segment_sum(src, seg, n)
kernel_name = 'mk_flamingo_gated_d1_seqx_r8_59b17f'

def setup_inputs(seed: int=0):
    np.random.seed(seed)
    _w = jnp.asarray

    def _rec_inputs():
        import jax
        import jax.numpy as jnp
        _rk = jax.random.key(seed)
        x = -0.0003929 + 0.9999 * jax.random.normal(jax.random.fold_in(_rk, 1), (64, 64, 256), jnp.float32)
        _lenS = 64 - jax.random.randint(jax.random.fold_in(_rk, 7), (64,), 0, max(1, 64 // 4) + 1, jnp.int32)
        _lenS2 = 64 - jax.random.randint(jax.random.fold_in(_rk, 8), (64,), 0, max(1, 64 // 4) + 1, jnp.int32)
        _ctx_1024P = jax.random.normal(jax.random.fold_in(_rk, 11), (64, 16, 128), jnp.float32)
        _ctx_1024c = jax.random.dirichlet(jax.random.fold_in(_rk, 511), 0.3 * jnp.ones((16,), jnp.float32), (64, 64))
        _ctx_1024t = jnp.einsum('bsk,bkd->bsd', _ctx_1024c, _ctx_1024P)
        _ctx_1024t = _ctx_1024t * jax.lax.rsqrt(jnp.mean(jnp.square(_ctx_1024t)) + 1e-12) * 0.953939
        ctx_1024 = -0.000494167 + 1.00018 * (_ctx_1024t + 0.3 * jax.random.normal(jax.random.fold_in(_rk, 611), (64, 64, 128), jnp.float32))
        _validS = jnp.arange(64)[None, :] < _lenS[:, None]
        _validS2 = jnp.arange(64)[None, :] < _lenS2[:, None]
        _causal = jnp.tril(jnp.ones((64, 64), dtype=bool))
        mask_BxS2_bf1 = jnp.ones((64, 64), dtype=bool)
        _g = jax.random.normal(jax.random.fold_in(_rk, 9001), (2, 1), jnp.float32)
        _g = jnp.sign(_g) * jnp.maximum(jnp.abs(_g), 1.0) + (_g == 0) * 1.0
        g_xattn = _g[0]
        g_ffn = _g[1]
        return (x, ctx_1024, mask_BxS2_bf1, g_xattn, g_ffn)
    x, ctx_1024, mask_BxS2_bf1, g_xattn, g_ffn = _rec_inputs()

    def _L0_xattn_setup():
        import jax, jax.numpy as jnp
        import numpy as np
        N_HEADS = 16
        N_KV_HEADS = 8
        HEAD_DIM = 128
        D_TEXT = 256
        D_VISION = 128
        GROUPS = N_HEADS // N_KV_HEADS
        key = jax.random.key(seed)
        ks = jax.random.split(key, 6)
        B, T_text, T_vis = (4, 256, 72)
        text_hidden = jax.random.normal(ks[0], (B, T_text, D_TEXT), dtype=jnp.float32)
        vision_tokens = jax.random.normal(ks[1], (B, T_vis, D_VISION), dtype=jnp.float32)
        vision_mask = jnp.ones((B, T_vis), dtype=bool)
        s = 0.02
        Wq = jax.random.normal(ks[2], (D_TEXT, N_HEADS * HEAD_DIM), dtype=jnp.float32) * s
        Wk = jax.random.normal(ks[3], (D_VISION, N_KV_HEADS * HEAD_DIM), dtype=jnp.float32) * s
        Wv = jax.random.normal(ks[4], (D_VISION, N_KV_HEADS * HEAD_DIM), dtype=jnp.float32) * s
        Wo = jax.random.normal(ks[5], (N_HEADS * HEAD_DIM, D_TEXT), dtype=jnp.float32) * s
        return {'text_hidden': text_hidden, 'vision_tokens': vision_tokens, 'vision_mask': vision_mask, 'Wq': Wq, 'Wk': Wk, 'Wv': Wv, 'Wo': Wo}
    _L0_xattn_all = _L0_xattn_setup()
    _L0_xattn_in = {k: v for k, v in _L0_xattn_all.items() if k in ('Wq', 'Wk', 'Wv', 'Wo')}
    del _L0_xattn_all

    def _L0_ffn_setup():
        import jax, jax.numpy as jnp
        import numpy as np
        NUM_EXPERTS = 8
        TOP_K = 2
        HIDDEN = 256
        INTER = 352
        BSZ, SEQ = (4, 256)
        key = jax.random.key(seed)
        ks = jax.random.split(key, 6)
        s = 0.02
        return {'hidden_states': jax.random.normal(ks[0], (BSZ, SEQ, HIDDEN), jnp.float32), 'gate_w': jax.random.normal(ks[1], (NUM_EXPERTS, HIDDEN), jnp.float32) * s, 'gate_b': jnp.zeros((NUM_EXPERTS,), jnp.float32), 'expert_bias': jax.random.normal(ks[2], (NUM_EXPERTS,), jnp.float32) * 0.01, 'w_gate_up': jax.random.normal(ks[3], (NUM_EXPERTS, 2 * INTER, HIDDEN), jnp.float32) * s, 'w_down': jax.random.normal(ks[4], (NUM_EXPERTS, HIDDEN, INTER), jnp.float32) * s}
    _L0_ffn_all = _L0_ffn_setup()
    _L0_ffn_in = {k: v for k, v in _L0_ffn_all.items() if k in ('gate_w', 'gate_b', 'expert_bias', 'w_gate_up', 'w_down')}
    del _L0_ffn_all
    return {'x': x, 'ctx_1024': ctx_1024, 'mask_BxS2_bf1': mask_BxS2_bf1, 'g_xattn': g_xattn, 'g_ffn': g_ffn, 'L0_xattn_Wq': _L0_xattn_in['Wq'], 'L0_xattn_Wk': _L0_xattn_in['Wk'], 'L0_xattn_Wv': _L0_xattn_in['Wv'], 'L0_xattn_Wo': _L0_xattn_in['Wo'], 'L0_ffn_gate_w': _L0_ffn_in['gate_w'], 'L0_ffn_gate_b': _L0_ffn_in['gate_b'], 'L0_ffn_expert_bias': _L0_ffn_in['expert_bias'], 'L0_ffn_w_gate_up': _L0_ffn_in['w_gate_up'], 'L0_ffn_w_down': _L0_ffn_in['w_down']}

def reference(x, ctx_1024, mask_BxS2_bf1, g_xattn, g_ffn, L0_xattn_Wq, L0_xattn_Wk, L0_xattn_Wv, L0_xattn_Wo, L0_ffn_gate_w, L0_ffn_gate_b, L0_ffn_expert_bias, L0_ffn_w_gate_up, L0_ffn_w_down):
    import jax
    import jax.numpy as jnp

    def _L0_xattn_ref(text_hidden, vision_tokens, vision_mask, Wq, Wk, Wv, Wo):
        import jax, jax.numpy as jnp
        import numpy as np
        N_HEADS = 16
        N_KV_HEADS = 8
        HEAD_DIM = 128
        D_TEXT = 256
        D_VISION = 128
        GROUPS = N_HEADS // N_KV_HEADS
        B, T_text, _ = text_hidden.shape
        T_vis = vision_tokens.shape[1]
        scale = jnp.float32(np.sqrt(HEAD_DIM))
        q = (text_hidden @ Wq).reshape(B, T_text, N_HEADS, HEAD_DIM).transpose(0, 2, 1, 3)
        k = (vision_tokens @ Wk).reshape(B, T_vis, N_KV_HEADS, HEAD_DIM).transpose(0, 2, 1, 3)
        v = (vision_tokens @ Wv).reshape(B, T_vis, N_KV_HEADS, HEAD_DIM).transpose(0, 2, 1, 3)
        k = jnp.repeat(k, GROUPS, axis=1)
        v = jnp.repeat(v, GROUPS, axis=1)
        scores = jnp.einsum('bhtd,bhsd->bhts', q, k) / scale
        mask = vision_mask[:, None, None, :]
        scores = jnp.where(mask, scores, -jnp.inf)
        attn = jax.nn.softmax(scores, axis=-1)
        attn = jnp.nan_to_num(attn, nan=0.0)
        out = jnp.einsum('bhts,bhsd->bhtd', attn, v)
        out = out.transpose(0, 2, 1, 3).reshape(B, T_text, N_HEADS * HEAD_DIM)
        return out @ Wo

    def _L0_ffn_ref(hidden_states, gate_w, gate_b, expert_bias, w_gate_up, w_down):
        import jax, jax.numpy as jnp
        import numpy as np
        NUM_EXPERTS = 8
        TOP_K = 2
        HIDDEN = 256
        INTER = 352
        BSZ, SEQ = (4, 256)
        bsz, seq_len, hidden_dim = hidden_states.shape
        x = hidden_states.reshape(-1, hidden_dim)
        T = x.shape[0]
        E = w_gate_up.shape[0]
        router_logits = x @ gate_w.T + gate_b
        routing = jax.nn.softmax(router_logits.astype(jnp.float32), axis=-1)
        routing = routing + expert_bias.astype(jnp.float32)
        topk_w, topk_idx = jax.lax.top_k(routing, TOP_K)
        topk_w = topk_w.astype(x.dtype)
        comb = jnp.zeros((T, E), x.dtype).at[jnp.arange(T)[:, None], topk_idx].add(topk_w)
        out = jnp.zeros_like(x)
        for e in range(E):
            gate_up = x @ w_gate_up[e].T
            g, u = jnp.split(gate_up, 2, axis=1)
            inter = jax.nn.silu(g) * u
            out = out + inter @ w_down[e].T * comb[:, e:e + 1]
        return out.reshape(bsz, seq_len, hidden_dim)
    x = x + jnp.tanh(g_xattn[0]) * _L0_xattn_ref(_layernorm(x, axis=-1), ctx_1024, mask_BxS2_bf1, L0_xattn_Wq, L0_xattn_Wk, L0_xattn_Wv, L0_xattn_Wo)
    x = x + jnp.tanh(g_ffn[0]) * _L0_ffn_ref(_layernorm(x, axis=-1), L0_ffn_gate_w, L0_ffn_gate_b, L0_ffn_expert_bias, L0_ffn_w_gate_up, L0_ffn_w_down)
    return x

_drawn_inputs = setup_inputs


def setup_inputs(seed=0):
    import zlib

    import numpy as np

    out = dict(_drawn_inputs(seed))
    spreads = {'L0_ffn_gate_b': (0.0, 0.8)}
    factors = {'L0_xattn_Wq': 8.0,
     'L0_xattn_Wk': 8.0,
     'L0_ffn_gate_w': 8.0,
     'L0_ffn_expert_bias': 8.0,
     'L0_ffn_w_gate_up': 8.0,
     'L0_ffn_w_down': 8.0}
    for name, (base, spread) in spreads.items():
        noise = np.random.default_rng([zlib.crc32(name.encode()), seed]).standard_normal(out[name].shape)
        drawn = base * np.exp(spread * noise) if base else spread * noise
        out[name] = jnp.asarray(drawn.astype(out[name].dtype))
    for name, factor in factors.items():
        out[name] = (out[name] * factor).astype(out[name].dtype)
    return out
```

```python
from contextlib import ExitStack

import concourse.bass as bass
from concourse import mybir

F32 = mybir.dt.float32
F16 = mybir.dt.float16
I32 = mybir.dt.int32
U8 = mybir.dt.uint8
ALU = mybir.AluOpType
ACT = mybir.ActivationFunctionType
AX_X = mybir.AxisListType.X

P = 128


def bass_flamingo_gated_block(
    nc: bass.Bass,
    x: bass.AP,
    ctx: bass.AP,
    ctx_t: bass.AP,
    mask: bass.AP,
    g_xattn: bass.AP,
    g_ffn: bass.AP,
    wq_t: bass.AP,
    wk_t: bass.AP,
    wv_t: bass.AP,
    wo: bass.AP,
    gate_w_t: bass.AP,
    gate_b: bass.AP,
    expert_bias: bass.AP,
    w_gu_t: bass.AP,
    w_down_t: bass.AP,
    out: bass.AP,
):
    B, T, D = x.shape
    S, C = ctx.shape[1:]
    H = wq_t.shape[0] // P
    KV = wk_t.shape[0] // P
    E, _, GU = w_gu_t.shape
    F = GU // 2
    KC = D // P
    TILES = B * T // P
    J = 4
    G = TILES // J
    NB = J * P // T
    GT = J * P
    Q = 4
    HU = H // Q
    HP = HU // 2
    FC = [(0, 128), (128, 128), (256, F - 256)]
    NF = len(FC)
    EPS = 1e-5
    LN_SCALE = 1024.0
    TOP = 14
    NEG = -1.0e30
    assert T == S == 64 and C == P and D == 256 and KC == 2

    x_tiles = x.rearrange("b t d -> (b t) d").rearrange("(g j p) d -> g p j d", j=J, p=P)
    out_tiles = out.rearrange("b t d -> (b t) d").rearrange("(g j p) d -> g p j d", j=J, p=P)
    ctx_tiles = ctx.rearrange("b s c -> (b s) c").rearrange("(g j p) c -> g p j c", j=J, p=P)
    ctx_t_groups = ctx_t.rearrange("c (g n) -> g c n", g=G)
    mask_groups = mask.rearrange("b s -> (b s)").rearrange("(g a n) -> g a n", g=G, a=1)

    es = ExitStack()
    with es:
        def sb(name, shape, dt=F32):
            return es.enter_context(nc.sbuf_tensor(name, shape, dt))

        def sem(name):
            return es.enter_context(nc.semaphore(name))

        x_res = sb("x_res", [P, TILES, D])
        m_hi = sb("m_hi", [P, KC, H, C], F16)
        m_lo = sb("m_lo", [P, KC, H, C], F16)
        n_hi = sb("n_hi", [P, H, D], F16)
        n_lo = sb("n_lo", [P, H, D], F16)
        ident = sb("ident", [P, P])
        ones = sb("ones", [32, P])
        xn = sb("xn", [P, J, D])
        mean_var = sb("mean_var", [P, TILES, 2])
        stats = sb("stats", [P, TILES, 6])
        rstd = sb("rstd", [P, TILES])
        nwt = sb("nwt", [P, 3, TILES])
        NM = 3 + 2 * E
        mx_part = sb("mx_part", [P, NM])
        mx_col = sb("mx_col", [32, 1])
        mx_diag = sb("mx_diag", [32, NM])
        mx_exp = sb("mx_exp", [P, NM], I32)
        scale_of = sb("scale_of", [P, NM])
        inv_of = sb("inv_of", [P, NM])
        gates = sb("gates", [P, 2])
        consts = sb("consts", [P, 8])
        PH1 = 8 * 1024
        ffn_w = sb("ffn_w", [P, E * (2 * KC * GU + 2 * 3 * D) // 2])
        stage = ffn_w[:, 0:14336]
        work = sb("work", [P, PH1])

        banks = es.enter_context(nc.psum_tensor("banks", [P, 8, 512], F32))
        acc = banks[:, 0:2, :].rearrange("p b n -> p (b n)").rearrange("p (j d) -> p j d", j=J)
        sp_ps = banks[:, 2:4, :]
        xo_ps = banks[:, 4:8, :]

        wq_s = stage[:, 0:H * D].rearrange("p (h d) -> p h d", h=H)
        wk_s = stage[:, 4096:4096 + KV * C].rearrange("p (h c) -> p h c", h=KV)
        wv_s = stage[:, 5120:5120 + KV * C].rearrange("p (h c) -> p h c", h=KV)
        wo_s = stage[:, 6144:6144 + H * D].rearrange("p (h d) -> p h d", h=H)
        ctx_all = stage[:, 10240:10240 + TILES * C]
        mf = work[:, 0:4096].rearrange("p (k h c) -> p k h c", k=KC, h=H)
        nf = work[:, 4096:8192].rearrange("p (h d) -> p h d", h=H)
        at = 0

        def take(words):
            nonlocal at
            at += words
            assert at <= PH1
            return work[:, at - words:at]

        xm = [take(HU * GT).rearrange("p (a b c t) -> p a c b t", a=HP, b=NB, c=2) for _ in range(2)]
        sm = take(HP * GT).rearrange("p (a n) -> p a n", a=HP)
        pr = pn = sm
        pt = take(HP * GT).rearrange("p (j a n) -> p j a n", j=J, a=HP)
        o_hi = take(HU * GT // 2).bitcast(F16).rearrange("p (h n) -> p h n", h=HU)
        o_lo = take(HU * GT // 2).bitcast(F16).rearrange("p (h n) -> p h n", h=HU)
        ctx_t_s = [sb(f"ctx_t_s{i}", [P, GT]) for i in range(2)]
        ctx_s = [sb(f"ctx_s{i}", [P, J, C]) for i in range(2)]
        mask_u = [sb(f"mask_u{i}", [P, GT], U8) for i in range(2)]
        mask_b = [sb(f"mask_b{i}", [P, GT]) for i in range(2)]
        any_of = [sb(f"any_of{i}", [P, NB]) for i in range(2)]
        xt_hi = [sb(f"xt_hi{i}", [P, KC, GT], F16) for i in range(2)]
        xt_lo = [sb(f"xt_lo{i}", [P, KC, GT], F16) for i in range(2)]
        nmax = sb("nmax", [P, HP * NB])
        rsum = sb("rsum", [P, HP * NB])
        rinv = sb("rinv", [P, HP * NB])


        def by_batch(hh):
            return xo_ps[:, hh, :].rearrange("p (b t) -> p b t", b=NB)

        def o_view(o, bank):
            half, b2 = bank // 2, bank % 2
            return o.rearrange("p h (j b t) -> p h j b t", j=J, b=2)[:, :, 2 * half:2 * half + 2, b2, :]

        s_x = [sem(f"x_loaded{g}") for g in range(G)]
        s_w = [sem(f"setup_weights_loaded{i}") for i in range(5)]
        s_g = sem("gates_loaded")
        s_ident = sem("ident_ready")
        s_ctx = [sem(f"ctx_loaded{i}") for i in range(2)]
        s_dve = sem("dve_setup_step")
        s_act = sem("act_setup_step")
        s_stat = sem("ln1_rstd_ready")
        s_var = sem("ln1_variance_ready")
        s_mxp = sem("partial_maxima_ready")
        s_mprod = sem("m_product_done")
        s_mcopied = sem("m_product_copied")
        s_nprod = sem("n_product_done")
        s_ncopied = sem("n_product_copied")
        s_maxt = sem("maxima_transposed")
        s_maxd = sem("maxima_diagonal")
        s_maxb = sem("maxima_broadcast")
        s_scale = sem("scales_ready")
        s_wready = sem("m_n_split")
        s_tanh = sem("tanh_ready")
        s_xnorm = sem("x_normalised")
        s_xt = sem("x_transposed")
        s_xth = sem("xt_high_ready")
        s_xtl = sem("xt_low_ready")
        s_cscale = sem("ctx_scaled")
        s_mbias = sem("mask_bias_ready")
        s_manyof = sem("mask_any_ready")
        s_xm = sem("xm_head_done")
        s_xma = sem("xm_copied_by_act")
        s_xmd = sem("xm_copied_by_dve")
        s_sc = sem("scores_done")
        s_msk = sem("scores_masked")
        s_max = sem("row_max_ready")
        s_exp = sem("exp_done")
        s_ri = sem("row_inverse_step")
        s_pn = sem("probs_normalised")
        s_pt = sem("probs_transposed")
        s_pta = sem("pt_copied_by_act")
        s_ptd = sem("pt_copied_by_dve")
        s_pv = sem("head_outputs_done")
        s_oh = sem("outputs_high_ready")
        s_ol = sem("outputs_low_ready")
        s_on = sem("projection_done")
        s_x1 = sem("x1_ready")

        def link(eng, sem_, chain, ins):
            chain[0] += 1
            ins.then_inc(sem_, 1)
            eng.wait_ge(sem_, chain[0])

        with nc.Block() as block:

            @block.sync
            def _(sp):
                sp.dma_start(wq_s, wq_t.rearrange("(h p) d -> p h d", p=P)).then_inc(s_w[0], 16)
                sp.dma_start(wk_s, wk_t.rearrange("(h p) c -> p h c", p=P)).then_inc(s_w[1], 16)
                sp.dma_start(wv_s, wv_t.rearrange("(h p) c -> p h c", p=P)).then_inc(s_w[2], 16)
                sp.dma_start(wo_s, wo.rearrange("(h p) d -> p h d", p=P)).then_inc(s_w[3], 16)
                for g in range(G):
                    sp.dma_start(x_res[:, g * J:(g + 1) * J, :], x_tiles[g]).then_inc(s_x[g], 16)
                sp.dma_start(ctx_all.rearrange("p (t c) -> p t c", t=TILES),
                             ctx.rearrange("b s c -> (b s) c").rearrange("(t p) c -> p t c", p=P)).then_inc(s_w[4], 16)

                def load_group(g, b):
                    if not (isinstance(g, int) and g < 2):
                        sp.wait_ge(s_on, Q * (g - 1))
                        sp.wait_ge(s_msk, Q * (g - 1))
                        sp.wait_ge(s_manyof, g - 1)
                    sp.dma_start(ctx_t_s[b][:], ctx_t_groups[bass.ds(g, 1), :, :].rearrange("a c n -> c (a n)")).then_inc(s_ctx[b], 16)
                    sp.dma_start(ctx_s[b][:], ctx_tiles[bass.ds(g, 1), :, :, :].rearrange("a p j c -> p (a j) c")).then_inc(s_ctx[b], 16)
                    sp.dma_start(mask_u[b][:], mask_groups[bass.ds(g, 1), :, :].rearrange("a b n -> (a b) n").to_broadcast([P, GT])).then_inc(s_ctx[b], 16)

                load_group(0, 0)
                load_group(1, 1)
                with nc.sync.Fori(0, (G - 2) // 2) as k:
                    load_group(2 + 2 * k, 0)
                    load_group(3 + 2 * k, 1)

            @block.gpsimd
            def _(pool):
                pool.memset(ident[:], 0.0).then_inc(s_ident, 1)
                pool.memset(ones[:], 1.0).then_inc(s_ident, 1)
                pool.wait_ge(s_ident, 2)
                pool.affine_select(out=ident[:], in_=ident[:], compare_op=ALU.not_equal, fill=1.0, base=0,
                                   pattern=[[-1, P]], channel_multiplier=1).then_inc(s_ident, 1)

                def normalise_probs(u):
                    pool.wait_ge(s_ri, 2 * (u + 1))
                    if not (isinstance(u, int) and u < 1):
                        pool.wait_ge(s_pt, u)
                    pool.tensor_tensor(pn.rearrange("p a (b s) -> p (a b) s", s=S), pr.rearrange("p a (b s) -> p (a b) s", s=S),
                                       rinv[:].unsqueeze(2).to_broadcast([P, HP * NB, S]), ALU.mult).then_inc(s_pn, 1)

                def group(g):
                    for q in range(Q):
                        normalise_probs(Q * g + q)

                group(0)
                with nc.gpsimd.Fori(0, (G - 2) // 2) as k:
                    group(1 + 2 * k)
                    group(2 + 2 * k)
                group(G - 1)

            @block.scalar
            def _(act):
                act.dma_start(gates[:, 0:1], g_xattn.rearrange("(a n) -> a n", a=1).to_broadcast([P, 1])).then_inc(s_g, 16)
                act.dma_start(gates[:, 1:2], g_ffn.rearrange("(a n) -> a n", a=1).to_broadcast([P, 1])).then_inc(s_g, 16)
                for i in range(H * KC // 4):
                    act.wait_ge(s_mprod, i + 1)
                    kc, hq = i % KC, i // KC
                    act.activation(mf[:, kc, 4 * hq:4 * hq + 4, :].rearrange("p h c -> p (h c)"), banks[:, i % 8, :], ACT.Copy).then_inc(s_mcopied, 1)
                for i in range(H // 2):
                    act.wait_ge(s_nprod, i + 1)
                    act.activation(nf[:, 2 * i:2 * i + 2, :].rearrange("p h d -> p (h d)"), banks[:, i % 8, :], ACT.Copy).then_inc(s_ncopied, 1)
                act.wait_ge(s_var, 1)
                act.activation(nwt[:, 0, :], nwt[:, 1, :], ACT.Sqrt).then_inc(s_act, 1)
                act.wait_ge(s_g, 32)
                act.activation(consts[:, 0:2], gates[:], ACT.Tanh).then_inc(s_tanh, 1)

                def xt_high(g, b):
                    act.wait_ge(s_xt, KC * (g + 1))
                    act.activation(xt_hi[b][:], sp_ps, ACT.Copy).then_inc(s_xth, 1)

                def unit(u, xm_next, last):
                    if not last:
                        act.wait_ge(s_xm, HU * (u + 1) + 1)
                        act.activation(xm_next[:, 0, 0, :, :], by_batch(0), ACT.Copy).then_inc(s_xma, 1)
                    act.wait_ge(s_max, u + 1)
                    if not (isinstance(u, int) and u < 1):
                        act.wait_ge(s_pn, u)
                    for i in range(HP * NB):
                        e = act.activation(pr[:, i // NB, (i % NB) * S:(i % NB + 1) * S], sm[:, i // NB, (i % NB) * S:(i % NB + 1) * S],
                                           ACT.Exp, bias=nmax[:, i:i + 1], accum_out=rsum[:, i:i + 1])
                    e.then_inc(s_exp, 1)
                    if not last:
                        act.wait_ge(s_xm, HU * (u + 1) + 2)
                        act.activation(xm_next[:, 0, 1, :, :], by_batch(1), ACT.Copy).then_inc(s_xma, 1)
                    act.wait_ge(s_pt, u + 1)
                    act.activation(pt[:, :, 0, :], sp_ps[:, 0, :].rearrange("p (j n) -> p j n", j=J), ACT.Copy).then_inc(s_pta, 1)
                    for bank in range(4):
                        act.wait_ge(s_pv, 4 * u + bank + 1)
                        act.activation(o_view(o_hi, bank), xo_ps[:, bank, :].rearrange("p (j h t) -> p h j t", j=2, h=HU), ACT.Copy).then_inc(s_oh, 1)

                act.wait_ge(s_stat, 1)
                xt_high(0, 0)
                for h in range(2):
                    act.wait_ge(s_xm, h + 1)
                    act.activation(xm[0][:, 0, h, :, :], by_batch(h), ACT.Copy).then_inc(s_xma, 1)

                def group(g, b, last):
                    for q in range(Q):
                        unit(Q * g + q, xm[(q + 1) % 2], last and q == Q - 1)
                        if q == 2 and not last:
                            xt_high(g + 1, 1 - b)

                group(0, 0, False)
                with nc.scalar.Fori(0, (G - 2) // 2) as k:
                    group(1 + 2 * k, 1, False)
                    group(2 + 2 * k, 0, False)
                group(G - 1, 1, True)

            @block.vector
            def _(dve):
                chain = [0]

                def step(ins):
                    link(dve, s_dve, chain, ins)

                def normalise(g):
                    if not (isinstance(g, int) and g < 1):
                        dve.wait_ge(s_xt, KC * g)
                    for j in range(J):
                        t = bass.ds(g * J + j, 1)
                        n = dve.tensor_scalar(xn[:, j, :], x_res[:, t, :].rearrange("p a d -> p (a d)"),
                                              mean_var[:, t, 0:1].rearrange("p a b -> p (a b)"), rstd[:, t], ALU.subtract, ALU.mult)
                    n.then_inc(s_xnorm, 1)

                step(dve.memset(mx_part[:], 0.0))
                for g in range(G):
                    dve.wait_ge(s_x[g], 16)
                    for j in range(J):
                        last = dve.bn_stats(stats[:, g * J + j, :], x_res[:, g * J + j, :])
                    step(last)
                    for j in range(J):
                        last = dve.bn_aggr(mean_var[:, g * J + j, :], stats[:, g * J + j, :])
                    step(last)
                var, root, y, t = nwt[:, 1, :], nwt[:, 0, :], rstd[:], nwt[:, 2, :]
                dve.tensor_scalar(var, mean_var[:, :, 1], EPS, None, ALU.add).then_inc(s_var, 1)
                dve.wait_ge(s_act, 1)
                step(dve.reciprocal(y, root))
                step(dve.tensor_tensor(t, y, y, ALU.mult))
                step(dve.tensor_tensor(t, t, var, ALU.mult))
                step(dve.tensor_scalar(t, t, -0.5 * LN_SCALE, 1.5 * LN_SCALE, ALU.mult, ALU.add))
                dve.tensor_tensor(y, y, t, ALU.mult).then_inc(s_stat, 1)
                dve.wait_ge(s_stat, 1)
                normalise(0)
                dve.wait_ge(s_mcopied, H * KC // 4)
                dve.tensor_reduce(mx_part[:, 0:1], work[:, 0:4096], AX_X, ALU.max, apply_absolute_value=True)
                dve.wait_ge(s_ncopied, H // 2)
                dve.tensor_reduce(mx_part[:, 1:2], work[:, 4096:8192], AX_X, ALU.max, apply_absolute_value=True)
                dve.wait_ge(s_w[4], 16)
                dve.tensor_reduce(mx_part[:, 2:3], ctx_all, AX_X, ALU.max, apply_absolute_value=True).then_inc(s_mxp, 1)
                dve.wait_ge(s_maxt, 1)
                step(dve.tensor_reduce(mx_col[0:NM, :], banks[0:NM, 0, 0:P], AX_X, ALU.max))
                dve.wait_ge(s_ident, 3)
                dve.tensor_scalar(mx_diag[0:NM, :], ident[0:NM, 0:NM], mx_col[0:NM, 0:1], None, ALU.mult).then_inc(s_maxd, 1)
                dve.wait_ge(s_maxb, 1)
                step(dve.tensor_scalar(scale_of[:], banks[:, 1, 0:NM], 1e-30, 1e30, ALU.max, ALU.min))
                step(dve.tensor_scalar(mx_exp[:], scale_of[:].bitcast(I32), 0x7F800000, None, ALU.bitwise_and))
                dve.tensor_scalar(scale_of[:].bitcast(I32), mx_exp[:], -1.0, float((254 + TOP) << 23), ALU.mult, ALU.add).then_inc(s_scale, 1)
                step(dve.tensor_scalar(inv_of[:].bitcast(I32), mx_exp[:], -float(TOP << 23), None, ALU.add))
                dve.wait_ge(s_scale, 1)
                for i, (full, hi, lo) in enumerate(((work[:, 0:4096], m_hi[:].rearrange("p k h c -> p (k h c)"), m_lo[:].rearrange("p k h c -> p (k h c)")),
                                                    (work[:, 4096:8192], n_hi[:].rearrange("p h d -> p (h d)"), n_lo[:].rearrange("p h d -> p (h d)")))):
                    step(dve.tensor_scalar(hi, full, scale_of[:, i:i + 1], None, ALU.mult))
                    dve.scalar_tensor_tensor(out=lo, in0=full, scalar=scale_of[:, i:i + 1], in1=hi, op0=ALU.mult, op1=ALU.subtract).then_inc(s_wready, 1)
                dve.wait_ge(s_tanh, 1)
                dve.tensor_scalar(consts[:, 2:3], inv_of[:, 0:1], 1.0 / LN_SCALE / float(C) ** 0.5, None, ALU.mult).then_inc(s_wready, 1)
                step(dve.tensor_tensor(consts[:, 3:4], inv_of[:, 1:2], inv_of[:, 2:3], ALU.mult))
                step(dve.tensor_tensor(consts[:, 4:5], consts[:, 3:4], consts[:, 0:1], ALU.mult))
                dve.wait_ge(s_wready, 3)

                def xt_low(g, b):
                    dve.wait_ge(s_xth, g + 1)
                    dve.tensor_tensor(xt_lo[b][:], sp_ps, xt_hi[b][:], ALU.subtract).then_inc(s_xtl, 1)

                def context(b, g, turn):
                    dve.wait_ge(s_ctx[b], 48 * turn)
                    dve.tensor_scalar(ctx_s[b][:], ctx_s[b][:], scale_of[:, 2:3], None, ALU.mult).then_inc(s_cscale, 1)
                    dve.tensor_scalar(mask_b[b][:], mask_u[b][:], -1.0, -NEG, ALU.add, ALU.mult).then_inc(s_mbias, 1)
                    dve.tensor_reduce(any_of[b][:], mask_u[b][:].rearrange("p (b s) -> p b s", s=S), AX_X, ALU.max).then_inc(s_manyof, 1)

                def unit(u, g, b, xm_next, last):
                    dve.wait_ge(s_sc, u + 1)
                    if not (isinstance(u, int) and u < 1):
                        dve.wait_ge(s_exp, u)
                    dve.scalar_tensor_tensor(out=sm, in0=sp_ps, scalar=consts[:, 2:3],
                                             in1=mask_b[b][:].unsqueeze(1).to_broadcast([P, HP, GT]),
                                             op0=ALU.mult, op1=ALU.add).then_inc(s_msk, 1)
                    dve.wait_ge(s_msk, u + 1)
                    dve.tensor_reduce(nmax[:], sm.rearrange("p a (b s) -> p (a b) s", s=S), AX_X, ALU.max, negate=True).then_inc(s_max, 1)
                    if not last:
                        for h in (2, 3):
                            dve.wait_ge(s_xm, HU * (u + 1) + h + 1)
                            dve.tensor_copy(xm_next[:, 1, h - 2, :, :], by_batch(h)).then_inc(s_xmd, 1)
                    dve.wait_ge(s_exp, u + 1)
                    if not (isinstance(u, int) and u < 1):
                        dve.wait_ge(s_pn, u)
                    dve.reciprocal(rinv[:], rsum[:]).then_inc(s_ri, 1)
                    dve.wait_ge(s_ri, 2 * u + 1)
                    dve.tensor_tensor(rinv[:].rearrange("p (a b) -> p a b", a=HP), rinv[:].rearrange("p (a b) -> p a b", a=HP),
                                      any_of[b][:].unsqueeze(1).to_broadcast([P, HP, NB]), ALU.mult).then_inc(s_ri, 1)
                    dve.wait_ge(s_pt, u + 1)
                    dve.tensor_copy(pt[:, :, 1, :], sp_ps[:, 1, :].rearrange("p (j n) -> p j n", j=J)).then_inc(s_ptd, 1)
                    for bank in range(4):
                        dve.wait_ge(s_oh, 4 * u + bank + 1)
                        dve.tensor_tensor(o_view(o_lo, bank), xo_ps[:, bank, :].rearrange("p (j h t) -> p h j t", j=2, h=HU),
                                          o_view(o_hi, bank), ALU.subtract).then_inc(s_ol, 1)

                def residual(g):
                    dve.wait_ge(s_on, Q * (g + 1))
                    t = bass.ds(g * J, J)
                    if isinstance(g, int):
                        t = slice(g * J, g * J + J)
                    dve.scalar_tensor_tensor(out=x_res[:, t, :], in0=acc, scalar=consts[:, 4:5], in1=x_res[:, t, :],
                                             op0=ALU.mult, op1=ALU.add).then_inc(s_x1, 1)

                context(0, 0, 1)
                xt_low(0, 0)
                for h in (2, 3):
                    dve.wait_ge(s_xm, h + 1)
                    dve.tensor_copy(xm[0][:, 1, h - 2, :, :], by_batch(h)).then_inc(s_xmd, 1)

                def group(g, b, turn_next, first, last):
                    for q in range(Q):
                        if q == 0:
                            dve.wait_ge(s_mbias, g + 1)
                            dve.wait_ge(s_manyof, g + 1)
                        unit(Q * g + q, g, b, xm[(q + 1) % 2], last and q == Q - 1)
                        if q == 0 and not first:
                            residual(g - 1)
                        if q == 1 and not last:
                            normalise(g + 1)
                            context(1 - b, g + 1, turn_next)
                        if q == 2 and not last:
                            xt_low(g + 1, 1 - b)

                group(0, 0, 1, True, False)
                with nc.vector.Fori(0, (G - 2) // 2) as k:
                    group(1 + 2 * k, 1, k + 2, False, False)
                    group(2 + 2 * k, 0, k + 2, False, False)
                group(G - 1, 1, 0, False, True)
                residual(G - 1)

            @block.tensor
            def _(pe):
                pe.wait_ge(s_w[0], 16)
                pe.wait_ge(s_w[1], 16)
                for i in range(H * KC // 4):
                    kc, hq = i % KC, i // KC
                    if i >= 8:
                        pe.wait_ge(s_mcopied, i - 7)
                    for h in range(4 * hq, 4 * hq + 4):
                        mm = pe.matmul(banks[:, i % 8, (h % 4) * C:(h % 4 + 1) * C], wq_s[:, h, kc * P:(kc + 1) * P], wk_s[:, h // (H // KV), :],
                                       start=True, stop=True)
                    mm.then_inc(s_mprod, 1)
                pe.wait_ge(s_w[2], 16)
                pe.wait_ge(s_w[3], 16)
                for i in range(H // 2):
                    pe.wait_ge(s_mcopied, H * KC // 4 - 8 + i + 1)
                    for h in (2 * i, 2 * i + 1):
                        mm = pe.matmul(banks[:, i % 8, (h % 2) * D:(h % 2 + 1) * D], wv_s[:, h // (H // KV), :], wo_s[:, h, :], start=True, stop=True)
                    mm.then_inc(s_nprod, 1)
                pe.wait_ge(s_ident, 3)
                pe.wait_ge(s_ncopied, H // 2)
                pe.wait_ge(s_mxp, 1)
                pe.transpose(banks[0:NM, 0, 0:P], mx_part[:], ident[:]).then_inc(s_maxt, 1)
                pe.wait_ge(s_maxd, 1)
                pe.matmul(banks[:, 1, 0:NM], ones[0:NM, :], mx_diag[0:NM, :], start=True, stop=True).then_inc(s_maxb, 1)

                def transposes(g):
                    pe.wait_ge(s_xnorm, g + 1)
                    for kc in range(KC):
                        for j in range(J):
                            mm = pe.transpose(sp_ps[:, kc, j * P:(j + 1) * P], xn[:, j, kc * P:(kc + 1) * P], ident[:])
                        mm.then_inc(s_xt, 1)

                def x_m(u, q, b):
                    for hh in range(HU):
                        if not (isinstance(u, int) and u < 2):
                            pe.wait_ge(s_ol, 4 * (u - 2) + hh + 1)
                        h = HU * q + hh
                        n = 0
                        for kc in range(KC):
                            for w, r in ((m_hi, xt_hi[b]), (m_hi, xt_lo[b]), (m_lo, xt_hi[b])):
                                mm = pe.matmul(xo_ps[:, hh, :], w[:, kc, h, :], r[:, kc, :], start=(n == 0), stop=(n == 3 * KC - 1))
                                n += 1
                        mm.then_inc(s_xm, 1)

                def scores(u, xm_u, b):
                    pe.wait_ge(s_xma, 2 * (u + 1))
                    pe.wait_ge(s_xmd, 2 * (u + 1))
                    if not (isinstance(u, int) and u < 1):
                        pe.wait_ge(s_pta, u)
                        pe.wait_ge(s_ptd, u)
                    for hp in range(HP):
                        for bt in range(NB):
                            mm = pe.matmul(sp_ps[:, hp, bt * S:(bt + 1) * S], xm_u[:, hp, :, bt, :].rearrange("p c t -> p (c t)"),
                                           ctx_t_s[b][:, bt * S:(bt + 1) * S], start=True, stop=True)
                    mm.then_inc(s_sc, 1)

                def project(u, q, js):
                    pe.wait_ge(s_oh, 4 * (u + 1))
                    pe.wait_ge(s_ol, 4 * (u + 1))
                    for j in js:
                        for hh in range(HU):
                            h = HU * q + hh
                            for n, (o, w) in enumerate(((o_hi, n_hi), (o_lo, n_hi), (o_hi, n_lo))):
                                mm = pe.matmul(acc[:, j, :], o[:, hh, j * P:(j + 1) * P], w[:, h, :],
                                               start=(h == 0 and n == 0 and j % 2 == 0), stop=(h == H - 1 and n == 2), skip_group_check=True)
                    if J - 1 in js:
                        mm.then_inc(s_on, 1)

                def probs_t(u):
                    pe.wait_ge(s_pn, u + 1)
                    for hp in range(HP):
                        for j in range(J):
                            mm = pe.transpose(sp_ps[:, hp, j * P:(j + 1) * P], pn[:, hp, j * P:(j + 1) * P], ident[:])
                    mm.then_inc(s_pt, 1)

                def head_outputs(u, b):
                    pe.wait_ge(s_pta, u + 1)
                    pe.wait_ge(s_ptd, u + 1)
                    for half in range(2):
                        for jj in range(2):
                            j = 2 * half + jj
                            for b2 in range(2):
                                rows = slice(b2 * S, (b2 + 1) * S)
                                mm = pe.matmul(xo_ps[:, 2 * half + b2, jj * 256:(jj + 1) * 256], ctx_s[b][rows, j, :], pt[rows, j, :, :],
                                               start=True, stop=True)
                                if jj == 1:
                                    mm.then_inc(s_pv, 1)

                def group(g, b, first, last):
                    for q in range(Q):
                        u = Q * g + q
                        more = not (last and q == Q - 1)
                        if q == 0:
                            pe.wait_ge(s_cscale, g + 1)
                        if q == Q - 1 and more:
                            pe.wait_ge(s_xth, g + 2)
                            pe.wait_ge(s_xtl, g + 2)
                        scores(u, xm[q % 2], b)
                        if more:
                            x_m(u + 1, (q + 1) % Q, b if q < Q - 1 else 1 - b)
                        before = not (first and q == 0)
                        if q == 1 and not first:
                            pe.wait_ge(s_x1, g)
                        if before:
                            project(u - 1, (q - 1) % Q, (0, 1, 2))
                        probs_t(u)
                        if before:
                            project(u - 1, (q - 1) % Q, (3,))
                        if more:
                            pe.wait_ge(s_xma, 2 * (u + 2))
                            pe.wait_ge(s_xmd, 2 * (u + 2))
                        head_outputs(u, b)
                        if q == 2 and not last:
                            transposes(g + 1)

                pe.wait_ge(s_scale, 1)
                transposes(0)
                pe.wait_ge(s_wready, 2)
                pe.wait_ge(s_xth, 1)
                pe.wait_ge(s_xtl, 1)
                x_m(0, 0, 0)
                group(0, 0, True, False)
                with nc.tensor.Fori(0, (G - 2) // 2) as k:
                    group(1 + 2 * k, 1, False, False)
                    group(2 + 2 * k, 0, False, False)
                group(G - 1, 1, False, True)
                project(Q * G - 1, Q - 1, range(J))

        ROW = D + 2
        REGION = B * T + P
        SKIP = 1 << 20
        TF = 72
        U = 4
        assert 2 * B * T // P + E - 1 <= TF and TF % U == 0
        rows_dram = nc.dram_tensor("expert_rows", [(E + 1) * REGION, ROW], F32, kind="Internal").ap()
        y_dram = nc.dram_tensor("expert_outputs", [2 * B * T, D], F32, kind="Internal").ap()
        y_tiles = y_dram.rearrange("(c g j p) d -> g p c j d", c=2, j=J, p=P)

        at2 = 0

        def take2(words, region=None):
            nonlocal at2
            at2 += words
            assert at2 <= PH1
            return work[:, at2 - words:at2]

        n_gu = E * KC * 2 * GU // 2
        w_gu = ffn_w[:, 0:n_gu].bitcast(F16).rearrange("p (e k w f) -> p e k w f", e=E, k=KC, w=2)
        w_dn = ffn_w[:, n_gu:].bitcast(F16).rearrange("p (e w c d) -> p e w c d", e=E, w=2, c=NF)
        st_gu = take2(KC * GU).rearrange("p (k f) -> p k f", k=KC)
        st_dn = take2(NF * D).rearrange("p (c d) -> p c d", c=NF)
        row = [take2(J * ROW).rearrange("p (j r) -> p j r", j=J) for _ in range(2)]
        xt32 = take2(KC * GT).rearrange("p (k n) -> p k n", k=KC)
        zero_row = take2(ROW)
        fm = sb("fm", [P, 4])
        f_exp = sb("f_exp", [P, 2], I32)
        f_scale = sb("f_scale", [P, E, 2])
        f_inv = sb("f_inv", [P, E, 2])
        tile_scales = sb("tile_scales", [P, 3, E])
        gate_w_s = sb("gate_w_s", [P, KC, E])
        gate_b_s = sb("gate_b_s", [P, E])
        bias_s = sb("bias_s", [P, E])
        strict = sb("strict", [P, P])
        ones_sq = sb("ones_sq", [P, P])
        place = [sb(f"place{c}", [P, TILES], I32) for c in range(2)]
        rev = sb("rev", [P, E])
        region0 = sb("region0", [P, E])
        tile_iota = sb("tile_iota", [P, TF])
        rank_p = sb("rank_p", [P, E + 1])
        region9 = sb("region9", [P, E + 1])
        stat2 = sb("stat2", [P, J, 6])
        mv2 = sb("mv2", [P, J, 2])
        v2 = sb("v2", [P, J])
        y2 = sb("y2", [P, J])
        t2 = sb("t2", [P, J])
        lg = sb("lg", [P, J, E])
        ex = sb("ex", [P, J, E])
        rt = sb("rt", [P, J, E])
        key = sb("key", [P, J, E])
        oh = [sb(f"oh{c}", [P, J, E]) for c in range(2)]
        chosen = sb("chosen", [P, J, E])
        rt2 = sb("rt2", [P, J, E])
        pos = sb("pos", [P, J, E])
        red = sb("red", [P, J])
        topw = [sb(f"topw{c}", [P, J]) for c in range(2)]
        slot = [sb(f"slot{c}", [P, J], I32) for c in range(2)]
        slot_f = sb("slot_f", [P, J])
        count = sb("count", [P, E])
        n_tiles = sb("n_tiles", [P, E])
        n_tiles_i = sb("n_tiles_i", [P, E], I32)
        t_end = sb("t_end", [P, E])
        past = sb("past", [P, TF, E])
        pick = sb("pick", [P, TF, E])
        t_e = sb("t_e", [P, TF])
        t_c = sb("t_c", [P, TF])
        t_s = sb("t_s", [P, TF])
        t_row = sb("t_row", [P, TF])
        t_e_i = sb("t_e_i", [P, TF], I32)
        t_row_i = sb("t_row_i", [P, TF], I32)
        t_sc = [sb(f"t_sc{i}", [P, TF]) for i in range(3)]
        tail_i = sb("tail_i", [P, E + 1], I32)
        tail_f = sb("tail_f", [P, E + 1])

        s_small = sem("router_constants_loaded")
        s_iota = sem("iotas_ready")
        s_fw = sem("expert_weights_loaded")
        s_fpm = sem("expert_partial_max")
        s_fam = sem("expert_max_everywhere")
        s_fch = sem("expert_scale_step")
        s_fsp = sem("expert_weights_split")
        s_rch = sem("routing_step")
        s_row = sem("rows_normalised")
        s_x2t = sem("x2_transposed")
        s_x2c = sem("x2_transposed_copied")
        s_lg = sem("logits_done")
        s_l1 = sem("logits_shifted")
        s_ex = sem("logits_exponentials")
        s_cho = sem("choices_ready")
        s_pos = sem("positions_done")
        s_slot = sem("slots_ready")
        s_scat = sem("rows_scattered")
        s_passed = sem("pool_passed")
        s_passed_v = sem("dve_passed")
        s_tail = sem("tail_places_ready")
        s_tab = sem("tile_tables_ready")

        RSTEPS = 42
        with nc.Block() as block:

            @block.sync
            def _(sp):
                sp.dma_start(gate_w_s[:], gate_w_t.rearrange("(k p) e -> p k e", p=P)).then_inc(s_small, 16)
                sp.dma_start(gate_b_s[:], gate_b.rearrange("(a e) -> a e", a=1).to_broadcast([P, E])).then_inc(s_small, 16)
                sp.dma_start(bias_s[:], expert_bias.rearrange("(a e) -> a e", a=1).to_broadcast([P, E])).then_inc(s_small, 16)
                sp.wait_ge(s_iota, 1)

                def load_expert(e):
                    e = bass.ds(e, 1)
                    sp.dma_start(st_gu, w_gu_t[e, :, :].rearrange("a (k p) f -> p (a k) f", p=P)).then_inc(s_fw, 16)
                    sp.dma_start(st_dn[:, 0:2, :], w_down_t[e, 0:2 * P, :].rearrange("a (c p) d -> p (a c) d", p=P)).then_inc(s_fw, 16)
                    sp.dma_start(st_dn[0:F - 2 * P, 2, :], w_down_t[e, 2 * P:F, :].rearrange("a p d -> p (a d)")).then_inc(s_fw, 16)

                load_expert(0)
                with nc.sync.Fori(1, E) as e:
                    sp.wait_ge(s_fsp, e)
                    load_expert(e)

            @block.gpsimd
            def _(pool):
                pool.memset(st_dn[:], 0.0).then_inc(s_iota, 1)
                n = 1

                def made(ins):
                    nonlocal n
                    n += 1
                    ins.then_inc(s_iota, 1)

                made(pool.memset(ones_sq[:], 1.0))
                made(pool.memset(strict[:], 0.0))
                pool.wait_ge(s_iota, n)
                made(pool.affine_select(out=strict[:], in_=strict[:], compare_op=ALU.is_ge, fill=1.0, base=0,
                                        pattern=[[-1, P]], channel_multiplier=1))
                made(pool.memset(count[:], 0.0))
                made(pool.memset(zero_row[:, 0:D + 1], 0.0))
                made(pool.iota(zero_row[:, D + 1:D + 2].bitcast(I32), pattern=[[0, 1]], base=SKIP, channel_multiplier=0))
                for c in range(2):
                    made(pool.iota(place[c][:], pattern=[[P, TILES]], base=c * B * T, channel_multiplier=1))
                made(pool.iota(rev[:], pattern=[[-1, E]], base=E, channel_multiplier=0, allow_small_or_imprecise_dtypes=True))
                made(pool.iota(region0[:], pattern=[[REGION, E]], base=0, channel_multiplier=0, allow_small_or_imprecise_dtypes=True))
                made(pool.iota(region9[:], pattern=[[REGION, E + 1]], base=0, channel_multiplier=0, allow_small_or_imprecise_dtypes=True))
                made(pool.iota(rank_p[:], pattern=[[0, E + 1]], base=0, channel_multiplier=1, allow_small_or_imprecise_dtypes=True))
                made(pool.iota(tile_iota[:], pattern=[[1, TF]], base=0, channel_multiplier=0, allow_small_or_imprecise_dtypes=True))
                assert n == 14

                def turn(g):
                    pool.wait_ge(s_fpm, g + 1)
                    pool.sem_inc(s_passed)
                    pool.partition_all_reduce(fm[:, 2:4], fm[:, 0:2], P, bass.bass_isa.ReduceOp.max).then_inc(s_fam, 1)
                    pool.wait_ge(s_slot, g + 1)
                    pool.sem_inc(s_passed)
                    for c in range(2):
                        for j in range(J):
                            pool.indirect_dma_start(rows_dram, bass.IndirectOffsetOnAxis(ap=slot[c][:, j:j + 1], axis=0),
                                                    row[c][:, j, :], None).then_inc(s_scat, 16)

                turn(0)
                with nc.gpsimd.Fori(1, G) as g:
                    turn(g)
                pool.wait_ge(s_tail, 1)
                for e in range(E + 1):
                    pool.indirect_dma_start(rows_dram, bass.IndirectOffsetOnAxis(ap=tail_i[:, e:e + 1], axis=0),
                                            zero_row, None).then_inc(s_scat, 16)
                pool.wait_ge(s_scat, 16 * (2 * TILES + E + 1))

            @block.scalar
            def _(act):
                def turn(g):
                    act.wait_ge(s_x2t, g + 1)
                    act.activation(xt32, banks[:, 2:4, :], ACT.Copy).then_inc(s_x2c, 1)
                    act.wait_ge(s_l1, g + 1)
                    act.activation(ex[:], lg[:], ACT.Exp).then_inc(s_ex, 1)

                turn(0)
                with nc.scalar.Fori(1, G) as g:
                    turn(g)

            @block.tensor
            def _(pe):
                pe.wait_ge(s_iota, 14)
                pe.wait_ge(s_small, 48)

                def turn(g):
                    pe.wait_ge(s_row, g + 1)
                    for kc in range(KC):
                        for j in range(J):
                            mm = pe.transpose(banks[:, 2 + kc, j * P:(j + 1) * P], row[0][:, j, kc * P:(kc + 1) * P], ident[:])
                    mm.then_inc(s_x2t, 1)
                    pe.wait_ge(s_x2c, g + 1)
                    for j in range(J):
                        for kc in range(KC):
                            mm = pe.matmul(banks[:, 4, j * E:(j + 1) * E], xt32[:, kc, j * P:(j + 1) * P], gate_w_s[:, kc, :],
                                           start=(kc == 0), stop=(kc == KC - 1))
                    mm.then_inc(s_lg, 1)
                    pe.wait_ge(s_cho, g + 1)
                    pe.matmul(banks[:, 5, 0:J * E], strict[:], chosen[:].rearrange("p j e -> p (j e)"), start=True, stop=False, skip_group_check=True)
                    for n in range(J - 1, 0, -1):
                        pe.matmul(banks[:, 5, (J - n) * E:J * E], ones_sq[:], chosen[:, 0:n, :].rearrange("p j e -> p (j e)"),
                                  start=False, stop=(n == 1), skip_group_check=True)
                    for j in range(J):
                        mm = pe.matmul(banks[:, 6, 0:E], ones_sq[:], chosen[:, j, :], start=(j == 0), stop=(j == J - 1))
                    mm.then_inc(s_pos, 1)

                turn(0)
                with nc.tensor.Fori(1, G) as g:
                    turn(g)

            @block.vector
            def _(dve):
                dve.wait_ge(s_iota, 14)
                dve.wait_ge(s_small, 48)

                def route(g):
                    k = 0

                    def step(ins):
                        nonlocal k
                        k += 1
                        ins.then_inc(s_rch, 1)
                        dve.wait_ge(s_rch, RSTEPS * g + k)

                    tiles = bass.ds(g * J, J)
                    for j in range(J):
                        b = dve.bn_stats(stat2[:, j, :], x_res[:, bass.ds(g * J + j, 1), :].rearrange("p a d -> p (a d)"))
                    k += 1
                    b.then_inc(s_rch, 1)
                    dve.wait_ge(s_rch, RSTEPS * g + k)
                    dve.sem_inc(s_passed_v)
                    for j in range(J):
                        b = dve.bn_aggr(mv2[:, j, :], stat2[:, j, :])
                    step(b)
                    step(dve.tensor_scalar(v2[:], mv2[:, :, 1], EPS, None, ALU.add))
                    step(dve.tensor_scalar(y2[:].bitcast(I32), v2[:].bitcast(I32), 1, None, ALU.logical_shift_right))
                    step(dve.tensor_scalar(y2[:].bitcast(I32), y2[:].bitcast(I32), -1.0, float(0x5F3759DF), ALU.mult, ALU.add))
                    for n in range(4):
                        step(dve.tensor_tensor(t2[:], y2[:], y2[:], ALU.mult))
                        step(dve.scalar_tensor_tensor(out=t2[:], in0=t2[:], scalar=-0.5, in1=v2[:], op0=ALU.mult, op1=ALU.mult))
                        step(dve.scalar_tensor_tensor(out=y2[:], in0=t2[:], scalar=1.5, in1=y2[:], op0=ALU.add, op1=ALU.mult))
                    step(dve.tensor_scalar(y2[:], y2[:], LN_SCALE, None, ALU.mult))
                    if not isinstance(g, int):
                        dve.wait_ge(s_scat, 16 * 2 * J * g)
                    for c in range(2):
                        for j in range(J):
                            b = dve.tensor_scalar(row[c][:, j, 0:D], x_res[:, bass.ds(g * J + j, 1), :].rearrange("p a d -> p (a d)"),
                                                  mv2[:, j, 0:1], y2[:, j:j + 1], ALU.subtract, ALU.mult)
                        if c == 0:
                            b.then_inc(s_row, 1)
                    for c in range(2):
                        dve.tensor_copy(row[c][:, :, D + 1].bitcast(I32), place[c][:, tiles])
                    dve.wait_ge(s_lg, g + 1)
                    step(dve.scalar_tensor_tensor(out=rt[:], in0=banks[:, 4, 0:J * E].rearrange("p (j e) -> p j e", j=J), scalar=1.0 / LN_SCALE,
                                                  in1=gate_b_s[:].unsqueeze(1).to_broadcast([P, J, E]), op0=ALU.mult, op1=ALU.add))
                    step(dve.tensor_reduce(red[:], rt[:], AX_X, ALU.max))
                    dve.tensor_tensor(lg[:], rt[:], red[:].unsqueeze(2).to_broadcast([P, J, E]), ALU.subtract).then_inc(s_l1, 1)
                    dve.wait_ge(s_ex, g + 1)
                    step(dve.tensor_reduce(red[:], ex[:], AX_X, ALU.add))
                    step(dve.reciprocal(red[:], red[:]))
                    step(dve.tensor_tensor(rt[:], ex[:], red[:].unsqueeze(2).to_broadcast([P, J, E]), ALU.mult))
                    step(dve.tensor_tensor(rt[:], rt[:], bias_s[:].unsqueeze(1).to_broadcast([P, J, E]), ALU.add))
                    for c in range(2):
                        src = rt if c == 0 else rt2
                        step(dve.tensor_reduce(topw[c][:], src[:], AX_X, ALU.max))
                        step(dve.tensor_tensor(key[:], src[:], topw[c][:].unsqueeze(2).to_broadcast([P, J, E]), ALU.is_equal))
                        step(dve.tensor_tensor(key[:], key[:], rev[:].unsqueeze(1).to_broadcast([P, J, E]), ALU.mult))
                        step(dve.tensor_reduce(red[:], key[:], AX_X, ALU.max))
                        step(dve.tensor_tensor(oh[c][:], key[:], red[:].unsqueeze(2).to_broadcast([P, J, E]), ALU.is_equal))
                        if c == 0:
                            step(dve.scalar_tensor_tensor(out=rt2[:], in0=oh[0][:], scalar=NEG, in1=rt[:], op0=ALU.mult, op1=ALU.add))
                    dve.tensor_tensor(chosen[:], oh[0][:], oh[1][:], ALU.add).then_inc(s_cho, 1)
                    for c in range(2):
                        dve.tensor_copy(row[c][:, :, D], topw[c][:])
                    dve.wait_ge(s_pos, g + 1)
                    step(dve.tensor_tensor(pos[:], banks[:, 5, 0:J * E].rearrange("p (j e) -> p j e", j=J), count[:].unsqueeze(1).to_broadcast([P, J, E]), ALU.add))
                    step(dve.tensor_tensor(pos[:], pos[:], region0[:].unsqueeze(1).to_broadcast([P, J, E]), ALU.add))
                    dve.tensor_tensor(count[:], banks[:, 6, 0:E], count[:], ALU.add)
                    for c in range(2):
                        step(dve.tensor_tensor(oh[c][:], oh[c][:], pos[:], ALU.mult))
                        step(dve.tensor_reduce(slot_f[:], oh[c][:], AX_X, ALU.add))
                        b = dve.tensor_copy(slot[c][:], slot_f[:])
                        if c == 0:
                            step(b)
                        else:
                            b.then_inc(s_slot, 1)
                    assert k == RSTEPS

                def expert(e):
                    dve.wait_ge(s_fw, 48 * (e + 1))
                    dve.tensor_reduce(fm[:, 0:1], st_gu.rearrange("p k f -> p (k f)"), AX_X, ALU.max, apply_absolute_value=True)
                    dve.tensor_reduce(fm[:, 1:2], st_dn.rearrange("p c d -> p (c d)"), AX_X, ALU.max, apply_absolute_value=True).then_inc(s_fpm, 1)
                    dve.wait_ge(s_fam, e + 1)
                    k = 0

                    def step(ins):
                        nonlocal k
                        k += 1
                        ins.then_inc(s_fch, 1)
                        dve.wait_ge(s_fch, FSTEPS * e + k)

                    one = bass.ds(e, 1)
                    sc = f_scale[:, one, :].rearrange("p a n -> p (a n)")
                    step(dve.tensor_scalar(sc, fm[:, 2:4], 1e-30, 1e30, ALU.max, ALU.min))
                    step(dve.tensor_scalar(f_exp[:], sc.bitcast(I32), 0x7F800000, None, ALU.bitwise_and))
                    step(dve.tensor_scalar(sc.bitcast(I32), f_exp[:], -1.0, float((254 + TOP) << 23), ALU.mult, ALU.add))
                    step(dve.tensor_scalar(f_inv[:, one, :].rearrange("p a n -> p (a n)").bitcast(I32), f_exp[:], -float(TOP << 23), None, ALU.add))
                    gu = [w_gu[:, one, :, i, :].rearrange("p a k f -> p (a k) f") for i in range(2)]
                    dn = [w_dn[:, one, i, :, :].rearrange("p a c d -> p (a c) d") for i in range(2)]
                    dve.tensor_scalar(gu[0], st_gu, sc[:, 0:1], None, ALU.mult)
                    step(dve.tensor_scalar(dn[0], st_dn, sc[:, 1:2], None, ALU.mult))
                    dve.scalar_tensor_tensor(out=gu[1], in0=st_gu, scalar=sc[:, 0:1], in1=gu[0], op0=ALU.mult, op1=ALU.subtract)
                    dve.scalar_tensor_tensor(out=dn[1], in0=st_dn, scalar=sc[:, 1:2], in1=dn[0], op0=ALU.mult, op1=ALU.subtract).then_inc(s_fsp, 1)
                    assert k == FSTEPS

                FSTEPS = 5
                expert(0)
                route(0)
                with nc.vector.Fori(1, G) as g:
                    expert(g)
                    route(g)

                n = 0

                def step(ins):
                    nonlocal n
                    n += 1
                    ins.then_inc(s_tab, 1)
                    dve.wait_ge(s_tab, n)

                step(dve.tensor_scalar(n_tiles_i[:], count[:], float(P - 1), None, ALU.add))
                dve.tensor_copy(tail_f[:, 0:E], count[:])
                step(dve.memset(tail_f[:, E:E + 1], 0.0))
                step(dve.tensor_tensor(tail_f[:], tail_f[:], region9[:], ALU.add))
                step(dve.tensor_tensor(tail_f[:], tail_f[:], rank_p[:], ALU.add))
                dve.tensor_copy(tail_i[:], tail_f[:]).then_inc(s_tail, 1)
                step(dve.tensor_scalar(n_tiles_i[:], n_tiles_i[:], P.bit_length() - 1, None, ALU.logical_shift_right))
                step(dve.tensor_copy(n_tiles[:], n_tiles_i[:]))
                step(dve.tensor_copy(t_end[:], n_tiles[:]))
                for e in range(1, E):
                    step(dve.tensor_tensor(t_end[:, e:e + 1], t_end[:, e:e + 1], t_end[:, e - 1:e], ALU.add))
                step(dve.tensor_tensor(past[:], tile_iota[:].unsqueeze(2).to_broadcast([P, TF, E]), t_end[:].unsqueeze(1).to_broadcast([P, TF, E]), ALU.is_ge))
                step(dve.tensor_reduce(t_e[:], past[:], AX_X, ALU.add))
                step(dve.tensor_tensor(pick[:], past[:], n_tiles[:].unsqueeze(1).to_broadcast([P, TF, E]), ALU.mult))
                step(dve.tensor_reduce(t_s[:], pick[:], AX_X, ALU.add))
                step(dve.tensor_tensor(t_s[:], tile_iota[:], t_s[:], ALU.subtract))
                step(dve.tensor_scalar(t_row[:], t_e[:], float(E), float(P), ALU.is_lt, ALU.mult))
                step(dve.tensor_tensor(t_s[:], t_s[:], t_row[:], ALU.mult))
                step(dve.scalar_tensor_tensor(out=t_row[:], in0=t_e[:], scalar=float(REGION), in1=t_s[:], op0=ALU.mult, op1=ALU.add))
                dve.tensor_copy(t_row_i[:], t_row[:])
                step(dve.tensor_scalar(t_c[:], t_e[:], float(E - 1), None, ALU.min))
                step(dve.tensor_copy(t_e_i[:], t_c[:]))
                dve.tensor_scalar(tile_scales[:, 0, :], f_inv[:, :, 0], 1.0 / LN_SCALE, None, ALU.mult)
                dve.tensor_scalar(tile_scales[:, 1, :], f_scale[:, :, 0], 2.0 ** -31 / LN_SCALE, None, ALU.mult)
                step(dve.tensor_tensor(tile_scales[:, 2, :], f_inv[:, :, 0], f_inv[:, :, 0], ALU.mult))
                step(dve.tensor_tensor(tile_scales[:, 2, :], tile_scales[:, 2, :], f_inv[:, :, 1], ALU.mult))
                step(dve.tensor_scalar(tile_scales[:, 2, :], tile_scales[:, 2, :], 2.0 ** 31, consts[:, 1:2], ALU.mult, ALU.mult))
                step(dve.tensor_scalar(past[:, 0, :], rev[:], -1.0, float(E), ALU.mult, ALU.add))
                step(dve.tensor_tensor(pick[:], t_c[:].unsqueeze(2).to_broadcast([P, TF, E]), past[:, 0:1, :].to_broadcast([P, TF, E]), ALU.is_equal))
                for i in range(3):
                    step(dve.tensor_tensor(past[:], pick[:], tile_scales[:, i:i + 1, :].to_broadcast([P, TF, E]), ALU.mult))
                    step(dve.tensor_reduce(t_sc[i][:], past[:], AX_X, ALU.add))

        at2 = 0
        xg = [take2(ROW) for _ in range(U)]
        xg_hi = take2(KC * P // 2).bitcast(F16).rearrange("p (k n) -> p k n", k=KC)
        xg_lo = take2(KC * P // 2).bitcast(F16).rearrange("p (k n) -> p k n", k=KC)
        silu_s = take2(F)
        inter = take2(NF * P)
        it_hi = take2(NF * P // 2).bitcast(F16).rearrange("p (c n) -> p c n", c=NF)
        it_lo = take2(NF * P // 2).bitcast(F16).rearrange("p (c n) -> p c n", c=NF)
        ys = [take2(D) for _ in range(U)]
        fin = [take2(2 * J * D).rearrange("p (c j d) -> p c j d", c=2, j=J) for _ in range(2)]

        s_xg = [sem(f"tile_rows_loaded{i}") for i in range(U)]
        s_yo = [sem(f"tile_output_stored{i}") for i in range(U)]
        s_zin = sem("inter_padding_zero")
        s_gt = sem("tile_transposed")
        s_gth = sem("tile_high_ready")
        s_gtl = sem("tile_low_ready")
        s_gu = sem("gate_up_done")
        s_si = sem("silu_ready")
        s_in = sem("inter_ready")
        s_it = sem("inter_transposed")
        s_ith = sem("inter_high_ready")
        s_itl = sem("inter_low_ready")
        s_dn = sem("down_done")
        s_ys = sem("tile_output_ready")
        s_fin = [sem(f"expert_outputs_loaded{i}") for i in range(2)]
        s_add = sem("expert_outputs_added")
        s_sum = sem("group_summed")
        s_out = sem("out_stored")
        x_ps, g_ps, u_ps, i_ps, y_ps = (banks[:, i, :] for i in range(5))

        with nc.Block() as block:

            @block.sync
            def _(sp):
                def load(t, i, turn):
                    r = sp.value_load(t_row_i[0:1, bass.ds(t, 1)], min_val=0, max_val=E * REGION)
                    if turn is not None:
                        sp.wait_ge(s_yo[i], 16 * turn)
                    sp.dma_start(xg[i], rows_dram[bass.ds(r, P), :]).then_inc(s_xg[i], 16)

                for i in range(U):
                    load(i, i, None)
                with nc.sync.Fori(1, TF // U) as k:
                    for i in range(U):
                        load(k * U + i, i, k)

            @block.gpsimd
            def _(pool):
                def store(t, i):
                    pool.wait_ge(s_ys, t + 1)
                    pool.sem_inc(s_passed)
                    pool.indirect_dma_start(y_dram, bass.IndirectOffsetOnAxis(ap=xg[i][:, D + 1:D + 2].bitcast(I32), axis=0),
                                            ys[i], None, bounds_check=2 * B * T - 1, oob_is_err=False).then_inc(s_yo[i], 16)

                for i in range(U):
                    store(i, i)
                with nc.gpsimd.Fori(1, TF // U) as k:
                    for i in range(U):
                        store(k * U + i, i)
                for i in range(U):
                    pool.wait_ge(s_yo[i], 16 * (TF // U))

            @block.scalar
            def _(act):
                def high(t):
                    act.wait_ge(s_gt, t + 1)
                    act.activation(xg_hi, x_ps[:, 0:KC * P].rearrange("p (k n) -> p k n", k=KC), ACT.Copy).then_inc(s_gth, 1)

                def tile(t, last):
                    act.wait_ge(s_gu, t + 1)
                    act.activation(silu_s, g_ps[:, 0:F], ACT.Silu, scale=t_sc[0][:, bass.ds(t, 1)]).then_inc(s_si, 1)
                    if not last:
                        high(t + 1)
                    act.wait_ge(s_it, t + 1)
                    act.activation(it_hi, i_ps[:, 0:NF * P].rearrange("p (c n) -> p c n", c=NF), ACT.Copy).then_inc(s_ith, 1)

                high(0)
                for i in range(U):
                    tile(i, False)
                with nc.scalar.Fori(1, TF // U - 1) as k:
                    for i in range(U):
                        tile(k * U + i, False)
                for i in range(U):
                    tile(TF - U + i, i == U - 1)

            @block.vector
            def _(dve):
                dve.memset(inter, 0.0).then_inc(s_zin, 1)
                dve.wait_ge(s_zin, 1)

                def low(t):
                    dve.wait_ge(s_gth, t + 1)
                    dve.tensor_tensor(xg_lo, x_ps[:, 0:KC * P].rearrange("p (k n) -> p k n", k=KC), xg_hi, ALU.subtract).then_inc(s_gtl, 1)

                def output(t, i):
                    dve.wait_ge(s_dn, t + 1)
                    dve.tensor_scalar(ys[i], y_ps[:, 0:D], xg[i][:, D:D + 1], t_sc[2][:, bass.ds(t, 1)], ALU.mult, ALU.mult).then_inc(s_ys, 1)

                def tile(t, i, first, last):
                    dve.wait_ge(s_si, t + 1)
                    dve.scalar_tensor_tensor(out=inter[:, 0:F], in0=u_ps[:, 0:F], scalar=t_sc[1][:, bass.ds(t, 1)], in1=silu_s,
                                             op0=ALU.mult, op1=ALU.mult).then_inc(s_in, 1)
                    if not last:
                        low(t + 1)
                    if not first:
                        output(t - 1, (i - 1) % U)
                    dve.wait_ge(s_ith, t + 1)
                    dve.tensor_tensor(it_lo, i_ps[:, 0:NF * P].rearrange("p (c n) -> p c n", c=NF), it_hi, ALU.subtract).then_inc(s_itl, 1)

                low(0)
                for i in range(U):
                    tile(i, i, i == 0, False)
                with nc.vector.Fori(1, TF // U - 1) as k:
                    for i in range(U):
                        tile(k * U + i, i, False, False)
                for i in range(U):
                    tile(TF - U + i, i, False, i == U - 1)
                output(TF - 1, U - 1)

            @block.tensor
            def _(pe):
                def rows_t(t, i, turn):
                    pe.wait_ge(s_xg[i], 16 * turn)
                    for kc in range(KC):
                        mm = pe.transpose(x_ps[:, kc * P:(kc + 1) * P], xg[i][:, kc * P:(kc + 1) * P], ident[:])
                    mm.then_inc(s_gt, 1)

                def gate_up(t, e):
                    pe.wait_ge(s_gtl, t + 1)
                    for half, ps in ((0, g_ps), (1, u_ps)):
                        n = 0
                        for kc in range(KC):
                            for xh, w in ((xg_hi, 0), (xg_lo, 0), (xg_hi, 1)):
                                mm = pe.matmul(ps[:, 0:F], xh[:, kc, :], w_gu[:, e, kc, w, half * F:(half + 1) * F].rearrange("p a f -> p (a f)"),
                                               start=(n == 0), stop=(n == 3 * KC - 1))
                                n += 1
                    mm.then_inc(s_gu, 1)

                def down(t, e):
                    pe.wait_ge(s_itl, t + 1)
                    n = 0
                    for c in range(NF):
                        for ih, w in ((it_hi, 0), (it_lo, 0), (it_hi, 1)):
                            mm = pe.matmul(y_ps[:, 0:D], ih[:, c, :], w_dn[:, e, w, c, :].rearrange("p a d -> p (a d)"),
                                           start=(n == 0), stop=(n == 3 * NF - 1))
                            n += 1
                    mm.then_inc(s_dn, 1)

                def expert_of(t):
                    return bass.ds(pe.value_load(t_e_i[0:1, bass.ds(t, 1)], min_val=0, max_val=E - 1), 1)

                def tile(t, i, turn, first, last):
                    gate_up(t, expert_of(t))
                    if not last:
                        rows_t(t + 1, (i + 1) % U, turn + 1 if i == U - 1 else turn)
                    if not first:
                        before = expert_of(t - 1)
                        if not (isinstance(t, int) and t < 2):
                            pe.wait_ge(s_ys, t - 1)
                        down(t - 1, before)
                    pe.wait_ge(s_in, t + 1)
                    for c in range(NF):
                        mm = pe.transpose(i_ps[:, c * P:(c + 1) * P], inter[:, c * P:(c + 1) * P], ident[:])
                    mm.then_inc(s_it, 1)

                rows_t(0, 0, 1)
                for i in range(U):
                    tile(i, i, 1, i == 0, False)
                with nc.tensor.Fori(1, TF // U - 1) as k:
                    for i in range(U):
                        tile(k * U + i, i, k + 1, False, False)
                for i in range(U):
                    tile(TF - U + i, i, TF // U, False, i == U - 1)
                pe.wait_ge(s_ys, TF - 1)
                down(TF - 1, expert_of(TF - 1))

        with nc.Block() as block:

            @block.sync
            def _(sp):
                for g in range(G):
                    if g >= 2:
                        sp.wait_ge(s_sum, g - 1)
                    for c in range(2):
                        sp.dma_start(fin[g % 2][:, c], y_tiles[g, :, c]).then_inc(s_fin[g % 2], 16)

            @block.vector
            def _(dve):
                for g in range(G):
                    dve.wait_ge(s_fin[g % 2], 32 * (g // 2 + 1))
                    t = slice(g * J, (g + 1) * J)
                    dve.tensor_tensor(fin[g % 2][:, 0], fin[g % 2][:, 0], fin[g % 2][:, 1], ALU.add).then_inc(s_add, 1)
                    dve.wait_ge(s_add, g + 1)
                    dve.tensor_tensor(x_res[:, t, :], x_res[:, t, :], fin[g % 2][:, 0], ALU.add).then_inc(s_sum, 1)

            @block.scalar
            def _(act):
                for g in range(G):
                    act.wait_ge(s_sum, g + 1)
                    act.dma_start(out_tiles[g], x_res[:, g * J:(g + 1) * J, :]).then_inc(s_out, 16)
                act.wait_ge(s_out, 16 * G)


def kernel(**inputs):
    import numpy as _np
    import concourse.bacc as _bacc
    from concourse import mybir as _mybir
    from concourse.bass_utils import run_bass_kernel_spmd as _run

    a = {k: _np.asarray(v) for k, v in inputs.items()}
    vision = a["ctx_1024"]
    arrays = {
        "x": a["x"],
        "ctx": vision,
        "ctx_t": vision.reshape(-1, vision.shape[-1]).T,
        "mask": a["mask_BxS2_bf1"].view(_np.uint8),
        "g_xattn": a["g_xattn"],
        "g_ffn": a["g_ffn"],
        "wq_t": a["L0_xattn_Wq"].T,
        "wk_t": a["L0_xattn_Wk"].T,
        "wv_t": a["L0_xattn_Wv"].T,
        "wo": a["L0_xattn_Wo"],
        "gate_w_t": a["L0_ffn_gate_w"].T,
        "gate_b": a["L0_ffn_gate_b"],
        "expert_bias": a["L0_ffn_expert_bias"],
        "w_gu_t": a["L0_ffn_w_gate_up"].transpose(0, 2, 1),
        "w_down_t": a["L0_ffn_w_down"].transpose(0, 2, 1),
    }
    arrays = {f"in_{k}": _np.ascontiguousarray(v) for k, v in arrays.items()}
    nc = _bacc.Bacc("TRN2", target_bir_lowering=False, num_devices=1)
    args = [nc.dram_tensor(k, v.shape, _mybir.dt.from_np(v.dtype), kind="ExternalInput").ap() for k, v in arrays.items()]
    args.append(nc.dram_tensor("out_0", a["x"].shape, _mybir.dt.float32, kind="ExternalOutput").ap())
    bass_flamingo_gated_block(nc, *args)
    return _run(nc, [arrays], core_ids=[0]).results[0]["out_0"]
```

```python
from contextlib import ExitStack

import concourse.bass as bass
from concourse import mybir

F32 = mybir.dt.float32
F16 = mybir.dt.float16
I32 = mybir.dt.int32
U8 = mybir.dt.uint8
ALU = mybir.AluOpType
ACT = mybir.ActivationFunctionType
AX_X = mybir.AxisListType.X

P = 128


def bass_flamingo_gated_block(
    nc: bass.Bass,
    x: bass.AP,
    ctx: bass.AP,
    ctx_t: bass.AP,
    mask: bass.AP,
    g_xattn: bass.AP,
    g_ffn: bass.AP,
    wq_t: bass.AP,
    wk_t: bass.AP,
    wv_t: bass.AP,
    wo: bass.AP,
    gate_w_t: bass.AP,
    gate_b: bass.AP,
    expert_bias: bass.AP,
    w_gu_t: bass.AP,
    w_down_t: bass.AP,
    out: bass.AP,
):
    B, T, D = x.shape
    S, C = ctx.shape[1:]
    H = wq_t.shape[0] // P
    KV = wk_t.shape[0] // P
    E, _, GU = w_gu_t.shape
    F = GU // 2
    KC = D // P
    TILES = B * T // P
    J = 4
    G = TILES // J
    NB = J * P // T
    GT = J * P
    Q = 4
    HU = H // Q
    HP = HU // 2
    FC = [(0, 128), (128, 128), (256, F - 256)]
    NF = len(FC)
    EPS = 1e-5
    LN_SCALE = 1024.0
    TOP = 14
    NEG = -1.0e30
    assert T == S == 64 and C == P and D == 256 and KC == 2

    x_tiles = x.rearrange("b t d -> (b t) d").rearrange("(g j p) d -> g p j d", j=J, p=P)
    out_tiles = out.rearrange("b t d -> (b t) d").rearrange("(g j p) d -> g p j d", j=J, p=P)
    ctx_tiles = ctx.rearrange("b s c -> (b s) c").rearrange("(g j p) c -> g p j c", j=J, p=P)
    ctx_t_groups = ctx_t.rearrange("c (g n) -> g c n", g=G)
    mask_groups = mask.rearrange("b s -> (b s)").rearrange("(g a n) -> g a n", g=G, a=1)

    es = ExitStack()
    with es:
        def sb(name, shape, dt=F32):
            return es.enter_context(nc.sbuf_tensor(name, shape, dt))

        def sem(name):
            return es.enter_context(nc.semaphore(name))

        x_res = sb("x_res", [P, TILES, D])
        MNW = H * D // 2
        mn = sb("mn", [P, 4 * MNW])
        m_hi, m_lo = (mn[:, i * MNW:(i + 1) * MNW].bitcast(F16).rearrange("p (k h c) -> p k h c", k=KC, h=H) for i in (0, 1))
        n_hi, n_lo = (mn[:, i * MNW:(i + 1) * MNW].bitcast(F16).rearrange("p (h d) -> p h d", h=H) for i in (2, 3))
        ident = sb("ident", [P, P])
        ones = sb("ones", [32, P])
        xn = sb("xn", [P, J, D])
        mean_var = sb("mean_var", [P, TILES, 2])
        stats = sb("stats", [P, TILES, 6])
        rstd = sb("rstd", [P, TILES])
        nwt = sb("nwt", [P, 3, TILES])
        NM = 3 + 2 * E
        mx_part = sb("mx_part", [P, NM])
        mx_col = sb("mx_col", [32, 1])
        mx_diag = sb("mx_diag", [32, NM])
        mx_exp = sb("mx_exp", [P, NM], I32)
        scale_of = sb("scale_of", [P, NM])
        inv_of = sb("inv_of", [P, NM])
        gates = sb("gates", [P, 2])
        consts = sb("consts", [P, 8])
        EW = KC * GU + 3 * D
        EARLY = E - 2
        PH1 = 8 * 1024
        AUX = 2 * EW
        big = sb("big", [P, EARLY * EW + PH1 + AUX])
        stage = big[:, 0:EARLY * EW]
        work = big[:, EARLY * EW:EARLY * EW + PH1]
        aux = big[:, EARLY * EW + PH1:]

        banks = es.enter_context(nc.psum_tensor("banks", [P, 8, 512], F32))
        acc = banks[:, 0:2, :].rearrange("p b n -> p (b n)").rearrange("p (j d) -> p j d", j=J)
        sp_ps = banks[:, 2:4, :]
        xo_ps = banks[:, 4:8, :]

        wq_s = stage[:, 0:H * D].rearrange("p (h d) -> p h d", h=H)
        wk_s = stage[:, 4096:4096 + KV * C].rearrange("p (h c) -> p h c", h=KV)
        wv_s = stage[:, 5120:5120 + KV * C].rearrange("p (h c) -> p h c", h=KV)
        wo_s = stage[:, 6144:6144 + H * D].rearrange("p (h d) -> p h d", h=H)
        ctx_all = aux[:, 0:TILES * C]
        mf = work[:, 0:4096].rearrange("p (k h c) -> p k h c", k=KC, h=H)
        nf = work[:, 4096:8192].rearrange("p (h d) -> p h d", h=H)
        at = 0

        def take(words):
            nonlocal at
            at += words
            assert at <= PH1
            return work[:, at - words:at]

        xm = [take(HU * GT).rearrange("p (a b c t) -> p a c b t", a=HP, b=NB, c=2) for _ in range(2)]
        sm = take(HP * GT).rearrange("p (a n) -> p a n", a=HP)
        pr = pn = sm
        pt = take(HP * GT).rearrange("p (j a n) -> p j a n", j=J, a=HP)
        o_hi = take(HU * GT // 2).bitcast(F16).rearrange("p (h n) -> p h n", h=HU)
        o_lo = take(HU * GT // 2).bitcast(F16).rearrange("p (h n) -> p h n", h=HU)
        ctx_t_s = [sb(f"ctx_t_s{i}", [P, GT]) for i in range(2)]
        ctx_s = [sb(f"ctx_s{i}", [P, J, C]) for i in range(2)]
        mask_u = [sb(f"mask_u{i}", [P, GT], U8) for i in range(2)]
        mask_b = [sb(f"mask_b{i}", [P, GT]) for i in range(2)]
        any_of = [sb(f"any_of{i}", [P, NB]) for i in range(2)]
        xt_hi = [sb(f"xt_hi{i}", [P, KC, GT], F16) for i in range(2)]
        xt_lo = [sb(f"xt_lo{i}", [P, KC, GT], F16) for i in range(2)]
        nmax = sb("nmax", [P, HP * NB])
        rsum = sb("rsum", [P, HP * NB])
        rinv = sb("rinv", [P, HP * NB])


        def by_batch(hh):
            return xo_ps[:, hh, :].rearrange("p (b t) -> p b t", b=NB)

        def o_view(o, bank):
            half, b2 = bank // 2, bank % 2
            return o.rearrange("p h (j b t) -> p h j b t", j=J, b=2)[:, :, 2 * half:2 * half + 2, b2, :]

        s_x = [sem(f"x_loaded{g}") for g in range(G)]
        s_w = [sem(f"setup_weights_loaded{i}") for i in range(5)]
        s_g = sem("gates_loaded")
        s_ident = sem("ident_ready")
        s_ctx = [sem(f"ctx_loaded{i}") for i in range(2)]
        s_dve = sem("dve_setup_step")
        s_act = sem("act_setup_step")
        s_stat = sem("ln1_rstd_ready")
        s_var = sem("ln1_variance_ready")
        s_mxp = sem("partial_maxima_ready")
        s_mprod = sem("m_product_done")
        s_mcopied = sem("m_product_copied")
        s_nprod = sem("n_product_done")
        s_ncopied = sem("n_product_copied")
        s_maxt = sem("maxima_transposed")
        s_maxd = sem("maxima_diagonal")
        s_maxb = sem("maxima_broadcast")
        s_scale = sem("scales_ready")
        s_wready = sem("m_n_split")
        s_tanh = sem("tanh_ready")
        s_xnorm = sem("x_normalised")
        s_xt = sem("x_transposed")
        s_xth = sem("xt_high_ready")
        s_xtl = sem("xt_low_ready")
        s_cscale = sem("ctx_scaled")
        s_mbias = sem("mask_bias_ready")
        s_manyof = sem("mask_any_ready")
        s_xm = sem("xm_head_done")
        s_xma = sem("xm_copied_by_act")
        s_xmd = sem("xm_copied_by_dve")
        s_sc = sem("scores_done")
        s_msk = sem("scores_masked")
        s_max = sem("row_max_ready")
        s_exp = sem("exp_done")
        s_ri = sem("row_inverse_step")
        s_pnp = sem("first_pair_normalised")
        s_pnd = sem("second_pair_normalised")
        s_pt = sem("probs_transposed")
        s_pta = sem("pt_copied_by_act")
        s_ptd = sem("pt_copied_by_dve")
        s_pv = sem("head_outputs_done")
        s_oh = sem("outputs_high_ready")
        s_ol = sem("outputs_low_ready")
        s_on = sem("projection_done")
        s_x1 = sem("x1_ready")

        ROW = D + 2
        REGION = B * T + P
        SKIP = 1 << 20
        TF = 72
        U = 8
        assert 2 * B * T // P + E - 1 <= TF and TF % U == 0
        rows_dram = nc.dram_tensor("expert_rows", [(E + 1) * REGION, ROW], F32, kind="Internal").ap()
        y_dram = nc.dram_tensor("expert_outputs", [2 * B * T, D], F32, kind="Internal").ap()
        y_tiles = y_dram.rearrange("(c g j p) d -> g p c j d", c=2, j=J, p=P)

        ew32 = big[:, 0:E * EW].rearrange("p (e x) -> p e x", e=E)
        ew16 = big[:, 0:E * EW].bitcast(F16).rearrange("p (e x) -> p e x", e=E)
        NGU = KC * GU
        pieces = [(0, GU, 0), (GU, GU, 0), (NGU, NF * D, 1)]
        w_gu = ew16[:, :, 0:2 * NGU].rearrange("p e (k w f) -> p e k w f", k=KC, w=2)
        w_dn = ew16[:, :, 2 * NGU:].rearrange("p e (w c d) -> p e w c d", w=2, c=NF)
        late32 = mn[:, 0:2 * EW].rearrange("p (e x) -> p e x", e=2)
        at_aux = 0

        def take_aux(words):
            nonlocal at_aux
            at_aux += words
            assert at_aux <= AUX
            return aux[:, at_aux - words:at_aux]

        row = [take_aux(J * ROW).rearrange("p (j r) -> p j r", j=J) for _ in range(2)]
        xt32 = take_aux(KC * GT).rearrange("p (k n) -> p k n", k=KC)
        zero_row = take_aux(ROW)
        split_tmp = take_aux(NF * D)
        fm = sb("fm", [P, 4])
        fm_late = sb("fm_late", [P, 8])
        f_exp = sb("f_exp", [P, 4], I32)
        f_scale = sb("f_scale", [P, E, 2])
        f_inv = sb("f_inv", [P, E, 2])
        tile_scales = sb("tile_scales", [P, 3, E])
        gate_w_s = sb("gate_w_s", [P, KC, E])
        gate_b_s = sb("gate_b_s", [P, E])
        bias_s = sb("bias_s", [P, E])
        strict = sb("strict", [P, P])
        ones_sq = sb("ones_sq", [P, P])
        place = [sb(f"place{c}", [P, TILES], I32) for c in range(2)]
        rev = sb("rev", [P, E])
        region0 = sb("region0", [P, E])
        count = sb("count", [P, E])
        tile_iota = sb("tile_iota", [P, TF])
        rank_p = sb("rank_p", [P, E + 1])
        c_1p5 = sb("c_1p5", [P, J])
        c_ln = sb("c_ln", [P, J])
        stat2 = sb("stat2", [P, J, 6])
        mv2 = sb("mv2", [P, J, 2])
        v2 = sb("v2", [P, J])
        v2_mhalf = sb("v2_mhalf", [P, J])
        y2 = sb("y2", [P, J])
        t2 = sb("t2", [P, J])
        lg = sb("lg", [P, J, E])
        ex = sb("ex", [P, J, E])
        rt = sb("rt", [P, J, E])
        rt2 = sb("rt2", [P, J, E])
        key = sb("key", [P, J, E])
        half4 = sb("half4", [P, J, E // 2])
        half2 = sb("half2", [P, J, E // 4])
        best = sb("best", [P, J])
        oh = [sb(f"oh{c}", [P, J, E]) for c in range(2)]
        chosen = sb("chosen", [P, J, E])
        pos = sb("pos", [P, J, E])
        red = sb("red", [P, J])
        rsum2 = sb("rsum2", [P, J])
        slot_f = sb("slot_f", [P, 2, J])
        slot = sb("slot", [P, 2, J], I32)
        n_tiles = sb("n_tiles", [P, E])
        n_tiles_i = sb("n_tiles_i", [P, E], I32)
        t_end = sb("t_end", [P, E])
        t_e_i = sb("t_e_i", [P, TF], I32)
        t_row_i = sb("t_row_i", [P, TF], I32)
        t_sc = [sb(f"t_sc{i}", [P, TF]) for i in range(3)]
        tail_i = sb("tail_i", [P, E + 1], I32)
        tail_f = sb("tail_f", [P, E + 1])
        at_t = 2 * EW

        def take_mn(words):
            nonlocal at_t
            at_t += words
            assert at_t <= 4 * MNW
            return mn[:, at_t - words:at_t]

        past = take_mn(TF * E).rearrange("p (t e) -> p t e", t=TF)
        pick = take_mn(TF * E).rearrange("p (t e) -> p t e", t=TF)
        t_e, t_c, t_s, t_row = (take_mn(TF) for _ in range(4))

        s_small = sem("router_constants_loaded")
        s_iota = sem("iotas_ready")
        s_fw = sem("expert_weights_loaded")
        s_fwl = sem("late_expert_weights_loaded")
        s_pad = sem("expert_padding_zero")
        s_fpm = sem("expert_partial_max")
        s_fam = sem("expert_max_everywhere")
        s_fch = sem("expert_scale_step")
        s_fsp = sem("expert_split_step")
        s_flate = sem("late_expert_step")
        s_rs = sem("stats_step")
        s_seed = sem("rstd_seed_ready")
        s_nw = sem("newton_step")
        s_rstd = sem("ln2_rstd_ready")
        s_row = sem("first_rows_ready")
        s_row1 = sem("second_rows_ready")
        s_x2t = sem("x2_transposed")
        s_x2c = sem("x2_transposed_copied")
        s_lg = sem("logits_done")
        s_sh = sem("logits_step")
        s_l1 = sem("logits_shifted")
        s_ex = sem("logits_exponentials")
        s_sm = sem("exponentials_summed")
        s_tk = sem("top2_step")
        s_cho = sem("choices_ready")
        s_pos = sem("positions_done")
        s_pc = sem("position_step")
        s_posr = sem("positions_ready")
        s_sl = sem("slot_step")
        s_scat = sem("rows_scattered")
        s_passed = sem("pool_passed")
        s_passed_v = sem("dve_passed")
        s_passed_s = sem("sp_passed")
        s_tail = sem("tail_places_ready")
        s_tab = sem("tile_tables_ready")

        def sum_experts(step, src, out):
            step(half4[:], src[:, :, 0:E // 2], src[:, :, E // 2:E], ALU.add)
            step(half2[:], half4[:, :, 0:E // 4], half4[:, :, E // 4:E // 2], ALU.add)
            step(out, half2[:, :, 0], half2[:, :, 1], ALU.add)

        def over_e(v):
            return v.unsqueeze(2).to_broadcast([P, J, E])

        def over_j(v):
            return v.unsqueeze(1).to_broadcast([P, J, E])

        IOTAS = 14
        RS, NW, SH, SM, TK, SL, PC = 4, 12, 2, 4, 12, 9, 2

        def route_stats(dve, r):
            dve.wait_ge(s_x1, r + 1)
            if not (isinstance(r, int) and r < 1):
                dve.wait_ge(s_row1, r)
            dve.sem_inc(s_passed_v)
            for j in range(J):
                b = dve.bn_stats(stat2[:, j, :], x_res[:, bass.ds(r * J + j, 1), :].rearrange("p a d -> p (a d)"))
            b.then_inc(s_rs, 1)
            dve.wait_ge(s_rs, RS * r + 1)
            dve.sem_inc(s_passed_v)
            for j in range(J):
                b = dve.bn_aggr(mv2[:, j, :], stat2[:, j, :])
            b.then_inc(s_rs, 1)
            dve.wait_ge(s_rs, RS * r + 2)
            dve.tensor_scalar(v2[:], mv2[:, :, 1], EPS, None, ALU.add).then_inc(s_rs, 1)
            dve.wait_ge(s_rs, RS * r + 3)
            dve.tensor_scalar(v2_mhalf[:], v2[:], -0.5, None, ALU.mult)
            dve.tensor_scalar(y2[:].bitcast(I32), v2[:].bitcast(I32), 1, None, ALU.logical_shift_right).then_inc(s_rs, 1)
            dve.wait_ge(s_rs, RS * r + 4)
            dve.tensor_scalar(y2[:].bitcast(I32), y2[:].bitcast(I32), -1.0, float(0x5F3759DF), ALU.mult, ALU.add).then_inc(s_seed, 1)

        def route_newton(pool, r):
            k = 0
            pool.wait_ge(s_seed, r + 1)
            for _ in range(3):
                for o, a, b in ((t2, y2, y2), (t2, t2, v2_mhalf), (t2, t2, c_1p5), (y2, y2, t2)):
                    pool.tensor_tensor(o[:], a[:], b[:], ALU.add if b is c_1p5 else ALU.mult).then_inc(s_nw, 1)
                    k += 1
                    pool.wait_ge(s_nw, NW * r + k)
            assert k == NW
            pool.tensor_tensor(y2[:], y2[:], c_ln[:], ALU.mult).then_inc(s_rstd, 1)

        def route_row(dve, r, c):
            for j in range(J):
                b = dve.tensor_scalar(row[c][:, j, 0:D], x_res[:, bass.ds(r * J + j, 1), :].rearrange("p a d -> p (a d)"),
                                      mv2[:, j, 0:1], y2[:, j:j + 1], ALU.subtract, ALU.mult)
            return b

        def route_rows_first(dve, r):
            dve.wait_ge(s_rstd, r + 1)
            if not (isinstance(r, int) and r < 1):
                dve.wait_ge(s_scat, 16 * 2 * J * r)
            route_row(dve, r, 0).then_inc(s_row, 1)

        def route_rows_second(dve, r):
            route_row(dve, r, 1)
            for c in range(2):
                b = dve.tensor_copy(row[c][:, :, D + 1].bitcast(I32), place[c][:, bass.ds(r * J, J)])
            b.then_inc(s_row1, 1)

        def route_transposes(pe, r):
            pe.wait_ge(s_row, r + 1)
            for kc in range(KC):
                for j in range(J):
                    mm = pe.transpose(sp_ps[:, kc, j * P:(j + 1) * P], row[0][:, j, kc * P:(kc + 1) * P], ident[:])
            mm.then_inc(s_x2t, 1)

        def route_copy(dve, r):
            dve.wait_ge(s_x2t, r + 1)
            if not (isinstance(r, int) and r < 1):
                dve.wait_ge(s_lg, r)
            dve.tensor_copy(xt32, sp_ps).then_inc(s_x2c, 1)

        def route_logits(pe, r):
            pe.wait_ge(s_x2c, r + 1)
            for j in range(J):
                for kc in range(KC):
                    mm = pe.matmul(banks[:, 6, j * E:(j + 1) * E], xt32[:, kc, j * P:(j + 1) * P], gate_w_s[:, kc, :],
                                   start=(kc == 0), stop=(kc == KC - 1))
            mm.then_inc(s_lg, 1)

        def route_shift(dve, r):
            dve.wait_ge(s_lg, r + 1)
            if not (isinstance(r, int) and r < 1):
                dve.wait_ge(s_cho, r)
            dve.scalar_tensor_tensor(out=rt[:], in0=banks[:, 6, 0:J * E].rearrange("p (j e) -> p j e", j=J), scalar=1.0 / LN_SCALE,
                                     in1=over_j(gate_b_s[:]), op0=ALU.mult, op1=ALU.add).then_inc(s_sh, 1)
            dve.wait_ge(s_sh, SH * r + 1)
            dve.tensor_reduce(red[:], rt[:], AX_X, ALU.max).then_inc(s_sh, 1)
            dve.wait_ge(s_sh, SH * r + 2)
            dve.tensor_tensor(lg[:], rt[:], over_e(red[:]), ALU.subtract).then_inc(s_l1, 1)

        def route_exp(act, r):
            act.wait_ge(s_l1, r + 1)
            if not (isinstance(r, int) and r < 1):
                act.wait_ge(s_cho, r)
            act.activation(ex[:], lg[:], ACT.Exp).then_inc(s_ex, 1)

        def route_weights(dve, r):
            dve.wait_ge(s_ex, r + 1)
            dve.tensor_reduce(rsum2[:], ex[:], AX_X, ALU.add).then_inc(s_sm, 1)
            dve.wait_ge(s_sm, SM * r + 1)
            dve.reciprocal(rsum2[:], rsum2[:]).then_inc(s_sm, 1)
            dve.wait_ge(s_sm, SM * r + 2)
            dve.tensor_tensor(rt[:], ex[:], over_e(rsum2[:]), ALU.mult).then_inc(s_sm, 1)
            dve.wait_ge(s_sm, SM * r + 3)
            dve.tensor_tensor(rt[:], rt[:], over_j(bias_s[:]), ALU.add).then_inc(s_sm, 1)

        def route_choice(dve, r, c):
            k = TK // 2 * c

            def step(ins):
                nonlocal k
                k += 1
                ins.then_inc(s_tk, 1)
                dve.wait_ge(s_tk, TK * r + k)

            if c == 0:
                dve.wait_ge(s_sm, SM * (r + 1))
            src, weight = (rt, rt2)[c], row[c][:, :, D]
            step(dve.tensor_reduce(weight, src[:], AX_X, ALU.max))
            step(dve.tensor_tensor(key[:], src[:], over_e(weight), ALU.is_equal))
            step(dve.tensor_tensor(key[:], key[:], over_j(rev[:]), ALU.mult))
            step(dve.tensor_reduce(best[:], key[:], AX_X, ALU.max))
            step(dve.tensor_tensor(oh[c][:], key[:], over_e(best[:]), ALU.is_equal))
            if c == 0:
                step(dve.scalar_tensor_tensor(out=rt2[:], in0=oh[0][:], scalar=NEG, in1=rt[:], op0=ALU.mult, op1=ALU.add))
            else:
                step(dve.tensor_tensor(chosen[:], oh[0][:], oh[1][:], ALU.add))
                dve.sem_inc(s_cho)

        def route_positions(pe, r):
            pe.wait_ge(s_cho, r + 1)
            pe.matmul(banks[:, 6, 0:J * E], strict[:], chosen[:].rearrange("p j e -> p (j e)"), start=True, stop=False, skip_group_check=True)
            for n in range(J - 1, 0, -1):
                pe.matmul(banks[:, 6, (J - n) * E:J * E], ones_sq[:], chosen[:, 0:n, :].rearrange("p j e -> p (j e)"),
                          start=False, stop=(n == 1), skip_group_check=True)
            for j in range(J):
                mm = pe.matmul(banks[:, 7, 0:E], ones_sq[:], chosen[:, j, :], start=(j == 0), stop=(j == J - 1))
            mm.then_inc(s_pos, 1)

        def route_places(dve, r):
            dve.wait_ge(s_pos, r + 1)
            dve.tensor_tensor(pos[:], banks[:, 6, 0:J * E].rearrange("p (j e) -> p j e", j=J), over_j(count[:]), ALU.add).then_inc(s_pc, 1)
            dve.wait_ge(s_pc, PC * r + 1)
            dve.tensor_tensor(count[:], banks[:, 7, 0:E], count[:], ALU.add).then_inc(s_pc, 1)
            dve.wait_ge(s_pc, PC * r + 2)
            dve.sem_inc(s_posr)

        def route_scatter(pool, r):
            k = 0

            def step(out, a, b, op):
                nonlocal k
                k += 1
                pool.tensor_tensor(out, a, b, op).then_inc(s_sl, 1)
                pool.wait_ge(s_sl, SL * r + k)

            pool.wait_ge(s_posr, r + 1)
            for c in range(2):
                step(oh[c][:], oh[c][:], pos[:], ALU.mult)
                sum_experts(step, oh[c], slot_f[:, c, :])
            pool.sem_inc(s_passed)
            pool.tensor_copy(slot[:], slot_f[:]).then_inc(s_sl, 1)
            assert k + 1 == SL
            pool.wait_ge(s_sl, SL * (r + 1))
            pool.sem_inc(s_passed)
            for c in range(2):
                for j in range(J):
                    pool.indirect_dma_start(rows_dram, bass.IndirectOffsetOnAxis(ap=slot[:, c, j:j + 1], axis=0),
                                            row[c][:, j, :], None).then_inc(s_scat, 16)

        def load_expert(sp, e, words, done):
            dn = words[:, NGU:EW].rearrange("p (c d) -> p c d", c=NF)
            sp.dma_start(words[:, 0:NGU].rearrange("p (k f) -> p k f", k=KC), w_gu_t[e].rearrange("(k p) f -> p k f", p=P)).then_inc(done, 16)
            sp.dma_start(dn[:, 0:2, :], w_down_t[e, 0:2 * P, :].rearrange("(c p) d -> p c d", p=P)).then_inc(done, 16)
            sp.dma_start(dn[0:F - 2 * P, 2, :], w_down_t[e, 2 * P:F, :]).then_inc(done, 16)

        def expert_max(dve, e):
            dve.wait_ge(s_fw, 48 * EARLY)
            if not (isinstance(e, int) and e < 1):
                dve.wait_ge(s_fam, e)
            one = bass.ds(e, 1)
            dve.tensor_reduce(fm[:, 0:1], ew32[:, one, 0:NGU].rearrange("p a x -> p (a x)"), AX_X, ALU.max, apply_absolute_value=True)
            dve.tensor_reduce(fm[:, 1:2], ew32[:, one, NGU:EW].rearrange("p a x -> p (a x)"), AX_X, ALU.max, apply_absolute_value=True).then_inc(s_fpm, 1)

        def expert_max_all(pool, e):
            pool.wait_ge(s_fpm, e + 1)
            pool.sem_inc(s_passed)
            pool.partition_all_reduce(fm[:, 2:4], fm[:, 0:2], P, bass.bass_isa.ReduceOp.max).then_inc(s_fam, 1)

        def powers_of_two(step, scale, inv, exponent, maxima):
            step(lambda v: v.tensor_scalar(scale, maxima, 1e-30, 1e30, ALU.max, ALU.min))
            step(lambda v: v.tensor_scalar(exponent, scale.bitcast(I32), 0x7F800000, None, ALU.bitwise_and))
            step(lambda v: v.tensor_scalar(scale.bitcast(I32), exponent, -1.0, float((254 + TOP) << 23), ALU.mult, ALU.add))
            step(lambda v: v.tensor_scalar(inv.bitcast(I32), exponent, -float(TOP << 23), None, ALU.add))

        def expert_scale(dve, e):
            dve.wait_ge(s_fam, e + 1)
            one = bass.ds(e, 1)
            k = 0

            def step(make):
                nonlocal k
                k += 1
                make(dve).then_inc(s_fch, 1)
                dve.wait_ge(s_fch, 4 * e + k)

            powers_of_two(step, f_scale[:, one, :].rearrange("p a n -> p (a n)"), f_inv[:, one, :].rearrange("p a n -> p (a n)"),
                          f_exp[:, 0:2], fm[:, 2:4])
            dve.sem_inc(s_passed_v)

        def expert_split(pool, e, i):
            first, n, which = pieces[i]
            one = bass.ds(e, 1)
            if i == 0:
                pool.wait_ge(s_fch, 4 * (e + 1))
            full = ew32[:, one, first:first + n].rearrange("p a x -> p (a x)")
            hi = ew16[:, one, 2 * first:2 * first + n].rearrange("p a x -> p (a x)")
            lo = ew16[:, one, 2 * first + n:2 * (first + n)].rearrange("p a x -> p (a x)")
            tmp = split_tmp[:, 0:n]
            steps = ((tmp, full, f_scale[:, one, which].to_broadcast([P, n]), ALU.mult), (hi, tmp, ones_sq[:, 0:1].to_broadcast([P, n]), ALU.mult), (lo, tmp, hi, ALU.subtract))
            for k, (out, a, b, op) in enumerate(steps):
                pool.tensor_tensor(out, a, b, op).then_inc(s_fsp, 1)
                pool.wait_ge(s_fsp, 9 * e + 3 * i + k + 1)
            pool.sem_inc(s_passed)

        def link(eng, sem_, chain, ins):
            chain[0] += 1
            ins.then_inc(sem_, 1)
            eng.wait_ge(sem_, chain[0])

        with nc.Block() as block:

            @block.sync
            def _(sp):
                sp.dma_start(wq_s, wq_t.rearrange("(h p) d -> p h d", p=P)).then_inc(s_w[0], 16)
                sp.dma_start(wk_s, wk_t.rearrange("(h p) c -> p h c", p=P)).then_inc(s_w[1], 16)
                sp.dma_start(wv_s, wv_t.rearrange("(h p) c -> p h c", p=P)).then_inc(s_w[2], 16)
                sp.dma_start(wo_s, wo.rearrange("(h p) d -> p h d", p=P)).then_inc(s_w[3], 16)
                for g in range(G):
                    sp.dma_start(x_res[:, g * J:(g + 1) * J, :], x_tiles[g]).then_inc(s_x[g], 16)
                sp.dma_start(ctx_all.rearrange("p (t c) -> p t c", t=TILES),
                             ctx.rearrange("b s c -> (b s) c").rearrange("(t p) c -> p t c", p=P)).then_inc(s_w[4], 16)

                def load_group(g, b):
                    if not (isinstance(g, int) and g < 2):
                        sp.wait_ge(s_on, Q * (g - 1))
                        sp.sem_inc(s_passed_s)
                        sp.wait_ge(s_msk, 2 * Q * (g - 1))
                        sp.wait_ge(s_manyof, g - 1)
                    sp.dma_start(ctx_t_s[b][:], ctx_t_groups[bass.ds(g, 1), :, :].rearrange("a c n -> c (a n)")).then_inc(s_ctx[b], 16)
                    sp.dma_start(ctx_s[b][:], ctx_tiles[bass.ds(g, 1), :, :, :].rearrange("a p j c -> p (a j) c")).then_inc(s_ctx[b], 16)
                    sp.dma_start(mask_u[b][:], mask_groups[bass.ds(g, 1), :, :].rearrange("a b n -> (a b) n").to_broadcast([P, GT])).then_inc(s_ctx[b], 16)

                load_group(0, 0)
                load_group(1, 1)
                sp.dma_start(gate_w_s[:], gate_w_t.rearrange("(k p) e -> p k e", p=P)).then_inc(s_small, 16)
                sp.dma_start(gate_b_s[:], gate_b.rearrange("(a e) -> a e", a=1).to_broadcast([P, E])).then_inc(s_small, 16)
                sp.dma_start(bias_s[:], expert_bias.rearrange("(a e) -> a e", a=1).to_broadcast([P, E])).then_inc(s_small, 16)
                sp.wait_ge(s_pad, 1)
                for e in range(EARLY):
                    load_expert(sp, e, ew32[:, e, :], s_fw)
                with nc.sync.Fori(0, (G - 2) // 2) as k:
                    load_group(2 + 2 * k, 0)
                    load_group(3 + 2 * k, 1)

            @block.gpsimd
            def _(pool):
                pool.memset(ident[:], 0.0).then_inc(s_ident, 1)
                pool.memset(ones[:], 1.0).then_inc(s_ident, 1)
                pool.wait_ge(s_ident, 2)
                pool.affine_select(out=ident[:], in_=ident[:], compare_op=ALU.not_equal, fill=1.0, base=0,
                                   pattern=[[-1, P]], channel_multiplier=1).then_inc(s_ident, 1)

                n = 0

                def made(ins):
                    nonlocal n
                    n += 1
                    ins.then_inc(s_iota, 1)

                made(pool.memset(ones_sq[:], 1.0))
                made(pool.memset(strict[:], 0.0))
                pool.wait_ge(s_iota, n)
                made(pool.affine_select(out=strict[:], in_=strict[:], compare_op=ALU.is_ge, fill=1.0, base=0,
                                        pattern=[[-1, P]], channel_multiplier=1))
                made(pool.memset(c_1p5[:], 1.5))
                made(pool.memset(c_ln[:], LN_SCALE))
                for c in range(2):
                    made(pool.iota(place[c][:], pattern=[[P, TILES]], base=c * B * T, channel_multiplier=1))
                made(pool.iota(rev[:], pattern=[[-1, E]], base=E, channel_multiplier=0, allow_small_or_imprecise_dtypes=True))
                made(pool.iota(region0[:], pattern=[[REGION, E]], base=0, channel_multiplier=0, allow_small_or_imprecise_dtypes=True))
                made(pool.iota(count[:], pattern=[[REGION, E]], base=0, channel_multiplier=0, allow_small_or_imprecise_dtypes=True))
                made(pool.iota(rank_p[:], pattern=[[0, E + 1]], base=0, channel_multiplier=1, allow_small_or_imprecise_dtypes=True))
                made(pool.iota(tile_iota[:], pattern=[[1, TF]], base=0, channel_multiplier=0, allow_small_or_imprecise_dtypes=True))
                pool.wait_ge(s_nprod, H // 2)
                pool.memset(ew32[:, 0:EARLY, NGU + 2 * D:EW], 0.0).then_inc(s_pad, 1)
                pool.wait_ge(s_mxp, 1)
                made(pool.memset(zero_row[:, 0:D + 1], 0.0))
                made(pool.iota(zero_row[:, D + 1:D + 2].bitcast(I32), pattern=[[0, 1]], base=SKIP, channel_multiplier=0))
                assert n == IOTAS
                pool.wait_ge(s_iota, IOTAS)
                pool.wait_ge(s_small, 48)

                def normalise_probs(u):
                    pool.wait_ge(s_ri, 4 * u + 2)
                    pool.tensor_tensor(pn[:, 0, :].rearrange("p (b s) -> p b s", s=S), pr[:, 0, :].rearrange("p (b s) -> p b s", s=S),
                                       rinv[:, 0:NB].unsqueeze(2).to_broadcast([P, NB, S]), ALU.mult).then_inc(s_pnp, 1)

                def group(g, route, experts):
                    for q in range(Q):
                        normalise_probs(Q * g + q)
                        if q == 0 and experts:
                            expert_max_all(pool, g - 1)
                        if q == 0 and route:
                            route_newton(pool, g - 1)
                        if q == 1 and experts:
                            expert_split(pool, g - 1, 0)
                            expert_split(pool, g - 1, 1)
                        if q == 2 and experts:
                            expert_split(pool, g - 1, 2)
                        if q == 3 and route:
                            route_scatter(pool, g - 1)

                group(0, False, False)
                with nc.gpsimd.Fori(0, (G - 2) // 2) as k:
                    group(1 + 2 * k, True, True)
                    group(2 + 2 * k, True, True)
                group(G - 1, True, False)

            @block.scalar
            def _(act):
                act.dma_start(gates[:, 0:1], g_xattn.rearrange("(a n) -> a n", a=1).to_broadcast([P, 1])).then_inc(s_g, 16)
                act.dma_start(gates[:, 1:2], g_ffn.rearrange("(a n) -> a n", a=1).to_broadcast([P, 1])).then_inc(s_g, 16)
                for i in range(H * KC // 4):
                    act.wait_ge(s_mprod, i + 1)
                    kc, hq = i % KC, i // KC
                    act.activation(mf[:, kc, 4 * hq:4 * hq + 4, :].rearrange("p h c -> p (h c)"), banks[:, i % 8, :], ACT.Copy).then_inc(s_mcopied, 1)
                for i in range(H // 2):
                    act.wait_ge(s_nprod, i + 1)
                    act.activation(nf[:, 2 * i:2 * i + 2, :].rearrange("p h d -> p (h d)"), banks[:, i % 8, :], ACT.Copy).then_inc(s_ncopied, 1)
                act.wait_ge(s_var, 1)
                act.activation(nwt[:, 0, :], nwt[:, 1, :], ACT.Sqrt).then_inc(s_act, 1)
                act.wait_ge(s_g, 32)
                act.activation(consts[:, 0:2], gates[:], ACT.Tanh).then_inc(s_tanh, 1)

                def unit(u, xm_next, last, g, q, route):
                    if not last:
                        act.wait_ge(s_xm, HU * (u + 1) + 1)
                        act.activation(xm_next[:, 0, 0, :, :], by_batch(0), ACT.Copy).then_inc(s_xma, 1)
                    for hp in range(HP):
                        act.wait_ge(s_max, HP * u + hp + 1)
                        if hp == 0 and not (isinstance(u, int) and u < 1):
                            act.wait_ge(s_pnd, u)
                        for b in range(NB):
                            i = hp * NB + b
                            e = act.activation(pr[:, hp, b * S:(b + 1) * S], sm[:, hp, b * S:(b + 1) * S],
                                               ACT.Exp, bias=nmax[:, i:i + 1], accum_out=rsum[:, i:i + 1])
                        e.then_inc(s_exp, 1)
                    if not last:
                        act.wait_ge(s_xm, HU * (u + 1) + 2)
                        act.activation(xm_next[:, 0, 1, :, :], by_batch(1), ACT.Copy).then_inc(s_xma, 1)
                    act.wait_ge(s_pt, HP * u + 1)
                    act.activation(pt[:, :, 0, :], sp_ps[:, 0, :].rearrange("p (j n) -> p j n", j=J), ACT.Copy).then_inc(s_pta, 1)
                    for bank in range(4):
                        act.wait_ge(s_pv, 4 * u + bank + 1)
                        act.activation(o_view(o_hi, bank), xo_ps[:, bank, :].rearrange("p (j h t) -> p h j t", j=2, h=HU), ACT.Copy).then_inc(s_oh, 1)
                    if q == 1 and route:
                        route_exp(act, g - 1)

                for h in range(2):
                    act.wait_ge(s_xm, h + 1)
                    act.activation(xm[0][:, 0, h, :, :], by_batch(h), ACT.Copy).then_inc(s_xma, 1)

                def group(g, route, last):
                    for q in range(Q):
                        unit(Q * g + q, xm[(q + 1) % 2], last and q == Q - 1, g, q, route)

                group(0, False, False)
                with nc.scalar.Fori(0, (G - 2) // 2) as k:
                    group(1 + 2 * k, True, False)
                    group(2 + 2 * k, True, False)
                group(G - 1, True, True)

            @block.vector
            def _(dve):
                chain = [0]

                def step(ins):
                    link(dve, s_dve, chain, ins)

                def normalise(g):
                    if not (isinstance(g, int) and g < 1):
                        dve.wait_ge(s_xt, KC * g)
                    for j in range(J):
                        t = bass.ds(g * J + j, 1)
                        n = dve.tensor_scalar(xn[:, j, :], x_res[:, t, :].rearrange("p a d -> p (a d)"),
                                              mean_var[:, t, 0:1].rearrange("p a b -> p (a b)"), rstd[:, t], ALU.subtract, ALU.mult)
                    n.then_inc(s_xnorm, 1)

                step(dve.memset(mx_part[:], 0.0))
                for g in range(G):
                    dve.wait_ge(s_x[g], 16)
                    for j in range(J):
                        last = dve.bn_stats(stats[:, g * J + j, :], x_res[:, g * J + j, :])
                    step(last)
                    for j in range(J):
                        last = dve.bn_aggr(mean_var[:, g * J + j, :], stats[:, g * J + j, :])
                    step(last)
                var, root, y, t = nwt[:, 1, :], nwt[:, 0, :], rstd[:], nwt[:, 2, :]
                dve.tensor_scalar(var, mean_var[:, :, 1], EPS, None, ALU.add).then_inc(s_var, 1)
                dve.wait_ge(s_act, 1)
                step(dve.reciprocal(y, root))
                step(dve.tensor_tensor(t, y, y, ALU.mult))
                step(dve.tensor_tensor(t, t, var, ALU.mult))
                step(dve.tensor_scalar(t, t, -0.5 * LN_SCALE, 1.5 * LN_SCALE, ALU.mult, ALU.add))
                dve.tensor_tensor(y, y, t, ALU.mult).then_inc(s_stat, 1)
                dve.wait_ge(s_stat, 1)
                normalise(0)
                dve.wait_ge(s_mcopied, H * KC // 4)
                dve.tensor_reduce(mx_part[:, 0:1], work[:, 0:4096], AX_X, ALU.max, apply_absolute_value=True)
                dve.wait_ge(s_ncopied, H // 2)
                dve.tensor_reduce(mx_part[:, 1:2], work[:, 4096:8192], AX_X, ALU.max, apply_absolute_value=True)
                dve.wait_ge(s_w[4], 16)
                dve.tensor_reduce(mx_part[:, 2:3], ctx_all, AX_X, ALU.max, apply_absolute_value=True).then_inc(s_mxp, 1)
                dve.wait_ge(s_maxt, 1)
                step(dve.tensor_reduce(mx_col[0:NM, :], banks[0:NM, 0, 0:P], AX_X, ALU.max))
                dve.wait_ge(s_ident, 3)
                dve.tensor_scalar(mx_diag[0:NM, :], ident[0:NM, 0:NM], mx_col[0:NM, 0:1], None, ALU.mult).then_inc(s_maxd, 1)
                dve.wait_ge(s_maxb, 1)
                step(dve.tensor_scalar(scale_of[:], banks[:, 1, 0:NM], 1e-30, 1e30, ALU.max, ALU.min))
                step(dve.tensor_scalar(mx_exp[:], scale_of[:].bitcast(I32), 0x7F800000, None, ALU.bitwise_and))
                dve.tensor_scalar(scale_of[:].bitcast(I32), mx_exp[:], -1.0, float((254 + TOP) << 23), ALU.mult, ALU.add).then_inc(s_scale, 1)
                step(dve.tensor_scalar(inv_of[:].bitcast(I32), mx_exp[:], -float(TOP << 23), None, ALU.add))
                dve.wait_ge(s_scale, 1)
                for i, (full, hi, lo) in enumerate(((work[:, 0:4096], m_hi[:].rearrange("p k h c -> p (k h c)"), m_lo[:].rearrange("p k h c -> p (k h c)")),
                                                    (work[:, 4096:8192], n_hi[:].rearrange("p h d -> p (h d)"), n_lo[:].rearrange("p h d -> p (h d)")))):
                    step(dve.tensor_scalar(hi, full, scale_of[:, i:i + 1], None, ALU.mult))
                    dve.scalar_tensor_tensor(out=lo, in0=full, scalar=scale_of[:, i:i + 1], in1=hi, op0=ALU.mult, op1=ALU.subtract).then_inc(s_wready, 1)
                dve.wait_ge(s_tanh, 1)
                dve.tensor_scalar(consts[:, 2:3], inv_of[:, 0:1], 1.0 / LN_SCALE / float(C) ** 0.5, None, ALU.mult).then_inc(s_wready, 1)
                step(dve.tensor_tensor(consts[:, 3:4], inv_of[:, 1:2], inv_of[:, 2:3], ALU.mult))
                step(dve.tensor_tensor(consts[:, 4:5], consts[:, 3:4], consts[:, 0:1], ALU.mult))
                dve.wait_ge(s_wready, 3)

                def xt_split(g, b):
                    dve.wait_ge(s_xt, KC * (g + 1))
                    dve.tensor_copy(xt_hi[b][:], sp_ps).then_inc(s_xth, 1)
                    dve.wait_ge(s_xth, g + 1)
                    dve.tensor_tensor(xt_lo[b][:], sp_ps, xt_hi[b][:], ALU.subtract).then_inc(s_xtl, 1)

                def context(b, g, turn):
                    dve.wait_ge(s_ctx[b], 48 * turn)
                    dve.tensor_scalar(ctx_s[b][:], ctx_s[b][:], scale_of[:, 2:3], None, ALU.mult).then_inc(s_cscale, 1)
                    dve.tensor_scalar(mask_b[b][:], mask_u[b][:], -1.0, -NEG, ALU.add, ALU.mult).then_inc(s_mbias, 1)
                    dve.tensor_reduce(any_of[b][:], mask_u[b][:].rearrange("p (b s) -> p b s", s=S), AX_X, ALU.max).then_inc(s_manyof, 1)

                def row_inverse(u, b, hp):
                    one = slice(hp * NB, (hp + 1) * NB)
                    dve.wait_ge(s_exp, HP * u + hp + 1)
                    if hp == 0 and not (isinstance(u, int) and u < 1):
                        dve.wait_ge(s_pnp, u)
                        dve.wait_ge(s_pnd, u)
                    dve.reciprocal(rinv[:, one], rsum[:, one]).then_inc(s_ri, 1)
                    dve.wait_ge(s_ri, 4 * u + 2 * hp + 1)
                    dve.tensor_tensor(rinv[:, one], rinv[:, one], any_of[b][:], ALU.mult).then_inc(s_ri, 1)

                def unit(u, g, b, q, xm_next, last, route, experts, more):
                    r = g - 1
                    for hp in range(HP):
                        dve.wait_ge(s_sc, HP * u + hp + 1)
                        if hp == 0 and not (isinstance(u, int) and u < 1):
                            dve.wait_ge(s_exp, HP * u)
                        dve.scalar_tensor_tensor(out=sm[:, hp, :], in0=sp_ps[:, hp, :], scalar=consts[:, 2:3], in1=mask_b[b][:],
                                                 op0=ALU.mult, op1=ALU.add).then_inc(s_msk, 1)
                        dve.wait_ge(s_msk, HP * u + hp + 1)
                        dve.tensor_reduce(nmax[:, hp * NB:(hp + 1) * NB], sm[:, hp, :].rearrange("p (b s) -> p b s", s=S),
                                          AX_X, ALU.max, negate=True).then_inc(s_max, 1)
                    if q == 0 and experts:
                        expert_max(dve, r)
                    if q == 1 and route:
                        route_rows_first(dve, r)
                    if q == 2 and more:
                        xt_split(g + 1, 1 - b)
                    if q == 2 and route:
                        route_weights(dve, r)
                    if q == 3 and route:
                        route_choice(dve, r, 1)
                    if not last:
                        dve.wait_ge(s_xm, HU * (u + 1) + 3)
                        dve.tensor_copy(xm_next[:, 1, 0, :, :], by_batch(2)).then_inc(s_xmd, 1)
                    row_inverse(u, b, 0)
                    if q == 1 and route:
                        route_rows_second(dve, r)
                        route_copy(dve, r)
                    if not last:
                        dve.wait_ge(s_xm, HU * (u + 1) + 4)
                        dve.tensor_copy(xm_next[:, 1, 1, :, :], by_batch(3)).then_inc(s_xmd, 1)
                    row_inverse(u, b, 1)
                    dve.wait_ge(s_ri, 4 * u + 4)
                    dve.tensor_tensor(pn[:, 1, :].rearrange("p (b s) -> p b s", s=S), pr[:, 1, :].rearrange("p (b s) -> p b s", s=S),
                                      rinv[:, NB:2 * NB].unsqueeze(2).to_broadcast([P, NB, S]), ALU.mult).then_inc(s_pnd, 1)
                    if q == 1 and experts:
                        expert_scale(dve, r)
                    if q == 1 and route:
                        route_shift(dve, r)
                    if q == 3 and route:
                        route_places(dve, r)
                    dve.wait_ge(s_pt, HP * (u + 1))
                    dve.tensor_copy(pt[:, :, 1, :], sp_ps[:, 1, :].rearrange("p (j n) -> p j n", j=J)).then_inc(s_ptd, 1)
                    for bank in range(4):
                        dve.wait_ge(s_oh, 4 * u + bank + 1)
                        dve.tensor_tensor(o_view(o_lo, bank), xo_ps[:, bank, :].rearrange("p (j h t) -> p h j t", j=2, h=HU),
                                          o_view(o_hi, bank), ALU.subtract).then_inc(s_ol, 1)

                def residual(g):
                    dve.wait_ge(s_on, Q * (g + 1))
                    t = bass.ds(g * J, J)
                    if isinstance(g, int):
                        t = slice(g * J, g * J + J)
                    dve.scalar_tensor_tensor(out=x_res[:, t, :], in0=acc, scalar=consts[:, 4:5], in1=x_res[:, t, :],
                                             op0=ALU.mult, op1=ALU.add).then_inc(s_x1, 1)

                context(0, 0, 1)
                xt_split(0, 0)
                for h in (2, 3):
                    dve.wait_ge(s_xm, h + 1)
                    dve.tensor_copy(xm[0][:, 1, h - 2, :, :], by_batch(h)).then_inc(s_xmd, 1)

                def group(g, b, turn_next, first, last, experts):
                    for q in range(Q):
                        if q == 0:
                            dve.wait_ge(s_mbias, g + 1)
                            dve.wait_ge(s_manyof, g + 1)
                        unit(Q * g + q, g, b, q, xm[(q + 1) % 2], last and q == Q - 1, not first, experts, not last)
                        if q == 0 and not first:
                            residual(g - 1)
                            route_stats(dve, g - 1)
                        if q == 2 and not first:
                            route_choice(dve, g - 1, 0)
                        if q == 1 and not last:
                            normalise(g + 1)
                            context(1 - b, g + 1, turn_next)

                group(0, 0, 1, True, False, False)
                with nc.vector.Fori(0, (G - 2) // 2) as k:
                    group(1 + 2 * k, 1, k + 2, False, False, True)
                    group(2 + 2 * k, 0, k + 2, False, False, True)
                group(G - 1, 1, 0, False, True, False)
                residual(G - 1)
                route_stats(dve, G - 1)

            @block.tensor
            def _(pe):
                pe.wait_ge(s_w[0], 16)
                pe.wait_ge(s_w[1], 16)
                for i in range(H * KC // 4):
                    kc, hq = i % KC, i // KC
                    if i >= 8:
                        pe.wait_ge(s_mcopied, i - 7)
                    for h in range(4 * hq, 4 * hq + 4):
                        mm = pe.matmul(banks[:, i % 8, (h % 4) * C:(h % 4 + 1) * C], wq_s[:, h, kc * P:(kc + 1) * P], wk_s[:, h // (H // KV), :],
                                       start=True, stop=True)
                    mm.then_inc(s_mprod, 1)
                pe.wait_ge(s_w[2], 16)
                pe.wait_ge(s_w[3], 16)
                for i in range(H // 2):
                    pe.wait_ge(s_mcopied, H * KC // 4 - 8 + i + 1)
                    for h in (2 * i, 2 * i + 1):
                        mm = pe.matmul(banks[:, i % 8, (h % 2) * D:(h % 2 + 1) * D], wv_s[:, h // (H // KV), :], wo_s[:, h, :], start=True, stop=True)
                    mm.then_inc(s_nprod, 1)
                pe.wait_ge(s_ident, 3)
                pe.wait_ge(s_ncopied, H // 2)
                pe.wait_ge(s_mxp, 1)
                pe.transpose(banks[0:NM, 0, 0:P], mx_part[:], ident[:]).then_inc(s_maxt, 1)
                pe.wait_ge(s_maxd, 1)
                pe.matmul(banks[:, 1, 0:NM], ones[0:NM, :], mx_diag[0:NM, :], start=True, stop=True).then_inc(s_maxb, 1)

                def transposes(g):
                    pe.wait_ge(s_xnorm, g + 1)
                    for kc in range(KC):
                        for j in range(J):
                            mm = pe.transpose(sp_ps[:, kc, j * P:(j + 1) * P], xn[:, j, kc * P:(kc + 1) * P], ident[:])
                        mm.then_inc(s_xt, 1)

                def x_m(u, q, b, heads=range(HU)):
                    for hh in heads:
                        if not (isinstance(u, int) and u < 2):
                            pe.wait_ge(s_ol, 4 * (u - 2) + hh + 1)
                        h = HU * q + hh
                        n = 0
                        for kc in range(KC):
                            for w, r in ((m_hi, xt_hi[b]), (m_hi, xt_lo[b]), (m_lo, xt_hi[b])):
                                mm = pe.matmul(xo_ps[:, hh, :], w[:, kc, h, :], r[:, kc, :], start=(n == 0), stop=(n == 3 * KC - 1))
                                n += 1
                        mm.then_inc(s_xm, 1)

                def scores(u, xm_u, b):
                    pe.wait_ge(s_xma, 2 * (u + 1))
                    pe.wait_ge(s_xmd, 2 * (u + 1))
                    if not (isinstance(u, int) and u < 1):
                        pe.wait_ge(s_pta, u)
                        pe.wait_ge(s_ptd, u)
                    for hp in range(HP):
                        for bt in range(NB):
                            mm = pe.matmul(sp_ps[:, hp, bt * S:(bt + 1) * S], xm_u[:, hp, :, bt, :].rearrange("p c t -> p (c t)"),
                                           ctx_t_s[b][:, bt * S:(bt + 1) * S], start=True, stop=True)
                        mm.then_inc(s_sc, 1)

                def project(u, q, js):
                    pe.wait_ge(s_oh, 4 * (u + 1))
                    pe.wait_ge(s_ol, 4 * (u + 1))
                    for j in js:
                        for hh in range(HU):
                            h = HU * q + hh
                            for n, (o, w) in enumerate(((o_hi, n_hi), (o_lo, n_hi), (o_hi, n_lo))):
                                mm = pe.matmul(acc[:, j, :], o[:, hh, j * P:(j + 1) * P], w[:, h, :],
                                               start=(h == 0 and n == 0 and j % 2 == 0), stop=(h == H - 1 and n == 2), skip_group_check=True)
                    if J - 1 in js:
                        mm.then_inc(s_on, 1)

                def probs_t(u):
                    for hp in range(HP):
                        pe.wait_ge(s_pnd if hp else s_pnp, u + 1)
                        for j in range(J):
                            mm = pe.transpose(sp_ps[:, hp, j * P:(j + 1) * P], pn[:, hp, j * P:(j + 1) * P], ident[:])
                        mm.then_inc(s_pt, 1)

                def head_outputs(u, b):
                    pe.wait_ge(s_pta, u + 1)
                    pe.wait_ge(s_ptd, u + 1)
                    for half in range(2):
                        for jj in range(2):
                            j = 2 * half + jj
                            for b2 in range(2):
                                rows = slice(b2 * S, (b2 + 1) * S)
                                mm = pe.matmul(xo_ps[:, 2 * half + b2, jj * 256:(jj + 1) * 256], ctx_s[b][rows, j, :], pt[rows, j, :, :],
                                               start=True, stop=True)
                                if jj == 1:
                                    mm.then_inc(s_pv, 1)

                def group(g, b, first, last):
                    r = g - 1
                    for q in range(Q):
                        u = Q * g + q
                        more = not (last and q == Q - 1)
                        if q == 0:
                            pe.wait_ge(s_cscale, g + 1)
                        if q == Q - 1 and more:
                            pe.wait_ge(s_xtl, g + 2)
                        scores(u, xm[q % 2], b)
                        b_next = b if q < Q - 1 else 1 - b
                        if more:
                            x_m(u + 1, (q + 1) % Q, b_next, (0, 1))
                        if q == 2 and not last:
                            pe.wait_ge(s_msk, HP * (u + 1))
                            transposes(g + 1)
                        if more:
                            x_m(u + 1, (q + 1) % Q, b_next, (2, 3))
                        if q == 1 and not first:
                            pe.wait_ge(s_msk, HP * (u + 1))
                            route_transposes(pe, r)
                            pe.wait_ge(s_x1, g)
                        before = not (first and q == 0)
                        if before:
                            project(u - 1, (q - 1) % Q, (0, 1, 2))
                        if more:
                            pe.wait_ge(s_xmd, 2 * (u + 2))
                        if q == 1 and not first:
                            route_logits(pe, r)
                        if q == 2 and not last:
                            pe.wait_ge(s_xtl, g + 2)
                        if q == 3 and not first:
                            route_positions(pe, r)
                        probs_t(u)
                        if before:
                            project(u - 1, (q - 1) % Q, (3,))
                        if more:
                            pe.wait_ge(s_xma, 2 * (u + 2))
                        if q == 1 and not first:
                            pe.wait_ge(s_l1, g)
                        if q == 3 and not first:
                            pe.wait_ge(s_posr, g)
                        head_outputs(u, b)

                pe.wait_ge(s_scale, 1)
                transposes(0)
                pe.wait_ge(s_wready, 2)
                pe.wait_ge(s_xtl, 1)
                pe.wait_ge(s_iota, IOTAS)
                pe.wait_ge(s_small, 48)
                x_m(0, 0, 0)
                group(0, 0, True, False)
                with nc.tensor.Fori(0, (G - 2) // 2) as k:
                    group(1 + 2 * k, 1, False, False)
                    group(2 + 2 * k, 0, False, False)
                group(G - 1, 1, False, True)
                project(Q * G - 1, Q - 1, range(J))

        with nc.Block() as block:

            @block.sync
            def _(sp):
                sp.wait_ge(s_pad, 2)
                for i in range(E - EARLY):
                    load_expert(sp, EARLY + i, late32[:, i, :], s_fwl)

            @block.gpsimd
            def _(pool):
                r = G - 1
                pool.memset(late32[:, :, NGU + 2 * D:EW], 0.0).then_inc(s_pad, 1)
                route_newton(pool, r)
                pool.wait_ge(s_flate, 1)
                pool.partition_all_reduce(fm_late[:, 4:8], fm_late[:, 0:4], P, bass.bass_isa.ReduceOp.max).then_inc(s_fam, 1)
                route_scatter(pool, r)
                pool.wait_ge(s_tail, 1)
                for e in range(E + 1):
                    pool.indirect_dma_start(rows_dram, bass.IndirectOffsetOnAxis(ap=tail_i[:, e:e + 1], axis=0),
                                            zero_row, None).then_inc(s_scat, 16)
                pool.wait_ge(s_scat, 16 * (2 * TILES + E + 1))

            @block.scalar
            def _(act):
                route_exp(act, G - 1)

            @block.tensor
            def _(pe):
                route_transposes(pe, G - 1)
                route_logits(pe, G - 1)
                route_positions(pe, G - 1)

            @block.vector
            def _(dve):
                r = G - 1
                route_rows_first(dve, r)
                route_rows_second(dve, r)
                route_copy(dve, r)
                route_shift(dve, r)
                route_weights(dve, r)
                route_choice(dve, r, 0)
                route_choice(dve, r, 1)
                dve.wait_ge(s_fwl, 48 * (E - EARLY))
                for i in range(E - EARLY):
                    dve.tensor_reduce(fm_late[:, 2 * i:2 * i + 1], late32[:, i, 0:NGU], AX_X, ALU.max, apply_absolute_value=True)
                    m = dve.tensor_reduce(fm_late[:, 2 * i + 1:2 * i + 2], late32[:, i, NGU:EW], AX_X, ALU.max, apply_absolute_value=True)
                m.then_inc(s_flate, 1)
                route_places(dve, r)
                dve.wait_ge(s_fam, EARLY + 1)
                late = 1

                def late_step(make):
                    nonlocal late
                    late += 1
                    make(dve).then_inc(s_flate, 1)
                    dve.wait_ge(s_flate, late)

                n = 0

                def step(ins):
                    nonlocal n
                    n += 1
                    ins.then_inc(s_tab, 1)
                    dve.wait_ge(s_tab, n)

                dve.tensor_copy(tail_f[:, 0:E], count[:])
                step(dve.memset(tail_f[:, E:E + 1], float(E * REGION)))
                step(dve.tensor_tensor(tail_f[:], tail_f[:], rank_p[:], ALU.add))
                dve.tensor_copy(tail_i[:], tail_f[:]).then_inc(s_tail, 1)
                powers_of_two(late_step, f_scale[:, EARLY:E, :].rearrange("p e n -> p (e n)"), f_inv[:, EARLY:E, :].rearrange("p e n -> p (e n)"),
                              f_exp[:], fm_late[:, 4:8])
                for i in range(E - EARLY):
                    for first, words, which in pieces:
                        full = late32[:, i, first:first + words]
                        hi, lo = (ew16[:, EARLY + i, 2 * first + w * words:2 * first + (w + 1) * words] for w in (0, 1))
                        late_step(lambda v: v.tensor_scalar(hi, full, f_scale[:, EARLY + i, which:which + 1], None, ALU.mult))
                        dve.scalar_tensor_tensor(out=lo, in0=full, scalar=f_scale[:, EARLY + i, which:which + 1], in1=hi, op0=ALU.mult, op1=ALU.subtract)
                step(dve.tensor_tensor(t_end[:], count[:], region0[:], ALU.subtract))
                step(dve.tensor_scalar(n_tiles_i[:], t_end[:], float(P - 1), None, ALU.add))
                step(dve.tensor_scalar(n_tiles_i[:], n_tiles_i[:], P.bit_length() - 1, None, ALU.logical_shift_right))
                step(dve.tensor_copy(n_tiles[:], n_tiles_i[:]))
                step(dve.tensor_copy(t_end[:], n_tiles[:]))
                for e in range(1, E):
                    step(dve.tensor_tensor(t_end[:, e:e + 1], t_end[:, e:e + 1], t_end[:, e - 1:e], ALU.add))
                step(dve.tensor_tensor(past, tile_iota[:].unsqueeze(2).to_broadcast([P, TF, E]), t_end[:].unsqueeze(1).to_broadcast([P, TF, E]), ALU.is_ge))
                step(dve.tensor_reduce(t_e, past, AX_X, ALU.add))
                step(dve.tensor_tensor(pick, past, n_tiles[:].unsqueeze(1).to_broadcast([P, TF, E]), ALU.mult))
                step(dve.tensor_reduce(t_s, pick, AX_X, ALU.add))
                step(dve.tensor_tensor(t_s, tile_iota[:], t_s, ALU.subtract))
                step(dve.tensor_scalar(t_row, t_e, float(E), float(P), ALU.is_lt, ALU.mult))
                step(dve.tensor_tensor(t_s, t_s, t_row, ALU.mult))
                step(dve.scalar_tensor_tensor(out=t_row[:], in0=t_e[:], scalar=float(REGION), in1=t_s[:], op0=ALU.mult, op1=ALU.add))
                dve.tensor_copy(t_row_i[:], t_row)
                step(dve.tensor_scalar(t_c, t_e, float(E - 1), None, ALU.min))
                step(dve.tensor_copy(t_e_i[:], t_c))
                dve.tensor_scalar(tile_scales[:, 0, :], f_inv[:, :, 0], 1.0 / LN_SCALE, None, ALU.mult)
                dve.tensor_scalar(tile_scales[:, 1, :], f_scale[:, :, 0], 2.0 ** -31 / LN_SCALE, None, ALU.mult)
                step(dve.tensor_tensor(tile_scales[:, 2, :], f_inv[:, :, 0], f_inv[:, :, 0], ALU.mult))
                step(dve.tensor_tensor(tile_scales[:, 2, :], tile_scales[:, 2, :], f_inv[:, :, 1], ALU.mult))
                step(dve.tensor_scalar(tile_scales[:, 2, :], tile_scales[:, 2, :], 2.0 ** 31, consts[:, 1:2], ALU.mult, ALU.mult))
                step(dve.tensor_scalar(past[:, 0, :], rev[:], -1.0, float(E), ALU.mult, ALU.add))
                step(dve.tensor_tensor(pick, t_c.unsqueeze(2).to_broadcast([P, TF, E]), past[:, 0:1, :].to_broadcast([P, TF, E]), ALU.is_equal))
                for i in range(3):
                    step(dve.tensor_tensor(past, pick, tile_scales[:, i:i + 1, :].to_broadcast([P, TF, E]), ALU.mult))
                    step(dve.tensor_reduce(t_sc[i][:], past, AX_X, ALU.add))

        at2 = (E - EARLY) * EW
        after = big[:, EARLY * EW:]

        def take2(words):
            nonlocal at2
            at2 += words
            assert at2 <= PH1 + AUX
            return after[:, at2 - words:at2]

        def halves(words, chunks):
            return take2(words // 2).bitcast(F16).rearrange("p (c n) -> p c n", c=chunks)

        xg = [take2(ROW) for _ in range(U)]
        xg_hi, xg_lo = ([halves(KC * P, KC) for _ in range(2)] for _ in range(2))
        silu_s = take2(F)
        inter = take2(NF * P)
        it_hi, it_lo = ([halves(NF * P, NF) for _ in range(2)] for _ in range(2))
        ys = [take2(D) for _ in range(U)]
        fin = [aux[:, i * 2 * J * D:(i + 1) * 2 * J * D].rearrange("p (c j d) -> p c j d", c=2, j=J) for i in range(2)]

        s_xg = [sem(f"tile_rows_loaded{i}") for i in range(U)]
        s_yo = [sem(f"tile_output_stored{i}") for i in range(U)]
        s_zin = sem("inter_padding_zero")
        s_gt = sem("tile_transposed")
        s_gth = sem("tile_high_ready")
        s_gtl = sem("tile_low_ready")
        s_gate = sem("gate_done")
        s_up = sem("up_done")
        s_si = sem("silu_ready")
        s_in = sem("inter_ready")
        s_it = sem("inter_transposed")
        s_ith = sem("inter_high_ready")
        s_itl = sem("inter_low_ready")
        s_dn = sem("down_done")
        s_ys = sem("tile_output_ready")
        s_fin = [sem(f"expert_outputs_loaded{i}") for i in range(2)]
        s_add = sem("expert_outputs_added")
        s_sum = sem("group_summed")
        s_out = sem("out_stored")
        x_ps, g_ps, u_ps, i_ps, y_ps = (banks[:, i, :] for i in range(5))

        with nc.Block() as block:

            @block.sync
            def _(sp):
                def load(t, i, turn):
                    r = sp.value_load(t_row_i[0:1, bass.ds(t, 1)], min_val=0, max_val=E * REGION)
                    if turn is not None:
                        sp.wait_ge(s_yo[i], 16 * turn)
                    sp.dma_start(xg[i], rows_dram[bass.ds(r, P), :]).then_inc(s_xg[i], 16)

                for i in range(U):
                    load(i, i, None)
                with nc.sync.Fori(1, TF // U) as k:
                    for i in range(U):
                        load(k * U + i, i, k)

            @block.gpsimd
            def _(pool):
                def store(t, i):
                    pool.wait_ge(s_ys, t + 1)
                    pool.sem_inc(s_passed)
                    pool.indirect_dma_start(y_dram, bass.IndirectOffsetOnAxis(ap=xg[i][:, D + 1:D + 2].bitcast(I32), axis=0),
                                            ys[i], None, bounds_check=2 * B * T - 1, oob_is_err=False).then_inc(s_yo[i], 16)

                for i in range(U):
                    store(i, i)
                with nc.gpsimd.Fori(1, TF // U) as k:
                    for i in range(U):
                        store(k * U + i, i)
                for i in range(U):
                    pool.wait_ge(s_yo[i], 16 * (TF // U))

            @block.scalar
            def _(act):
                def high(t, i):
                    act.wait_ge(s_gt, t + 1)
                    act.activation(xg_hi[i % 2], x_ps[:, 0:KC * P].rearrange("p (k n) -> p k n", k=KC), ACT.Copy).then_inc(s_gth, 1)

                def inner_high(t, i):
                    act.wait_ge(s_it, t + 1)
                    act.activation(it_hi[i % 2], i_ps[:, 0:NF * P].rearrange("p (c n) -> p c n", c=NF), ACT.Copy).then_inc(s_ith, 1)

                def tile(t, i, first, last):
                    if not first:
                        act.wait_ge(s_in, t)
                    act.wait_ge(s_gate, t + 1)
                    act.activation(silu_s, g_ps[:, 0:F], ACT.Silu, scale=t_sc[0][:, bass.ds(t, 1)]).then_inc(s_si, 1)
                    if not first:
                        inner_high(t - 1, i - 1)
                    if not last:
                        high(t + 1, i + 1)

                high(0, 0)
                for i in range(U):
                    tile(i, i, i == 0, False)
                with nc.scalar.Fori(1, TF // U - 1) as k:
                    for i in range(U):
                        tile(k * U + i, i, False, False)
                for i in range(U):
                    tile(TF - U + i, i, False, i == U - 1)
                inner_high(TF - 1, U - 1)

            @block.vector
            def _(dve):
                dve.memset(inter, 0.0).then_inc(s_zin, 1)
                dve.wait_ge(s_zin, 1)

                def low(t, i):
                    dve.wait_ge(s_gth, t + 1)
                    dve.tensor_tensor(xg_lo[i % 2], x_ps[:, 0:KC * P].rearrange("p (k n) -> p k n", k=KC), xg_hi[i % 2], ALU.subtract).then_inc(s_gtl, 1)

                def inner_low(t, i):
                    dve.wait_ge(s_ith, t + 1)
                    dve.tensor_tensor(it_lo[i % 2], i_ps[:, 0:NF * P].rearrange("p (c n) -> p c n", c=NF), it_hi[i % 2], ALU.subtract).then_inc(s_itl, 1)

                def output(t, i):
                    dve.wait_ge(s_dn, t + 1)
                    dve.tensor_scalar(ys[i % U], y_ps[:, 0:D], xg[i % U][:, D:D + 1], t_sc[2][:, bass.ds(t, 1)], ALU.mult, ALU.mult).then_inc(s_ys, 1)

                def tile(t, i, n, last):
                    if n > 0:
                        inner_low(t - 1, i - 1)
                    if not last:
                        low(t + 1, i + 1)
                    dve.wait_ge(s_si, t + 1)
                    dve.wait_ge(s_up, t + 1)
                    dve.scalar_tensor_tensor(out=inter[:, 0:F], in0=u_ps[:, 0:F], scalar=t_sc[1][:, bass.ds(t, 1)], in1=silu_s,
                                             op0=ALU.mult, op1=ALU.mult).then_inc(s_in, 1)
                    if n > 1:
                        output(t - 2, i - 2)

                low(0, 0)
                for i in range(U):
                    tile(i, i, i, False)
                with nc.vector.Fori(1, TF // U - 1) as k:
                    for i in range(U):
                        tile(k * U + i, i, 2, False)
                for i in range(U):
                    tile(TF - U + i, i, 2, i == U - 1)
                inner_low(TF - 1, U - 1)
                output(TF - 2, U - 2)
                output(TF - 1, U - 1)

            @block.tensor
            def _(pe):
                def rows_t(t, i, turn):
                    pe.wait_ge(s_xg[i], 16 * turn)
                    for kc in range(KC):
                        mm = pe.transpose(x_ps[:, kc * P:(kc + 1) * P], xg[i][:, kc * P:(kc + 1) * P], ident[:])
                    mm.then_inc(s_gt, 1)

                def product(ps, half, e, i):
                    n = 0
                    for kc in range(KC):
                        for xh, w in ((xg_hi, 0), (xg_lo, 0), (xg_hi, 1)):
                            mm = pe.matmul(ps[:, 0:F], xh[i % 2][:, kc, :], w_gu[:, e, kc, w, half * F:(half + 1) * F].rearrange("p a f -> p (a f)"),
                                           start=(n == 0), stop=(n == 3 * KC - 1))
                            n += 1
                    return mm

                def inner_t(t):
                    pe.wait_ge(s_in, t + 1)
                    for c in range(NF):
                        mm = pe.transpose(i_ps[:, c * P:(c + 1) * P], inter[:, c * P:(c + 1) * P], ident[:])
                    mm.then_inc(s_it, 1)

                def down(t, i, e, first):
                    pe.wait_ge(s_itl, t + 1)
                    if not first:
                        pe.wait_ge(s_ys, t)
                    n = 0
                    for c in range(NF):
                        for ih, w in ((it_hi, 0), (it_lo, 0), (it_hi, 1)):
                            mm = pe.matmul(y_ps[:, 0:D], ih[i % 2][:, c, :], w_dn[:, e, w, c, :].rearrange("p a d -> p (a d)"),
                                           start=(n == 0), stop=(n == 3 * NF - 1))
                            n += 1
                    mm.then_inc(s_dn, 1)

                def expert_of(t):
                    return bass.ds(pe.value_load(t_e_i[0:1, bass.ds(t, 1)], min_val=0, max_val=E - 1), 1)

                def tiles(t0, turn, first, last):
                    e = {}
                    if not first:
                        e[-2], e[-1] = expert_of(t0 - 2), expert_of(t0 - 1)
                    e[0] = expert_of(t0)
                    for i in range(U):
                        t = t0 + i
                        pe.wait_ge(s_gtl, t + 1)
                        product(g_ps, 0, e[i], i).then_inc(s_gate, 1)
                        if not (first and i == 0):
                            inner_t(t - 1)
                        if not (last and i == U - 1):
                            rows_t(t + 1, (i + 1) % U, turn + (i + 1) // U)
                        product(u_ps, 1, e[i], i).then_inc(s_up, 1)
                        if i < U - 1:
                            e[i + 1] = expert_of(t + 1)
                        if not (first and i < 2):
                            down(t - 2, i, e[i - 2], first and i == 2)
                    if last:
                        inner_t(TF - 1)
                        down(TF - 2, U - 2, e[U - 2], False)
                        down(TF - 1, U - 1, e[U - 1], False)

                rows_t(0, 0, 1)
                tiles(0, 1, True, False)
                with nc.tensor.Fori(1, TF // U - 1) as k:
                    tiles(k * U, k + 1, False, False)
                tiles(TF - U, TF // U, False, True)

        with nc.Block() as block:

            @block.sync
            def _(sp):
                for g in range(G):
                    if g >= 2:
                        sp.wait_ge(s_sum, g - 1)
                    for c in range(2):
                        sp.dma_start(fin[g % 2][:, c], y_tiles[g, :, c]).then_inc(s_fin[g % 2], 16)

            @block.vector
            def _(dve):
                for g in range(G):
                    dve.wait_ge(s_fin[g % 2], 32 * (g // 2 + 1))
                    t = slice(g * J, (g + 1) * J)
                    dve.tensor_tensor(fin[g % 2][:, 0], fin[g % 2][:, 0], fin[g % 2][:, 1], ALU.add).then_inc(s_add, 1)
                    dve.wait_ge(s_add, g + 1)
                    dve.tensor_tensor(x_res[:, t, :], x_res[:, t, :], fin[g % 2][:, 0], ALU.add).then_inc(s_sum, 1)

            @block.scalar
            def _(act):
                for g in range(G):
                    act.wait_ge(s_sum, g + 1)
                    act.dma_start(out_tiles[g], x_res[:, g * J:(g + 1) * J, :]).then_inc(s_out, 16)
                act.wait_ge(s_out, 16 * G)


def kernel(**inputs):
    import numpy as _np
    import concourse.bacc as _bacc
    from concourse import mybir as _mybir
    from concourse.bass_utils import run_bass_kernel_spmd as _run

    a = {k: _np.asarray(v) for k, v in inputs.items()}
    vision = a["ctx_1024"]
    arrays = {
        "x": a["x"],
        "ctx": vision,
        "ctx_t": vision.reshape(-1, vision.shape[-1]).T,
        "mask": a["mask_BxS2_bf1"].view(_np.uint8),
        "g_xattn": a["g_xattn"],
        "g_ffn": a["g_ffn"],
        "wq_t": a["L0_xattn_Wq"].T,
        "wk_t": a["L0_xattn_Wk"].T,
        "wv_t": a["L0_xattn_Wv"].T,
        "wo": a["L0_xattn_Wo"],
        "gate_w_t": a["L0_ffn_gate_w"].T,
        "gate_b": a["L0_ffn_gate_b"],
        "expert_bias": a["L0_ffn_expert_bias"],
        "w_gu_t": a["L0_ffn_w_gate_up"].transpose(0, 2, 1),
        "w_down_t": a["L0_ffn_w_down"].transpose(0, 2, 1),
    }
    arrays = {f"in_{k}": _np.ascontiguousarray(v) for k, v in arrays.items()}
    nc = _bacc.Bacc("TRN2", target_bir_lowering=False, num_devices=1)
    args = [nc.dram_tensor(k, v.shape, _mybir.dt.from_np(v.dtype), kind="ExternalInput").ap() for k, v in arrays.items()]
    args.append(nc.dram_tensor("out_0", a["x"].shape, _mybir.dt.float32, kind="ExternalOutput").ap())
    bass_flamingo_gated_block(nc, *args)
    return _run(nc, [arrays], core_ids=[0]).results[0]["out_0"]
```

```python
from contextlib import ExitStack

import concourse.bass as bass
from concourse import mybir

F32 = mybir.dt.float32
F16 = mybir.dt.float16
I32 = mybir.dt.int32
U8 = mybir.dt.uint8
ALU = mybir.AluOpType
ACT = mybir.ActivationFunctionType
AX_X = mybir.AxisListType.X

P = 128


def bass_flamingo_gated_block(
    nc: bass.Bass,
    x: bass.AP,
    ctx: bass.AP,
    ctx_t: bass.AP,
    mask: bass.AP,
    g_xattn: bass.AP,
    g_ffn: bass.AP,
    wq_t: bass.AP,
    wk_t: bass.AP,
    wv_t: bass.AP,
    wo: bass.AP,
    gate_w_t: bass.AP,
    gate_b: bass.AP,
    expert_bias: bass.AP,
    w_gu_t: bass.AP,
    w_down_t: bass.AP,
    out: bass.AP,
):
    B, T, D = x.shape
    S, C = ctx.shape[1:]
    H = wq_t.shape[0] // P
    KV = wk_t.shape[0] // P
    E, _, GU = w_gu_t.shape
    F = GU // 2
    KC = D // P
    TILES = B * T // P
    J = 4
    G = TILES // J
    NB = J * P // T
    GT = J * P
    Q = 4
    HU = H // Q
    HP = HU // 2
    NF = -(-F // P)
    EPS = 1e-5
    LN_SCALE = 1024.0
    TOP = 14
    XM_SCALE = 2.0 ** -19
    NEG = -1.0e30
    assert T == S == 64 and C == P and D == 256 and KC == 2

    x_tiles = x.rearrange("b t d -> (b t) d").rearrange("(g j p) d -> g p j d", j=J, p=P)
    out_tiles = out.rearrange("b t d -> (b t) d").rearrange("(g j p) d -> g p j d", j=J, p=P)
    ctx_tiles = ctx.rearrange("b s c -> (b s) c").rearrange("(g j p) c -> g p j c", j=J, p=P)
    ctx_t_groups = ctx_t.rearrange("c (g n) -> g c n", g=G)
    mask_groups = mask.rearrange("b s -> (b s)").rearrange("(g a n) -> g a n", g=G, a=1)

    es = ExitStack()
    with es:
        def sb(name, shape, dt=F32):
            return es.enter_context(nc.sbuf_tensor(name, shape, dt))

        def sem(name):
            return es.enter_context(nc.semaphore(name))

        x_res = sb("x_res", [P, TILES, D])
        MNW = H * D // 2
        mn = sb("mn", [P, 4 * MNW])
        m_hi, m_lo = (mn[:, i * MNW:(i + 1) * MNW].bitcast(F16).rearrange("p (k h c) -> p k h c", k=KC, h=H) for i in (0, 1))
        n_hi, n_lo = (mn[:, i * MNW:(i + 1) * MNW].bitcast(F16).rearrange("p (h d) -> p h d", h=H) for i in (2, 3))
        ident = sb("ident", [P, P])
        ones = sb("ones", [32, P])
        xn = sb("xn", [P, J, D])
        mean_var = sb("mean_var", [P, TILES, 2])
        stats = sb("stats", [P, TILES, 6])
        rstd = sb("rstd", [P, TILES])
        nwt = sb("nwt", [P, 2, TILES])
        NM = 4
        mx_chunk = sb("mx_chunk", [P, 3, 8])
        mx_part = sb("mx_part", [P, NM])
        mx_col = sb("mx_col", [32, 1])
        mx_diag = sb("mx_diag", [32, NM])
        mx_exp = sb("mx_exp", [P, NM], I32)
        scale_of = sb("scale_of", [P, NM])
        inv_of = sb("inv_of", [P, NM])
        gates = sb("gates", [P, 2])
        consts = sb("consts", [P, 8])
        EW = KC * GU + NF * D
        EARLY = E - 2
        PH1 = 8 * 1024
        AUX = 2 * EW
        big = sb("big", [P, EARLY * EW + PH1 + AUX])
        stage = big[:, 0:EARLY * EW]
        work = big[:, EARLY * EW:EARLY * EW + PH1]
        aux = big[:, EARLY * EW + PH1:]

        banks = es.enter_context(nc.psum_tensor("banks", [P, 8, 512], F32))
        acc = banks[:, 0:2, :].rearrange("p b n -> p (b n)").rearrange("p (j d) -> p j d", j=J)
        sp_ps = banks[:, 2:4, :]
        tr_ps = banks[:, 4:6, :]
        xo_ps = banks[:, 4:8, :]

        wq_s = stage[:, 0:H * D].rearrange("p (h d) -> p h d", h=H)
        wo_s = stage[:, H * D:2 * H * D].rearrange("p (h d) -> p h d", h=H)
        wk_s, wv_s = (stage[:, 2 * H * D + i * KV * C:2 * H * D + (i + 1) * KV * C].rearrange("p (h c) -> p h c", h=KV) for i in range(2))
        ctx_all = work[:, 0:TILES * C]
        mf = aux[:, 0:2 * MNW].rearrange("p (k h c) -> p k h c", k=KC, h=H)
        nf = stage[:, 0:2 * MNW].rearrange("p (h d) -> p h d", h=H)
        at = 0

        def take(words):
            nonlocal at
            at += words
            assert at <= PH1
            return work[:, at - words:at]

        xm = [tuple(take(HU * GT // 2).bitcast(F16).rearrange("p (a b c t) -> p a c b t", a=HP, b=NB, c=2) for _ in range(2)) for _ in range(2)]
        sm = take(HP * GT).rearrange("p (a n) -> p a n", a=HP)
        pr = pn = sm
        pt = take(HP * GT).rearrange("p (j a n) -> p j a n", j=J, a=HP)
        o_hi = take(HU * GT // 2).bitcast(F16).rearrange("p (h n) -> p h n", h=HU)
        o_lo = take(HU * GT // 2).bitcast(F16).rearrange("p (h n) -> p h n", h=HU)
        ctx_t_s = sb("ctx_t_s", [P, GT])
        ctx_t_hi = [sb(f"ctx_t_hi{i}", [P, GT], F16) for i in range(2)]
        ctx_t_lo = [sb(f"ctx_t_lo{i}", [P, GT], F16) for i in range(2)]
        ctx_s = [sb(f"ctx_s{i}", [P, J, C]) for i in range(2)]
        mask_u = [sb(f"mask_u{i}", [P, GT], U8) for i in range(2)]
        mask_b = [sb(f"mask_b{i}", [P, GT]) for i in range(2)]
        any_of = [sb(f"any_of{i}", [P, NB]) for i in range(2)]
        xt_hi = [sb(f"xt_hi{i}", [P, KC, GT], F16) for i in range(2)]
        xt_lo = [sb(f"xt_lo{i}", [P, KC, GT], F16) for i in range(2)]
        nmax = sb("nmax", [P, HP * NB])
        rsum = sb("rsum", [P, HP * NB])
        rinv = sb("rinv", [P, HP * NB])


        NMB = H * KC // 4

        def product_bank(i):
            return banks[:, (0, 1, 2, 3, 6, 7)[i % 6], :]

        def by_batch(hh):
            return xo_ps[:, hh, :].rearrange("p (b t) -> p b t", b=NB)

        def o_view(o, bank):
            half, b2 = bank // 2, bank % 2
            return o.rearrange("p h (j b t) -> p h j b t", j=J, b=2)[:, :, 2 * half:2 * half + 2, b2, :]

        s_x = [sem(f"x_loaded{g}") for g in range(G)]
        s_wk, s_wv, s_wo, s_call = (sem(n) for n in ("wk_loaded", "wv_loaded", "wo_loaded", "all_ctx_loaded"))
        s_wq = [sem(f"wq_loaded{i}") for i in range(2)]
        s_g = sem("gates_loaded")
        s_ident = sem("ident_ready")
        s_ctx = [sem(f"ctx_loaded{i}") for i in range(2)]
        s_dve = sem("dve_setup_step")
        s_mxp = sem("partial_maxima_ready")
        s_mprod = sem("m_product_done")
        s_mcopied = sem("m_product_copied")
        s_nprod = sem("n_product_done")
        s_ncopied = sem("n_product_copied")
        s_maxt = sem("maxima_transposed")
        s_maxd = sem("maxima_diagonal")
        s_maxb = sem("maxima_broadcast")
        s_msh = sem("m_high_ready")
        s_msplit = sem("m_split")
        s_nsh = sem("n_high_ready")
        s_nsplit = sem("n_split")
        s_factor = sem("scores_factor_ready")
        s_tanh = sem("tanh_ready")
        s_xnorm = sem("x_normalised")
        s_xt = sem("x_transposed")
        s_xth = sem("xt_high_ready")
        s_xtl = sem("xt_low_ready")
        s_chigh = sem("ctx_high_ready")
        s_cscale = sem("ctx_scaled_and_split")
        s_mbias = sem("mask_bias_ready")
        s_manyof = sem("mask_any_ready")
        s_xm = sem("xm_head_done")
        s_xma = sem("xm_high_ready")
        s_xmd = sem("xm_low_ready")
        s_sc = sem("scores_done")
        s_msk = sem("scores_masked")
        s_max = sem("row_max_ready")
        s_exp = sem("exp_done")
        s_ri = sem("row_inverse_step")
        s_pnp = sem("first_pair_normalised")
        s_pnd = sem("second_pair_normalised")
        s_pt = sem("probs_transposed")
        s_pta = sem("pt_copied")
        s_pv = sem("head_outputs_done")
        s_oh = sem("outputs_high_ready")
        s_ol = sem("outputs_low_ready")
        s_on = sem("projection_done")
        s_x1 = sem("x1_ready")

        ROW = D + 2
        REGION = B * T + P
        SKIP = 1 << 20
        TF = 2 * B * T // P + E - 1
        U = 8
        REST = TF % U
        assert TF // U > 1 and 2 <= REST
        rows_dram = nc.dram_tensor("expert_rows", [(E + 1) * REGION, ROW], F32, kind="Internal").ap()
        y_dram = nc.dram_tensor("expert_outputs", [2 * B * T, D], F32, kind="Internal").ap()
        y_tiles = y_dram.rearrange("(c g j p) d -> g p c j d", c=2, j=J, p=P)

        ew32 = big[:, 0:E * EW].rearrange("p (e x) -> p e x", e=E)
        ew16 = big[:, 0:E * EW].bitcast(F16).rearrange("p (e x) -> p e x", e=E)
        NGU = KC * GU
        pieces = [(0, GU, 0), (GU, GU, 0), (NGU, NF * D, 1)]
        w_gu = ew16[:, :, 0:2 * NGU].rearrange("p e (k w f) -> p e k w f", k=KC, w=2)
        w_dn = ew16[:, :, 2 * NGU:].rearrange("p e (w c d) -> p e w c d", w=2, c=NF)
        at_aux = 0

        def take_aux(words):
            nonlocal at_aux
            at_aux += words
            assert at_aux <= AUX
            return aux[:, at_aux - words:at_aux]

        row = [take_aux(J * ROW).rearrange("p (j r) -> p j r", j=J) for _ in range(2)]
        x2t_hi, x2t_lo = (take_aux(KC * GT // 2).bitcast(F16).rearrange("p (k n) -> p k n", k=KC) for _ in range(2))
        zero_row = take_aux(ROW)
        split_tmp = take_aux(NF * D)
        late_gu_dn = [(mn[:, 0:NGU], mn[:, NGU:EW]), (mn[:, EW:EW + NGU], split_tmp)]
        fm = sb("fm", [P, 4])
        fm_late = sb("fm_late", [P, 8])
        f_exp = sb("f_exp", [P, 4], I32)
        f_scale = sb("f_scale", [P, E, 2])
        f_inv = sb("f_inv", [P, E, 2])
        tile_scales = sb("tile_scales", [P, 3, E])
        gate_w_s = sb("gate_w_s", [P, KC, E])
        gate_hi = sb("gate_hi", [P, KC, E], F16)
        gate_lo = sb("gate_lo", [P, KC, E], F16)
        gate_b_s = sb("gate_b_s", [P, E])
        bias_s = sb("bias_s", [P, E])
        strict = sb("strict", [P, P], F16)
        ones_sq = sb("ones_sq", [P, P], F16)
        c_one = sb("c_one", [P, 1])
        place = [sb(f"place{c}", [P, TILES], I32) for c in range(2)]
        rev = sb("rev", [P, E])
        region0 = sb("region0", [P, E])
        count = sb("count", [P, E])
        tile_iota = sb("tile_iota", [P, TF])
        c_1p5 = sb("c_1p5", [P, J])
        c_ln = sb("c_ln", [P, J])
        stat2 = sb("stat2", [P, J, 6])
        mv2 = sb("mv2", [P, J, 2])
        v2 = sb("v2", [P, J])
        v2_mhalf = sb("v2_mhalf", [P, J])
        y2 = sb("y2", [P, J])
        t2 = sb("t2", [P, J])
        lg = sb("lg", [P, J, E])
        ex = sb("ex", [P, J, E])
        rt = sb("rt", [P, J, E])
        rt2 = sb("rt2", [P, J, E])
        key = sb("key", [P, J, E])
        half4 = sb("half4", [P, J, E // 2])
        half2 = sb("half2", [P, J, E // 4])
        best = sb("best", [P, J])
        oh = [sb(f"oh{c}", [P, J, E]) for c in range(2)]
        chosen = sb("chosen", [P, J, E], F16)
        pos = sb("pos", [P, J, E])
        red = sb("red", [P, J])
        rsum2 = sb("rsum2", [P, J])
        slot_f = sb("slot_f", [P, 2, J])
        slot = sb("slot", [P, 2, J], I32)
        numbers = sb("numbers", [P, E])
        n_tiles = sb("n_tiles", [P, E])
        n_tiles_i = sb("n_tiles_i", [P, E], I32)
        t_end = sb("t_end", [P, E])
        t_e_i = sb("t_e_i", [P, TF], I32)
        t_row_i = sb("t_row_i", [P, TF], I32)
        t_sc = [sb(f"t_sc{i}", [P, TF]) for i in range(3)]
        tail_i = sb("tail_i", [P, E], I32)
        at_t = 2 * EW

        def take_mn(words):
            nonlocal at_t
            at_t += words
            assert at_t <= 4 * MNW
            return mn[:, at_t - words:at_t]

        past = take_mn(TF * E).rearrange("p (t e) -> p t e", t=TF)
        pick = take_mn(TF * E).rearrange("p (t e) -> p t e", t=TF)
        t_e, t_c, t_s, t_row = (take_mn(TF) for _ in range(4))

        s_small = sem("router_constants_loaded")
        s_iota = sem("iotas_ready")
        s_fw = sem("expert_weights_loaded")
        s_fwl = sem("late_expert_weights_loaded")
        s_pad = sem("expert_padding_zero")
        s_fpm = sem("expert_partial_max")
        s_fam = sem("expert_max_everywhere")
        s_fch = sem("expert_scale_step")
        s_fsp = sem("expert_split_step")
        s_flate = sem("late_expert_step")
        s_fpl = sem("late_expert_step_on_pool")
        s_rs = sem("stats_step")
        s_seed = sem("rstd_seed_ready")
        s_nw = sem("newton_step")
        s_rstd = sem("ln2_rstd_ready")
        s_row = sem("first_rows_ready")
        s_row1 = sem("second_rows_ready")
        s_x2t = sem("x2_transposed")
        s_x2h = sem("x2_high_ready")
        s_x2c = sem("x2_low_ready")
        s_gate_w = sem("gate_weights_split_step")
        s_lg = sem("logits_done")
        s_sh = sem("logits_step")
        s_l1 = sem("logits_shifted")
        s_ex = sem("logits_exponentials")
        s_sm = sem("exponentials_summed")
        s_tk = sem("top2_step")
        s_cho = sem("choices_ready")
        s_pos = sem("positions_done")
        s_pc = sem("position_step")
        s_posr = sem("positions_ready")
        s_sl = sem("slot_step")
        s_scat = sem("rows_scattered")
        s_passed = sem("pool_passed")
        s_passed_v = sem("dve_passed")
        s_passed_s = sem("sp_passed")
        s_tail = sem("tail_places_ready")
        s_tailz = sem("tail_rows_stored")
        s_zero = sem("zero_row_ready")
        s_tab = sem("tile_tables_ready")

        def sum_experts(step, src, out):
            step(half4[:], src[:, :, 0:E // 2], src[:, :, E // 2:E], ALU.add)
            step(half2[:], half4[:, :, 0:E // 4], half4[:, :, E // 4:E // 2], ALU.add)
            step(out, half2[:, :, 0], half2[:, :, 1], ALU.add)

        def over_e(v):
            return v.unsqueeze(2).to_broadcast([P, J, E])

        def over_j(v):
            return v.unsqueeze(1).to_broadcast([P, J, E])

        IOTAS = 12
        RS, NW, SH, SM, TK, SL, PC = 4, 12, 2, 4, 12, 9, 2

        def route_stats(dve, r):
            dve.wait_ge(s_x1, r + 1)
            if not (isinstance(r, int) and r < 1):
                dve.wait_ge(s_row1, r)
            dve.sem_inc(s_passed_v)
            for j in range(J):
                b = dve.bn_stats(stat2[:, j, :], x_res[:, bass.ds(r * J + j, 1), :].rearrange("p a d -> p (a d)"))
            b.then_inc(s_rs, 1)
            dve.wait_ge(s_rs, RS * r + 1)
            dve.sem_inc(s_passed_v)
            for j in range(J):
                b = dve.bn_aggr(mv2[:, j, :], stat2[:, j, :])
            b.then_inc(s_rs, 1)
            dve.wait_ge(s_rs, RS * r + 2)
            dve.tensor_scalar(v2[:], mv2[:, :, 1], EPS, None, ALU.add).then_inc(s_rs, 1)
            dve.wait_ge(s_rs, RS * r + 3)
            dve.tensor_scalar(v2_mhalf[:], v2[:], -0.5, None, ALU.mult)
            dve.tensor_scalar(y2[:].bitcast(I32), v2[:].bitcast(I32), 1, None, ALU.logical_shift_right).then_inc(s_rs, 1)
            dve.wait_ge(s_rs, RS * r + 4)
            dve.tensor_scalar(y2[:].bitcast(I32), y2[:].bitcast(I32), -1.0, float(0x5F3759DF), ALU.mult, ALU.add).then_inc(s_seed, 1)

        def route_newton(pool, r):
            k = 0
            pool.wait_ge(s_seed, r + 1)
            for _ in range(3):
                for o, a, b in ((t2, y2, y2), (t2, t2, v2_mhalf), (t2, t2, c_1p5), (y2, y2, t2)):
                    pool.tensor_tensor(o[:], a[:], b[:], ALU.add if b is c_1p5 else ALU.mult).then_inc(s_nw, 1)
                    k += 1
                    pool.wait_ge(s_nw, NW * r + k)
            assert k == NW
            pool.tensor_tensor(y2[:], y2[:], c_ln[:], ALU.mult).then_inc(s_rstd, 1)

        def route_row(dve, r, c):
            for j in range(J):
                b = dve.tensor_scalar(row[c][:, j, 0:D], x_res[:, bass.ds(r * J + j, 1), :].rearrange("p a d -> p (a d)"),
                                      mv2[:, j, 0:1], y2[:, j:j + 1], ALU.subtract, ALU.mult)
            return b

        def route_rows_first(dve, r):
            dve.wait_ge(s_rstd, r + 1)
            if not (isinstance(r, int) and r < 1):
                dve.wait_ge(s_scat, 16 * 2 * J * r)
            route_row(dve, r, 0).then_inc(s_row, 1)

        def route_rows_second(dve, r):
            route_row(dve, r, 1)
            for c in range(2):
                b = dve.tensor_copy(row[c][:, :, D + 1].bitcast(I32), place[c][:, bass.ds(r * J, J)])
            b.then_inc(s_row1, 1)

        def route_transposes(pe, r):
            pe.wait_ge(s_row, r + 1)
            for kc in range(KC):
                for j in range(J):
                    mm = pe.transpose(tr_ps[:, kc, j * P:(j + 1) * P], row[0][:, j, kc * P:(kc + 1) * P], ident[:])
            mm.then_inc(s_x2t, 1)

        def route_high(act, r):
            act.wait_ge(s_x2t, r + 1)
            act.activation(x2t_hi, tr_ps, ACT.Copy).then_inc(s_x2h, 1)

        def route_low(dve, r):
            dve.wait_ge(s_x2h, r + 1)
            dve.tensor_tensor(x2t_lo, tr_ps, x2t_hi, ALU.subtract).then_inc(s_x2c, 1)

        def route_logits(pe, r):
            pe.wait_ge(s_x2c, r + 1)
            for j in range(J):
                n = 0
                for kc in range(KC):
                    for x, w in ((x2t_hi, gate_hi), (x2t_hi, gate_lo), (x2t_lo, gate_hi)):
                        mm = pe.matmul(banks[:, 6, j * E:(j + 1) * E], x[:, kc, j * P:(j + 1) * P], w[:, kc, :],
                                       start=(n == 0), stop=(n == 3 * KC - 1))
                        n += 1
            mm.then_inc(s_lg, 1)

        def route_shift(dve, r):
            dve.wait_ge(s_lg, r + 1)
            if not (isinstance(r, int) and r < 1):
                dve.wait_ge(s_cho, r)
            dve.scalar_tensor_tensor(out=rt[:], in0=banks[:, 6, 0:J * E].rearrange("p (j e) -> p j e", j=J), scalar=consts[:, 6:7],
                                     in1=over_j(gate_b_s[:]), op0=ALU.mult, op1=ALU.add).then_inc(s_sh, 1)
            dve.wait_ge(s_sh, SH * r + 1)
            dve.tensor_reduce(red[:], rt[:], AX_X, ALU.max).then_inc(s_sh, 1)
            dve.wait_ge(s_sh, SH * r + 2)
            dve.tensor_tensor(lg[:], rt[:], over_e(red[:]), ALU.subtract).then_inc(s_l1, 1)

        def route_exp(act, r):
            act.wait_ge(s_l1, r + 1)
            if not (isinstance(r, int) and r < 1):
                act.wait_ge(s_cho, r)
            act.activation(ex[:], lg[:], ACT.Exp).then_inc(s_ex, 1)

        def route_weights(dve, r):
            dve.wait_ge(s_ex, r + 1)
            dve.tensor_reduce(rsum2[:], ex[:], AX_X, ALU.add).then_inc(s_sm, 1)
            dve.wait_ge(s_sm, SM * r + 1)
            dve.reciprocal(rsum2[:], rsum2[:]).then_inc(s_sm, 1)
            dve.wait_ge(s_sm, SM * r + 2)
            dve.tensor_tensor(rt[:], ex[:], over_e(rsum2[:]), ALU.mult).then_inc(s_sm, 1)
            dve.wait_ge(s_sm, SM * r + 3)
            dve.tensor_tensor(rt[:], rt[:], over_j(bias_s[:]), ALU.add).then_inc(s_sm, 1)

        def route_choice(dve, r, c):
            k = TK // 2 * c

            def step(ins):
                nonlocal k
                k += 1
                ins.then_inc(s_tk, 1)
                dve.wait_ge(s_tk, TK * r + k)

            if c == 0:
                dve.wait_ge(s_sm, SM * (r + 1))
            src, weight = (rt, rt2)[c], row[c][:, :, D]
            step(dve.tensor_reduce(weight, src[:], AX_X, ALU.max))
            step(dve.tensor_tensor(key[:], src[:], over_e(weight), ALU.is_equal))
            step(dve.tensor_tensor(key[:], key[:], over_j(rev[:]), ALU.mult))
            step(dve.tensor_reduce(best[:], key[:], AX_X, ALU.max))
            step(dve.tensor_tensor(oh[c][:], key[:], over_e(best[:]), ALU.is_equal))
            if c == 0:
                step(dve.scalar_tensor_tensor(out=rt2[:], in0=oh[0][:], scalar=NEG, in1=rt[:], op0=ALU.mult, op1=ALU.add))
            else:
                step(dve.tensor_tensor(chosen[:], oh[0][:], oh[1][:], ALU.add))
                dve.sem_inc(s_cho)

        def route_positions(pe, r):
            pe.wait_ge(s_cho, r + 1)
            pe.matmul(banks[:, 6, 0:J * E], strict[:], chosen[:].rearrange("p j e -> p (j e)"), start=True, stop=False, skip_group_check=True)
            for n in range(J - 1, 0, -1):
                pe.matmul(banks[:, 6, (J - n) * E:J * E], ones_sq[:], chosen[:, 0:n, :].rearrange("p j e -> p (j e)"),
                          start=False, stop=(n == 1), skip_group_check=True)
            for j in range(J):
                mm = pe.matmul(banks[:, 6, J * E:(J + 1) * E], ones_sq[:], chosen[:, j, :], start=(j == 0), stop=(j == J - 1), skip_group_check=True)
            mm.then_inc(s_pos, 1)

        def route_places(dve, r):
            dve.wait_ge(s_pos, r + 1)
            dve.tensor_tensor(pos[:], banks[:, 6, 0:J * E].rearrange("p (j e) -> p j e", j=J), over_j(count[:]), ALU.add).then_inc(s_pc, 1)
            dve.wait_ge(s_pc, PC * r + 1)
            dve.tensor_tensor(count[:], banks[:, 6, J * E:(J + 1) * E], count[:], ALU.add).then_inc(s_pc, 1)
            dve.wait_ge(s_pc, PC * r + 2)
            dve.sem_inc(s_posr)

        def route_scatter(pool, r):
            k = 0

            def step(out, a, b, op):
                nonlocal k
                k += 1
                pool.tensor_tensor(out, a, b, op).then_inc(s_sl, 1)
                pool.wait_ge(s_sl, SL * r + k)

            pool.wait_ge(s_posr, r + 1)
            for c in range(2):
                step(oh[c][:], oh[c][:], pos[:], ALU.mult)
                sum_experts(step, oh[c], slot_f[:, c, :])
            pool.sem_inc(s_passed)
            pool.tensor_copy(slot[:], slot_f[:]).then_inc(s_sl, 1)
            assert k + 1 == SL
            pool.wait_ge(s_sl, SL * (r + 1))
            pool.sem_inc(s_passed)
            for c in range(2):
                for j in range(J):
                    pool.indirect_dma_start(rows_dram, bass.IndirectOffsetOnAxis(ap=slot[:, c, j:j + 1], axis=0),
                                            row[c][:, j, :], None).then_inc(s_scat, 16)

        def load_expert(sp, e, gu, dn, done):
            dn = dn.rearrange("p (c d) -> p c d", c=NF)
            sp.dma_start(gu.rearrange("p (k f) -> p k f", k=KC), w_gu_t[e].rearrange("(k p) f -> p k f", p=P)).then_inc(done, 16)
            sp.dma_start(dn[:, 0:2, :], w_down_t[e, 0:2 * P, :].rearrange("(c p) d -> p c d", p=P)).then_inc(done, 16)
            sp.dma_start(dn[0:F - 2 * P, 2, :], w_down_t[e, 2 * P:F, :]).then_inc(done, 16)

        def expert_max(dve, e):
            dve.wait_ge(s_fw, 48 * EARLY)
            if not (isinstance(e, int) and e < 1):
                dve.wait_ge(s_fam, e)
            one = bass.ds(e, 1)
            dve.tensor_reduce(fm[:, 0:1], ew32[:, one, 0:NGU].rearrange("p a x -> p (a x)"), AX_X, ALU.max, apply_absolute_value=True)
            dve.tensor_reduce(fm[:, 1:2], ew32[:, one, NGU:EW].rearrange("p a x -> p (a x)"), AX_X, ALU.max, apply_absolute_value=True).then_inc(s_fpm, 1)

        def expert_max_all(pool, e):
            pool.wait_ge(s_fpm, e + 1)
            pool.sem_inc(s_passed)
            pool.partition_all_reduce(fm[:, 2:4], fm[:, 0:2], P, bass.bass_isa.ReduceOp.max).then_inc(s_fam, 1)

        def powers_of_two(step, scale, inv, exponent, maxima):
            step(lambda v: v.tensor_scalar(scale, maxima, 1e-30, 1e30, ALU.max, ALU.min))
            step(lambda v: v.tensor_scalar(exponent, scale.bitcast(I32), 0x7F800000, None, ALU.bitwise_and))
            step(lambda v: v.tensor_scalar(scale.bitcast(I32), exponent, -1.0, float((254 + TOP) << 23), ALU.mult, ALU.add))
            step(lambda v: v.tensor_scalar(inv.bitcast(I32), exponent, -float(TOP << 23), None, ALU.add))

        def expert_scale(dve, e):
            dve.wait_ge(s_fam, e + 1)
            one = bass.ds(e, 1)
            k = 0

            def step(make):
                nonlocal k
                k += 1
                make(dve).then_inc(s_fch, 1)
                dve.wait_ge(s_fch, 4 * e + k)

            powers_of_two(step, f_scale[:, one, :].rearrange("p a n -> p (a n)"), f_inv[:, one, :].rearrange("p a n -> p (a n)"),
                          f_exp[:, 0:2], fm[:, 2:4])
            dve.sem_inc(s_passed_v)

        late_tmp = take_mn(NF * D)

        def late_piece(i, n):
            first, words, which = pieces[n]
            full = late_gu_dn[i][which][:, first:first + words] if which == 0 else late_gu_dn[i][which]
            hi, lo = (ew16[:, EARLY + i, 2 * first + w * words:2 * first + (w + 1) * words] for w in (0, 1))
            return full, hi, lo, f_scale[:, EARLY + i, which:which + 1], words

        def expert_split(pool, e, i):
            first, n, which = pieces[i]
            one = bass.ds(e, 1)
            if i == 0:
                pool.wait_ge(s_fch, 4 * (e + 1))
            full = ew32[:, one, first:first + n].rearrange("p a x -> p (a x)")
            hi = ew16[:, one, 2 * first:2 * first + n].rearrange("p a x -> p (a x)")
            lo = ew16[:, one, 2 * first + n:2 * (first + n)].rearrange("p a x -> p (a x)")
            tmp = split_tmp[:, 0:n]
            steps = ((tmp, full, f_scale[:, one, which].to_broadcast([P, n]), ALU.mult), (hi, tmp, c_one[:].to_broadcast([P, n]), ALU.mult), (lo, tmp, hi, ALU.subtract))
            for k, (out, a, b, op) in enumerate(steps):
                pool.tensor_tensor(out, a, b, op).then_inc(s_fsp, 1)
                pool.wait_ge(s_fsp, 9 * e + 3 * i + k + 1)
            pool.sem_inc(s_passed)

        def link(eng, sem_, chain, ins):
            chain[0] += 1
            ins.then_inc(sem_, 1)
            eng.wait_ge(sem_, chain[0])

        with nc.Block() as block:

            @block.sync
            def _(sp):
                sp.dma_start(wk_s, wk_t.rearrange("(h p) c -> p h c", p=P)).then_inc(s_wk, 16)
                for i in range(2):
                    half = slice(i * H // 2, (i + 1) * H // 2)
                    sp.dma_start(wq_s[:, half, :], wq_t.rearrange("(h p) d -> p h d", p=P)[:, half, :]).then_inc(s_wq[i], 16)
                sp.dma_start(gate_w_s[:], gate_w_t.rearrange("(k p) e -> p k e", p=P)).then_inc(s_small, 16)
                sp.dma_start(gate_b_s[:], gate_b.rearrange("(a e) -> a e", a=1).to_broadcast([P, E])).then_inc(s_small, 16)
                sp.dma_start(bias_s[:], expert_bias.rearrange("(a e) -> a e", a=1).to_broadcast([P, E])).then_inc(s_small, 16)
                sp.dma_start(ctx_all.rearrange("p (t c) -> p t c", t=TILES),
                             ctx.rearrange("b s c -> (b s) c").rearrange("(t p) c -> p t c", p=P)).then_inc(s_call, 16)

                def load_group(g, b):
                    if not (isinstance(g, int) and g < 2):
                        sp.wait_ge(s_on, Q * (g - 1))
                        sp.sem_inc(s_passed_s)
                        sp.wait_ge(s_msk, 2 * Q * (g - 1))
                        sp.wait_ge(s_manyof, g - 1)
                        sp.sem_inc(s_passed_s)
                    if not (isinstance(g, int) and g < 1):
                        sp.wait_ge(s_cscale, g)
                        sp.sem_inc(s_passed_s)
                    sp.dma_start(ctx_t_s[:], ctx_t_groups[bass.ds(g, 1), :, :].rearrange("a c n -> c (a n)")).then_inc(s_ctx[b], 16)
                    sp.dma_start(ctx_s[b][:], ctx_tiles[bass.ds(g, 1), :, :, :].rearrange("a p j c -> p (a j) c")).then_inc(s_ctx[b], 16)
                    sp.dma_start(mask_u[b][:], mask_groups[bass.ds(g, 1), :, :].rearrange("a b n -> (a b) n").to_broadcast([P, GT])).then_inc(s_ctx[b], 16)

                load_group(0, 0)
                for g in range(1, G):
                    sp.dma_start(x_res[:, g * J:(g + 1) * J, :], x_tiles[g]).then_inc(s_x[g], 16)
                load_group(1, 1)
                sp.wait_ge(s_pad, 1)
                for e in range(EARLY):
                    load_expert(sp, e, ew32[:, e, 0:NGU], ew32[:, e, NGU:EW], s_fw)
                with nc.sync.Fori(0, (G - 2) // 2) as k:
                    load_group(2 + 2 * k, 0)
                    load_group(3 + 2 * k, 1)
                sp.wait_ge(s_pad, 2)
                for i in range(E - EARLY):
                    load_expert(sp, EARLY + i, *late_gu_dn[i], s_fwl)

            @block.gpsimd
            def _(pool):
                pool.memset(ident[:], 0.0).then_inc(s_ident, 1)
                pool.memset(ones[:], 1.0).then_inc(s_ident, 1)
                pool.wait_ge(s_ident, 2)
                pool.affine_select(out=ident[:], in_=ident[:], compare_op=ALU.not_equal, fill=1.0, base=0,
                                   pattern=[[-1, P]], channel_multiplier=1).then_inc(s_ident, 1)

                n = 0

                def made(ins):
                    nonlocal n
                    n += 1
                    ins.then_inc(s_iota, 1)

                made(pool.memset(ones_sq[:], 1.0))
                made(pool.memset(strict[:], 0.0))
                pool.wait_ge(s_iota, n)
                made(pool.affine_select(out=strict[:], in_=strict[:], compare_op=ALU.is_ge, fill=1.0, base=0,
                                        pattern=[[-1, P]], channel_multiplier=1))
                made(pool.memset(c_1p5[:], 1.5))
                made(pool.memset(c_ln[:], LN_SCALE))
                made(pool.memset(c_one[:], 1.0))
                for c in range(2):
                    made(pool.iota(place[c][:], pattern=[[P, TILES]], base=c * B * T, channel_multiplier=1))
                made(pool.iota(rev[:], pattern=[[-1, E]], base=E, channel_multiplier=0, allow_small_or_imprecise_dtypes=True))
                made(pool.iota(region0[:], pattern=[[REGION, E]], base=0, channel_multiplier=0, allow_small_or_imprecise_dtypes=True))
                made(pool.iota(count[:], pattern=[[REGION, E]], base=0, channel_multiplier=0, allow_small_or_imprecise_dtypes=True))
                made(pool.iota(tile_iota[:], pattern=[[1, TF]], base=0, channel_multiplier=0, allow_small_or_imprecise_dtypes=True))
                assert n == IOTAS
                pool.wait_ge(s_iota, IOTAS)
                pool.wait_ge(s_small, 48)

                def normalise_probs(u):
                    pool.wait_ge(s_ri, 4 * u + 2)
                    pool.tensor_tensor(pn[:, 0, :].rearrange("p (b s) -> p b s", s=S), pr[:, 0, :].rearrange("p (b s) -> p b s", s=S),
                                       rinv[:, 0:NB].unsqueeze(2).to_broadcast([P, NB, S]), ALU.mult).then_inc(s_pnp, 1)

                def group(g, route, experts):
                    for q in range(Q):
                        if q == 3 and route and not experts:
                            pool.wait_ge(s_xm, HU * Q * G)
                            pool.memset(late_gu_dn[0][1][:, 2 * D:], 0.0)
                            pool.memset(late_gu_dn[1][1][:, 2 * D:], 0.0).then_inc(s_pad, 1)
                        normalise_probs(Q * g + q)
                        if q == 2 and not route:
                            pool.wait_ge(s_nsplit, Q)
                            pool.wait_ge(s_msplit, Q)
                            pool.memset(ew32[:, 0:EARLY, NGU + 2 * D:EW], 0.0).then_inc(s_pad, 1)
                            pool.memset(zero_row[:, 0:D + 1], 0.0).then_inc(s_zero, 1)
                            pool.iota(zero_row[:, D + 1:D + 2].bitcast(I32), pattern=[[0, 1]], base=SKIP, channel_multiplier=0).then_inc(s_zero, 1)
                        if q == 0 and experts:
                            expert_max_all(pool, g - 1)
                        if q == 1 and route:
                            route_newton(pool, g - 1)
                        if q == 1 and experts:
                            expert_split(pool, g - 1, 0)
                        if q == 2 and experts:
                            expert_split(pool, g - 1, 1)
                            expert_split(pool, g - 1, 2)
                        if q == 3 and route:
                            route_scatter(pool, g - 1)

                group(0, False, False)
                with nc.gpsimd.Fori(0, (G - 2) // 2) as k:
                    group(1 + 2 * k, True, True)
                    group(2 + 2 * k, True, True)
                group(G - 1, True, False)
                pool.wait_ge(s_flate, 1)
                pool.partition_all_reduce(fm_late[:, 4:8], fm_late[:, 0:4], P, bass.bass_isa.ReduceOp.max).then_inc(s_fam, 1)

            @block.scalar
            def _(act):
                act.dma_start(gates[:, 0:1], g_xattn.rearrange("(a n) -> a n", a=1).to_broadcast([P, 1])).then_inc(s_g, 16)
                act.dma_start(gates[:, 1:2], g_ffn.rearrange("(a n) -> a n", a=1).to_broadcast([P, 1])).then_inc(s_g, 16)
                act.dma_start(x_res[:, 0:J, :], x_tiles[0]).then_inc(s_x[0], 16)
                act.dma_start(wv_s, wv_t.rearrange("(h p) c -> p h c", p=P)).then_inc(s_wv, 16)
                act.dma_start(wo_s, wo.rearrange("(h p) d -> p h d", p=P)).then_inc(s_wo, 16)
                act.wait_ge(s_g, 32)
                act.activation(consts[:, 0:2], gates[:], ACT.Tanh).then_inc(s_tanh, 1)
                for i in range(NMB):
                    act.wait_ge(s_mprod, i + 1)
                    kc, hq = i % KC, i // KC
                    act.activation(mf[:, kc, 4 * hq:4 * hq + 4, :].rearrange("p h c -> p (h c)"), product_bank(i), ACT.Copy).then_inc(s_mcopied, 1)
                for i in range(H // 2):
                    act.wait_ge(s_nprod, i + 1)
                    act.activation(nf[:, 2 * i:2 * i + 2, :].rearrange("p h d -> p (h d)"), product_bank(NMB + i), ACT.Copy).then_inc(s_ncopied, 1)

                def xm_high(u, xm_u, h):
                    act.wait_ge(s_xm, HU * u + h + 1)
                    act.activation(xm_u[0][:, h // 2, h % 2, :, :], by_batch(h), ACT.Copy, scale=XM_SCALE).then_inc(s_xma, 1)

                def xt_high(g, b):
                    act.wait_ge(s_xt, KC * (g + 1))
                    act.activation(xt_hi[b][:], tr_ps, ACT.Copy).then_inc(s_xth, 1)

                def unit(u, xm_next, last, g, b, q, route, more):
                    if not last:
                        xm_high(u + 1, xm_next, 0)
                    for hp in range(HP):
                        act.wait_ge(s_max, HP * u + hp + 1)
                        if hp == 0 and not (isinstance(u, int) and u < 1):
                            act.wait_ge(s_pnd, u)
                        for batch in range(NB):
                            i = hp * NB + batch
                            e = act.activation(pr[:, hp, batch * S:(batch + 1) * S], sm[:, hp, batch * S:(batch + 1) * S],
                                               ACT.Exp, bias=nmax[:, i:i + 1], accum_out=rsum[:, i:i + 1])
                        e.then_inc(s_exp, 1)
                        if not last:
                            for h in ((1,), (2, 3))[hp]:
                                xm_high(u + 1, xm_next, h)
                        if hp == 1 and q == 1 and more:
                            xt_high(g + 1, 1 - b)
                        if hp == 1 and q == 2 and route:
                            route_high(act, g - 1)
                    for hp in range(HP):
                        act.wait_ge(s_pt, HP * u + hp + 1)
                        act.activation(pt[:, :, hp, :], sp_ps[:, hp, :].rearrange("p (j n) -> p j n", j=J), ACT.Copy).then_inc(s_pta, 1)
                    for bank in range(4):
                        act.wait_ge(s_pv, 4 * u + bank + 1)
                        act.activation(o_view(o_hi, bank), xo_ps[:, bank, :].rearrange("p (j h t) -> p h j t", j=2, h=HU), ACT.Copy).then_inc(s_oh, 1)
                    if q == 2 and route:
                        route_exp(act, g - 1)

                xt_high(0, 0)
                for h in range(HU):
                    xm_high(0, xm[0], h)

                def group(g, b, route, last):
                    for q in range(Q):
                        unit(Q * g + q, xm[(q + 1) % 2], last and q == Q - 1, g, b, q, route, not last)

                group(0, 0, False, False)
                with nc.scalar.Fori(0, (G - 2) // 2) as k:
                    group(1 + 2 * k, 1, True, False)
                    group(2 + 2 * k, 0, True, False)
                group(G - 1, 1, True, True)

            @block.vector
            def _(dve):
                chain = [0]

                def step(ins):
                    link(dve, s_dve, chain, ins)

                def normalise(g):
                    if not (isinstance(g, int) and g < 1):
                        dve.wait_ge(s_xt, KC * g)
                    for j in range(J):
                        t = bass.ds(g * J + j, 1)
                        n = dve.tensor_scalar(xn[:, j, :], x_res[:, t, :].rearrange("p a d -> p (a d)"),
                                              mean_var[:, t, 0:1].rearrange("p a b -> p (a b)"), rstd[:, t], ALU.subtract, ALU.mult)
                    n.then_inc(s_xnorm, 1)

                def token_stats(groups):
                    for g in groups:
                        dve.wait_ge(s_x[g], 16)
                        for j in range(J):
                            last = dve.bn_stats(stats[:, g * J + j, :], x_res[:, g * J + j, :])
                        step(last)
                        for j in range(J):
                            last = dve.bn_aggr(mean_var[:, g * J + j, :], stats[:, g * J + j, :])
                    step(last)
                    tiles = slice(groups[0] * J, (groups[-1] + 1) * J)
                    v, t, y = nwt[:, 0, tiles], nwt[:, 1, tiles], rstd[:, tiles]
                    step(dve.tensor_scalar(v, mean_var[:, tiles, 1], EPS, None, ALU.add))
                    step(dve.tensor_scalar(y.bitcast(I32), v.bitcast(I32), 1, None, ALU.logical_shift_right))
                    step(dve.tensor_scalar(y.bitcast(I32), y.bitcast(I32), -1.0, float(0x5F3759DF), ALU.mult, ALU.add))
                    for n in range(3):
                        step(dve.tensor_tensor(t, y, y, ALU.mult))
                        step(dve.scalar_tensor_tensor(out=t, in0=t, scalar=-0.5, in1=v, op0=ALU.mult, op1=ALU.mult))
                        step(dve.scalar_tensor_tensor(out=y, in0=t, scalar=1.5, in1=y, op0=ALU.add, op1=ALU.mult))
                    step(dve.tensor_scalar(y, y, LN_SCALE, None, ALU.mult))

                def xt_low(g, b):
                    dve.wait_ge(s_xth, g + 1)
                    dve.tensor_tensor(xt_lo[b][:], tr_ps, xt_hi[b][:], ALU.subtract).then_inc(s_xtl, 1)

                def context(b, g, turn):
                    dve.wait_ge(s_ctx[b], 48 * turn)
                    dve.tensor_scalar(ctx_s[b][:], ctx_s[b][:], scale_of[:, 2:3], None, ALU.mult)
                    dve.tensor_scalar(ctx_t_hi[b][:], ctx_t_s[:], scale_of[:, 2:3], None, ALU.mult).then_inc(s_chigh, 1)
                    dve.wait_ge(s_chigh, g + 1)
                    dve.scalar_tensor_tensor(out=ctx_t_lo[b][:], in0=ctx_t_s[:], scalar=scale_of[:, 2:3], in1=ctx_t_hi[b][:],
                                             op0=ALU.mult, op1=ALU.subtract).then_inc(s_cscale, 1)
                    dve.tensor_scalar(mask_b[b][:], mask_u[b][:], -1.0, -NEG, ALU.add, ALU.mult).then_inc(s_mbias, 1)
                    dve.tensor_reduce(any_of[b][:], mask_u[b][:].rearrange("p (b s) -> p b s", s=S), AX_X, ALU.max).then_inc(s_manyof, 1)

                def split_m(q):
                    heads = slice(HU * q, HU * (q + 1))
                    dve.tensor_scalar(m_hi[:, :, heads, :], mf[:, :, heads, :], scale_of[:, 0:1], None, ALU.mult).then_inc(s_msh, 1)
                    dve.wait_ge(s_msh, q + 1)
                    for kc in range(KC):
                        last = dve.scalar_tensor_tensor(out=m_lo[:, kc, heads, :], in0=mf[:, kc, heads, :], scalar=scale_of[:, 0:1],
                                                        in1=m_hi[:, kc, heads, :], op0=ALU.mult, op1=ALU.subtract)
                    last.then_inc(s_msplit, 1)

                def split_n(q):
                    heads = slice(HU * q, HU * (q + 1))
                    dve.tensor_scalar(n_hi[:, heads, :], nf[:, heads, :], scale_of[:, 1:2], None, ALU.mult).then_inc(s_nsh, 1)
                    dve.wait_ge(s_nsh, q + 1)
                    dve.scalar_tensor_tensor(out=n_lo[:, heads, :], in0=nf[:, heads, :], scalar=scale_of[:, 1:2],
                                             in1=n_hi[:, heads, :], op0=ALU.mult, op1=ALU.subtract).then_inc(s_nsplit, 1)

                def xm_low(u, xm_u, h):
                    dve.wait_ge(s_xma, HU * u + h + 1)
                    dve.scalar_tensor_tensor(out=xm_u[1][:, h // 2, h % 2, :, :], in0=by_batch(h), scalar=XM_SCALE, in1=xm_u[0][:, h // 2, h % 2, :, :],
                                             op0=ALU.mult, op1=ALU.subtract).then_inc(s_xmd, 1)

                def row_inverse(u, b, hp):
                    one = slice(hp * NB, (hp + 1) * NB)
                    dve.wait_ge(s_exp, HP * u + hp + 1)
                    if hp == 0 and not (isinstance(u, int) and u < 1):
                        dve.wait_ge(s_pnp, u)
                        dve.wait_ge(s_pnd, u)
                    dve.reciprocal(rinv[:, one], rsum[:, one]).then_inc(s_ri, 1)
                    dve.wait_ge(s_ri, 4 * u + 2 * hp + 1)
                    dve.tensor_tensor(rinv[:, one], rinv[:, one], any_of[b][:], ALU.mult).then_inc(s_ri, 1)

                def unit(u, g, b, q, xm_next, last, route, experts, more, turn_next):
                    r = g - 1
                    for hp in range(HP):
                        dve.wait_ge(s_sc, HP * u + hp + 1)
                        if hp == 0 and not (isinstance(u, int) and u < 1):
                            dve.wait_ge(s_exp, HP * u)
                        dve.scalar_tensor_tensor(out=sm[:, hp, :], in0=sp_ps[:, hp, :], scalar=consts[:, 2:3], in1=mask_b[b][:],
                                                 op0=ALU.mult, op1=ALU.add).then_inc(s_msk, 1)
                        dve.wait_ge(s_msk, HP * u + hp + 1)
                        dve.tensor_reduce(nmax[:, hp * NB:(hp + 1) * NB], sm[:, hp, :].rearrange("p (b s) -> p b s", s=S),
                                          AX_X, ALU.max, negate=True).then_inc(s_max, 1)
                    if q == 0 and not route:
                        split_n(0)
                        split_m(2)
                    if q == 1 and not route:
                        split_n(1)
                    if q == 2 and not route:
                        split_n(2)
                    if q == 3 and not route:
                        token_stats((2, 3, 4))
                    if q == 1 and more and not route:
                        normalise(g + 1)
                    if q == 1 and experts:
                        expert_scale(dve, r)
                    if q == 3 and route:
                        route_weights(dve, r)
                        route_choice(dve, r, 0)
                    if not last:
                        xm_low(u + 1, xm_next, 0)
                    row_inverse(u, b, 0)
                    if q == 2 and route:
                        route_rows_first(dve, r)
                    if q == 3 and route:
                        route_choice(dve, r, 1)
                    if not last:
                        xm_low(u + 1, xm_next, 1)
                    row_inverse(u, b, 1)
                    dve.wait_ge(s_ri, 4 * u + 4)
                    dve.tensor_tensor(pn[:, 1, :].rearrange("p (b s) -> p b s", s=S), pr[:, 1, :].rearrange("p (b s) -> p b s", s=S),
                                      rinv[:, NB:2 * NB].unsqueeze(2).to_broadcast([P, NB, S]), ALU.mult).then_inc(s_pnd, 1)
                    if not last:
                        xm_low(u + 1, xm_next, 2)
                        xm_low(u + 1, xm_next, 3)
                    if q == 0 and not route:
                        token_stats((1,))
                    if q == 2 and not route:
                        split_n(3)
                        dve.wait_ge(s_msplit, Q)
                    if q == 3 and not route:
                        token_stats((5, 6, 7))
                    if q == 0 and more and route:
                        normalise(g + 1)
                    if q == 0 and experts:
                        expert_max(dve, r)
                    if q == 1 and more:
                        xt_low(g + 1, 1 - b)
                    if q == 1 and not route:
                        split_m(3)
                    if q == 1 and route:
                        route_stats(dve, r)
                    if q == 2 and route:
                        route_low(dve, r)
                        route_shift(dve, r)
                        route_rows_second(dve, r)
                    if q == 2 and more:
                        context(1 - b, g + 1, turn_next)
                    if q == 3 and route:
                        route_places(dve, r)
                    for bank in range(4):
                        dve.wait_ge(s_oh, 4 * u + bank + 1)
                        dve.tensor_tensor(o_view(o_lo, bank), xo_ps[:, bank, :].rearrange("p (j h t) -> p h j t", j=2, h=HU),
                                          o_view(o_hi, bank), ALU.subtract).then_inc(s_ol, 1)

                def residual(g):
                    dve.wait_ge(s_on, Q * (g + 1))
                    t = bass.ds(g * J, J)
                    if isinstance(g, int):
                        t = slice(g * J, g * J + J)
                    dve.scalar_tensor_tensor(out=x_res[:, t, :], in0=acc, scalar=consts[:, 4:5], in1=x_res[:, t, :],
                                             op0=ALU.mult, op1=ALU.add).then_inc(s_x1, 1)

                dve.memset(mx_chunk[:], 0.0)
                step(dve.memset(mx_part[:], 0.0))
                token_stats((0,))
                normalise(0)
                for q in range(Q):
                    dve.wait_ge(s_mcopied, NMB // Q * (q + 1))
                    dve.tensor_reduce(mx_chunk[:, 0, 2 * q:2 * q + 2], mf[:, :, HU * q:HU * (q + 1), :].rearrange("p k h c -> p k (h c)"),
                                      AX_X, ALU.max, apply_absolute_value=True)
                xt_low(0, 0)
                dve.wait_ge(s_small, 48)
                dve.tensor_reduce(mx_part[:, 3:4], gate_w_s[:].rearrange("p k e -> p (k e)"), AX_X, ALU.max, apply_absolute_value=True)
                dve.wait_ge(s_call, 16)
                dve.tensor_reduce(mx_chunk[:, 2, 0:1], ctx_all, AX_X, ALU.max, apply_absolute_value=True)
                for q in range(Q):
                    dve.wait_ge(s_ncopied, H // 2 // Q * (q + 1))
                    last = dve.tensor_reduce(mx_chunk[:, 1, q:q + 1], nf[:, HU * q:HU * (q + 1), :].rearrange("p h d -> p (h d)"),
                                             AX_X, ALU.max, apply_absolute_value=True)
                step(last)
                dve.tensor_reduce(mx_part[:, 0:3], mx_chunk[:], AX_X, ALU.max).then_inc(s_mxp, 1)
                dve.wait_ge(s_maxt, 1)
                step(dve.tensor_reduce(mx_col[0:NM, :], banks[0:NM, 0, 0:P], AX_X, ALU.max))
                dve.wait_ge(s_ident, 3)
                dve.tensor_scalar(mx_diag[0:NM, :], ident[0:NM, 0:NM], mx_col[0:NM, 0:1], None, ALU.mult).then_inc(s_maxd, 1)
                dve.wait_ge(s_maxb, 1)
                step(dve.tensor_scalar(scale_of[:], banks[:, 1, 0:NM], 1e-30, 1e30, ALU.max, ALU.min))
                step(dve.tensor_scalar(mx_exp[:], scale_of[:].bitcast(I32), 0x7F800000, None, ALU.bitwise_and))
                step(dve.tensor_scalar(scale_of[:].bitcast(I32), mx_exp[:], -1.0, float((254 + TOP) << 23), ALU.mult, ALU.add))
                split_m(0)
                step(dve.tensor_scalar(inv_of[:].bitcast(I32), mx_exp[:], -float(TOP << 23), None, ALU.add))
                dve.wait_ge(s_tanh, 1)
                dve.tensor_scalar(consts[:, 2:3], inv_of[:, 0:1], inv_of[:, 2:3], 1.0 / XM_SCALE / LN_SCALE / float(C) ** 0.5, ALU.mult, ALU.mult).then_inc(s_factor, 1)
                step(dve.tensor_tensor(consts[:, 3:4], inv_of[:, 1:2], inv_of[:, 2:3], ALU.mult))
                step(dve.tensor_tensor(consts[:, 4:5], consts[:, 3:4], consts[:, 0:1], ALU.mult))
                dve.wait_ge(s_factor, 1)
                context(0, 0, 1)
                split_m(1)
                dve.tensor_scalar(gate_hi[:], gate_w_s[:], scale_of[:, 3:4], None, ALU.mult).then_inc(s_gate_w, 1)
                dve.wait_ge(s_gate_w, 1)
                dve.scalar_tensor_tensor(out=gate_lo[:], in0=gate_w_s[:], scalar=scale_of[:, 3:4], in1=gate_hi[:], op0=ALU.mult, op1=ALU.subtract)
                step(dve.tensor_scalar(consts[:, 6:7], inv_of[:, 3:4], 1.0 / LN_SCALE, None, ALU.mult))
                for h in range(HU):
                    xm_low(0, xm[0], h)

                def group(g, b, turn_next, first, last, experts):
                    for q in range(Q):
                        if q == 0:
                            dve.wait_ge(s_mbias, g + 1)
                            dve.wait_ge(s_manyof, g + 1)
                        unit(Q * g + q, g, b, q, xm[(q + 1) % 2], last and q == Q - 1, not first, experts, not last, turn_next)
                        if q == 0 and not first:
                            residual(g - 1)

                group(0, 0, 1, True, False, False)
                with nc.vector.Fori(0, (G - 2) // 2) as k:
                    group(1 + 2 * k, 1, k + 2, False, False, True)
                    group(2 + 2 * k, 0, k + 2, False, False, True)
                group(G - 1, 1, 0, False, True, False)
                dve.wait_ge(s_fwl, 48 * (E - EARLY))
                for i in range(E - EARLY):
                    for n in range(2):
                        m = dve.tensor_reduce(fm_late[:, 2 * i + n:2 * i + n + 1], late_gu_dn[i][n], AX_X, ALU.max, apply_absolute_value=True)
                m.then_inc(s_flate, 1)
                residual(G - 1)
                route_stats(dve, G - 1)

            @block.tensor
            def _(pe):
                def transposes(g):
                    pe.wait_ge(s_xnorm, g + 1)
                    for kc in range(KC):
                        for j in range(J):
                            mm = pe.transpose(tr_ps[:, kc, j * P:(j + 1) * P], xn[:, j, kc * P:(kc + 1) * P], ident[:])
                        mm.then_inc(s_xt, 1)

                pe.wait_ge(s_wk, 16)
                for i in range(NMB):
                    kc, hq = i % KC, i // KC
                    if i % (NMB // 2) == 0:
                        pe.wait_ge(s_wq[i // (NMB // 2)], 16)
                    if i >= 6:
                        pe.wait_ge(s_mcopied, i - 5)
                    for h in range(4 * hq, 4 * hq + 4):
                        mm = pe.matmul(product_bank(i)[:, (h % 4) * C:(h % 4 + 1) * C], wq_s[:, h, kc * P:(kc + 1) * P], wk_s[:, h // (H // KV), :],
                                       start=True, stop=True)
                    mm.then_inc(s_mprod, 1)
                pe.wait_ge(s_ident, 3)
                transposes(0)
                pe.wait_ge(s_wv, 16)
                pe.wait_ge(s_wo, 16)
                for i in range(H // 2):
                    n = NMB + i
                    if n - 6 < NMB:
                        pe.wait_ge(s_mcopied, n - 5)
                    else:
                        pe.wait_ge(s_ncopied, n - 5 - NMB)
                    for h in (2 * i, 2 * i + 1):
                        mm = pe.matmul(product_bank(n)[:, (h % 2) * D:(h % 2 + 1) * D], wv_s[:, h // (H // KV), :], wo_s[:, h, :], start=True, stop=True)
                    mm.then_inc(s_nprod, 1)
                pe.wait_ge(s_ncopied, H // 2)
                pe.wait_ge(s_mxp, 1)
                pe.transpose(banks[0:NM, 0, 0:P], mx_part[:], ident[:]).then_inc(s_maxt, 1)
                pe.wait_ge(s_maxd, 1)
                pe.matmul(banks[:, 1, 0:NM], ones[0:NM, :], mx_diag[0:NM, :], start=True, stop=True).then_inc(s_maxb, 1)

                def x_m(u, q, b):
                    for hh in range(HU):
                        if not (isinstance(u, int) and u < 2):
                            pe.wait_ge(s_ol, 4 * (u - 2) + hh + 1)
                        h = HU * q + hh
                        n = 0
                        for kc in range(KC):
                            for w, r in ((m_hi, xt_hi[b]), (m_hi, xt_lo[b]), (m_lo, xt_hi[b])):
                                mm = pe.matmul(xo_ps[:, hh, :], w[:, kc, h, :], r[:, kc, :], start=(n == 0), stop=(n == 3 * KC - 1))
                                n += 1
                        mm.then_inc(s_xm, 1)

                def scores(u, xm_u, b):
                    pe.wait_ge(s_xmd, HU * (u + 1))
                    if not (isinstance(u, int) and u < 1):
                        pe.wait_ge(s_pta, HP * u)
                    for hp in range(HP):
                        for bt in range(NB):
                            for n, (x, c) in enumerate(((xm_u[0], ctx_t_hi[b]), (xm_u[0], ctx_t_lo[b]), (xm_u[1], ctx_t_hi[b]))):
                                mm = pe.matmul(sp_ps[:, hp, bt * S:(bt + 1) * S], x[:, hp, :, bt, :].rearrange("p c t -> p (c t)"),
                                               c[:, bt * S:(bt + 1) * S], start=(n == 0), stop=(n == 2))
                        mm.then_inc(s_sc, 1)

                def project(u, q, js):
                    pe.wait_ge(s_oh, 4 * (u + 1))
                    pe.wait_ge(s_ol, 4 * (u + 1))
                    for j in js:
                        for hh in range(HU):
                            h = HU * q + hh
                            for n, (o, w) in enumerate(((o_hi, n_hi), (o_lo, n_hi), (o_hi, n_lo))):
                                mm = pe.matmul(acc[:, j, :], o[:, hh, j * P:(j + 1) * P], w[:, h, :],
                                               start=(h == 0 and n == 0 and j % 2 == 0), stop=(h == H - 1 and n == 2), skip_group_check=True)
                    if J - 1 in js:
                        mm.then_inc(s_on, 1)

                def probs_t(u):
                    for hp in range(HP):
                        pe.wait_ge(s_pnd if hp else s_pnp, u + 1)
                        for j in range(J):
                            mm = pe.transpose(sp_ps[:, hp, j * P:(j + 1) * P], pn[:, hp, j * P:(j + 1) * P], ident[:])
                        mm.then_inc(s_pt, 1)

                def head_outputs(u, b):
                    pe.wait_ge(s_pta, HP * (u + 1))
                    for half in range(2):
                        for jj in range(2):
                            j = 2 * half + jj
                            for b2 in range(2):
                                rows = slice(b2 * S, (b2 + 1) * S)
                                mm = pe.matmul(xo_ps[:, 2 * half + b2, jj * 256:(jj + 1) * 256], ctx_s[b][rows, j, :], pt[rows, j, :, :],
                                               start=True, stop=True)
                                if jj == 1:
                                    mm.then_inc(s_pv, 1)

                def group(g, b, first, last):
                    r = g - 1
                    for q in range(Q):
                        u = Q * g + q
                        more = not (last and q == Q - 1)
                        if q == 0:
                            pe.wait_ge(s_cscale, g + 1)
                        scores(u, xm[q % 2], b)
                        if more:
                            if first and q < Q - 1:
                                pe.wait_ge(s_msplit, q + 2)
                            x_m(u + 1, (q + 1) % Q, b if q < Q - 1 else 1 - b)
                        before = not (first and q == 0)
                        if q == 1 and not first:
                            pe.wait_ge(s_x1, g)
                        if first and before:
                            pe.wait_ge(s_nsplit, q)
                        if before:
                            project(u - 1, (q - 1) % Q, (0, 1))
                        if q == 1 and not last:
                            pe.wait_ge(s_xmd, HU * (u + 1) + 2)
                            transposes(g + 1)
                        if q == 2 and not first:
                            pe.wait_ge(s_xmd, HU * (u + 1) + 2)
                            route_transposes(pe, r)
                        if before:
                            project(u - 1, (q - 1) % Q, (2,))
                        probs_t(u)
                        if more and q >= 2:
                            pe.wait_ge(s_xmd, HU * (u + 1) + 3)
                        if q == 3 and not first:
                            route_positions(pe, r)
                        if before:
                            project(u - 1, (q - 1) % Q, (3,))
                        if q == 2 and not first:
                            route_logits(pe, r)
                        if more:
                            pe.wait_ge(s_xmd, HU * (u + 2))
                        if q == 1 and not last:
                            pe.wait_ge(s_xtl, g + 2)
                        if q == 2 and not first:
                            pe.wait_ge(s_l1, g)
                        if q == 3 and not first:
                            pe.wait_ge(s_posr, g)
                        head_outputs(u, b)

                pe.wait_ge(s_msplit, 1)
                pe.wait_ge(s_xtl, 1)
                pe.wait_ge(s_iota, IOTAS)
                pe.wait_ge(s_small, 48)
                x_m(0, 0, 0)
                group(0, 0, True, False)
                pe.wait_ge(s_nsplit, Q)
                with nc.tensor.Fori(0, (G - 2) // 2) as k:
                    group(1 + 2 * k, 1, False, False)
                    group(2 + 2 * k, 0, False, False)
                group(G - 1, 1, False, True)
                project(Q * G - 1, Q - 1, range(J))

        with nc.Block() as block:

            POOL_PIECES = ((0, 2), (1, 0), (1, 1))

            def tail(eng, experts):
                eng.wait_ge(s_tail, 1)
                for e in experts:
                    first = eng.value_load(tail_i[0:1, e:e + 1], min_val=0, max_val=E * REGION)
                    eng.dma_start(rows_dram[bass.ds(first, P), :], zero_row).then_inc(s_tailz, 16)

            @block.sync
            def _(sp):
                sp.wait_ge(s_zero, 2)
                sp.dma_start(rows_dram[E * REGION:E * REGION + P, :], zero_row).then_inc(s_tailz, 16)
                tail(sp, range(0, E // 2))
                sp.wait_ge(s_tailz, 16 * (E + 1))

            @block.gpsimd
            def _(pool):
                route_newton(pool, G - 1)
                pool.wait_ge(s_flate, 5)
                k = 0
                for i, n in POOL_PIECES:
                    full, hi, lo, factor, words = late_piece(i, n)
                    tmp = late_tmp[:, 0:words]
                    for out, a, b, op in ((tmp, full, factor.to_broadcast([P, words]), ALU.mult),
                                          (hi, tmp, c_one[:].to_broadcast([P, words]), ALU.mult), (lo, tmp, hi, ALU.subtract)):
                        k += 1
                        pool.tensor_tensor(out, a, b, op).then_inc(s_fpl, 1)
                        pool.wait_ge(s_fpl, k)
                route_scatter(pool, G - 1)
                pool.wait_ge(s_scat, 16 * 2 * TILES)

            @block.scalar
            def _(act):
                route_high(act, G - 1)
                route_exp(act, G - 1)
                act.wait_ge(s_zero, 2)
                tail(act, range(E // 2, E))

            @block.tensor
            def _(pe):
                route_transposes(pe, G - 1)
                route_logits(pe, G - 1)
                route_positions(pe, G - 1)

            @block.vector
            def _(dve):
                r = G - 1
                late = 1

                def late_step(make):
                    nonlocal late
                    late += 1
                    make(dve).then_inc(s_flate, 1)
                    dve.wait_ge(s_flate, late)

                def late_split(i, n):
                    full, hi, lo, factor, _ = late_piece(i, n)
                    late_step(lambda v: v.tensor_scalar(hi, full, factor, None, ALU.mult))
                    dve.scalar_tensor_tensor(out=lo, in0=full, scalar=factor, in1=hi, op0=ALU.mult, op1=ALU.subtract)

                n = 0

                def step(ins):
                    nonlocal n
                    n += 1
                    ins.then_inc(s_tab, 1)
                    dve.wait_ge(s_tab, n)

                dve.wait_ge(s_fam, EARLY + 1)
                powers_of_two(late_step, f_scale[:, EARLY:E, :].rearrange("p e n -> p (e n)"), f_inv[:, EARLY:E, :].rearrange("p e n -> p (e n)"),
                              f_exp[:], fm_late[:, 4:8])
                late_split(0, 0)
                late_split(0, 1)
                route_rows_first(dve, r)
                route_rows_second(dve, r)
                route_low(dve, r)
                route_shift(dve, r)
                route_weights(dve, r)
                route_choice(dve, r, 0)
                route_choice(dve, r, 1)
                dve.tensor_scalar(tile_scales[:, 0, :], f_inv[:, :, 0], 1.0 / LN_SCALE, None, ALU.mult)
                dve.tensor_scalar(tile_scales[:, 1, :], f_scale[:, :, 0], 2.0 ** -31 / LN_SCALE, None, ALU.mult)
                step(dve.tensor_tensor(tile_scales[:, 2, :], f_inv[:, :, 0], f_inv[:, :, 0], ALU.mult))
                step(dve.tensor_tensor(tile_scales[:, 2, :], tile_scales[:, 2, :], f_inv[:, :, 1], ALU.mult))
                step(dve.tensor_scalar(tile_scales[:, 2, :], tile_scales[:, 2, :], 2.0 ** 31, consts[:, 1:2], ALU.mult, ALU.mult))
                route_places(dve, r)

                dve.tensor_copy(tail_i[:], count[:]).then_inc(s_tail, 1)
                late_split(1, 2)
                step(dve.tensor_tensor(t_end[:], count[:], region0[:], ALU.subtract))
                step(dve.tensor_scalar(n_tiles_i[:], t_end[:], float(P - 1), None, ALU.add))
                step(dve.tensor_scalar(n_tiles_i[:], n_tiles_i[:], P.bit_length() - 1, None, ALU.logical_shift_right))
                step(dve.tensor_copy(n_tiles[:], n_tiles_i[:]))
                step(dve.tensor_copy(t_end[:], n_tiles[:]))
                for e in range(1, E):
                    step(dve.tensor_tensor(t_end[:, e:e + 1], t_end[:, e:e + 1], t_end[:, e - 1:e], ALU.add))
                step(dve.tensor_tensor(past, tile_iota[:].unsqueeze(2).to_broadcast([P, TF, E]), t_end[:].unsqueeze(1).to_broadcast([P, TF, E]), ALU.is_ge))
                step(dve.tensor_reduce(t_e, past, AX_X, ALU.add))
                step(dve.tensor_tensor(pick, past, n_tiles[:].unsqueeze(1).to_broadcast([P, TF, E]), ALU.mult))
                step(dve.tensor_reduce(t_s, pick, AX_X, ALU.add))
                step(dve.tensor_tensor(t_s, tile_iota[:], t_s, ALU.subtract))
                step(dve.tensor_scalar(t_row, t_e, float(E), float(P), ALU.is_lt, ALU.mult))
                step(dve.tensor_tensor(t_s, t_s, t_row, ALU.mult))
                step(dve.scalar_tensor_tensor(out=t_row[:], in0=t_e[:], scalar=float(REGION), in1=t_s[:], op0=ALU.mult, op1=ALU.add))
                dve.tensor_copy(t_row_i[:], t_row)
                step(dve.tensor_scalar(t_c, t_e, float(E - 1), None, ALU.min))
                step(dve.tensor_copy(t_e_i[:], t_c))

        at2 = (E - EARLY) * EW
        after = big[:, EARLY * EW:]

        def take2(words):
            nonlocal at2
            at2 += words
            assert at2 <= PH1 + AUX
            return after[:, at2 - words:at2]

        def halves(words, chunks):
            return take2(words // 2).bitcast(F16).rearrange("p (c n) -> p c n", c=chunks)

        xg = [take2(ROW) for _ in range(U)]
        xg_hi, xg_lo = ([halves(KC * P, KC) for _ in range(2)] for _ in range(2))
        silu_s = take2(F)
        inter = take2(NF * P)
        it_hi, it_lo = ([halves(NF * P, NF) for _ in range(2)] for _ in range(2))
        ys = [take2(D) for _ in range(U)]
        fin = [big[:, g * 2 * J * D:(g + 1) * 2 * J * D].rearrange("p (c j d) -> p c j d", c=2, j=J) for g in range(G)]

        s_xg = [sem(f"tile_rows_loaded{i}") for i in range(U)]
        s_yo = [sem(f"tile_output_stored{i}") for i in range(U)]
        s_zin = sem("inter_padding_zero")
        s_fac = sem("tile_factors_step")
        FAC = 8
        s_gt = sem("tile_transposed")
        s_gth = sem("tile_high_ready")
        s_gtl = sem("tile_low_ready")
        s_gate = sem("gate_done")
        s_up = sem("up_done")
        s_si = sem("silu_ready")
        s_in = sem("inter_ready")
        s_it = sem("inter_transposed")
        s_ith = sem("inter_high_ready")
        s_itl = sem("inter_low_ready")
        s_dn = sem("down_done")
        s_ys = sem("tile_output_ready")
        s_fin = [sem(f"expert_outputs_loaded{g}") for g in range(G)]
        s_add = sem("expert_outputs_added")
        s_sum = sem("group_summed")
        s_out = sem("out_stored")
        x_ps, g_ps, u_ps, i_ps, y_ps = (banks[:, i, :] for i in range(5))

        with nc.Block() as block:

            @block.sync
            def _(sp):
                def load(t, i, turn):
                    r = sp.value_load(t_row_i[0:1, bass.ds(t, 1)], min_val=0, max_val=E * REGION)
                    if turn is not None:
                        sp.wait_ge(s_yo[i], 16 * turn)
                    sp.dma_start(xg[i], rows_dram[bass.ds(r, P), :]).then_inc(s_xg[i], 16)

                for i in range(U):
                    load(i, i, None)
                with nc.sync.Fori(1, TF // U) as k:
                    for i in range(U):
                        load(k * U + i, i, k)
                for i in range(REST):
                    load(TF - REST + i, i, TF // U)

            @block.gpsimd
            def _(pool):
                def store(t, i):
                    pool.wait_ge(s_ys, t + 1)
                    pool.sem_inc(s_passed)
                    pool.indirect_dma_start(y_dram, bass.IndirectOffsetOnAxis(ap=xg[i][:, D + 1:D + 2].bitcast(I32), axis=0),
                                            ys[i], None, bounds_check=2 * B * T - 1, oob_is_err=False).then_inc(s_yo[i], 16)

                for i in range(U):
                    store(i, i)
                with nc.gpsimd.Fori(1, TF // U) as k:
                    for i in range(U):
                        store(k * U + i, i)
                for i in range(REST):
                    store(TF - REST + i, i)
                for i in range(U):
                    pool.wait_ge(s_yo[i], 16 * (TF // U + (1 if i < REST else 0)))

            @block.scalar
            def _(act):
                def high(t, i):
                    act.wait_ge(s_gt, t + 1)
                    act.activation(xg_hi[i % 2], x_ps[:, 0:KC * P].rearrange("p (k n) -> p k n", k=KC), ACT.Copy).then_inc(s_gth, 1)

                def inner_high(t, i):
                    act.wait_ge(s_it, t + 1)
                    act.activation(it_hi[i % 2], i_ps[:, 0:NF * P].rearrange("p (c n) -> p c n", c=NF), ACT.Copy).then_inc(s_ith, 1)

                def tile(t, i, first, last):
                    if not first:
                        act.wait_ge(s_in, t)
                    act.wait_ge(s_gate, t + 1)
                    act.activation(silu_s, g_ps[:, 0:F], ACT.Silu, scale=t_sc[0][:, bass.ds(t, 1)]).then_inc(s_si, 1)
                    if not first:
                        inner_high(t - 1, i - 1)
                    if not last:
                        high(t + 1, i + 1)

                high(0, 0)
                act.wait_ge(s_fac, 4)
                for i in range(U):
                    tile(i, i, i == 0, False)
                with nc.scalar.Fori(1, TF // U) as k:
                    for i in range(U):
                        tile(k * U + i, i, False, False)
                for i in range(REST):
                    tile(TF - REST + i, i, False, i == REST - 1)
                inner_high(TF - 1, REST - 1)

            @block.vector
            def _(dve):
                dve.memset(inter, 0.0).then_inc(s_zin, 1)
                dve.wait_ge(s_zin, 1)

                def low(t, i):
                    dve.wait_ge(s_gth, t + 1)
                    dve.tensor_tensor(xg_lo[i % 2], x_ps[:, 0:KC * P].rearrange("p (k n) -> p k n", k=KC), xg_hi[i % 2], ALU.subtract).then_inc(s_gtl, 1)

                def inner_low(t, i):
                    dve.wait_ge(s_ith, t + 1)
                    dve.tensor_tensor(it_lo[i % 2], i_ps[:, 0:NF * P].rearrange("p (c n) -> p c n", c=NF), it_hi[i % 2], ALU.subtract).then_inc(s_itl, 1)

                def output(t, i):
                    dve.wait_ge(s_dn, t + 1)
                    dve.tensor_scalar(ys[i % U], y_ps[:, 0:D], xg[i % U][:, D:D + 1], t_sc[2][:, bass.ds(t, 1)], ALU.mult, ALU.mult).then_inc(s_ys, 1)

                def tile(t, i, n, last):
                    if n > 0:
                        inner_low(t - 1, i - 1)
                    if not last:
                        low(t + 1, i + 1)
                    dve.wait_ge(s_si, t + 1)
                    dve.wait_ge(s_up, t + 1)
                    dve.scalar_tensor_tensor(out=inter[:, 0:F], in0=u_ps[:, 0:F], scalar=t_sc[1][:, bass.ds(t, 1)], in1=silu_s,
                                             op0=ALU.mult, op1=ALU.mult).then_inc(s_in, 1)
                    if n > 1:
                        output(t - 2, i - 2)

                n = 0

                def step(ins):
                    nonlocal n
                    n += 1
                    ins.then_inc(s_fac, 1)
                    dve.wait_ge(s_fac, n)

                step(dve.tensor_scalar(numbers[:], rev[:], -1.0, float(E), ALU.mult, ALU.add))
                step(dve.tensor_tensor(pick, t_c.unsqueeze(2).to_broadcast([P, TF, E]), numbers[:].unsqueeze(1).to_broadcast([P, TF, E]), ALU.is_equal))
                for i in range(3):
                    if i == 2:
                        low(0, 0)
                    step(dve.tensor_tensor(past, pick, tile_scales[:, i:i + 1, :].to_broadcast([P, TF, E]), ALU.mult))
                    step(dve.tensor_reduce(t_sc[i][:], past, AX_X, ALU.add))
                assert n == FAC
                for i in range(U):
                    tile(i, i, i, False)
                with nc.vector.Fori(1, TF // U) as k:
                    for i in range(U):
                        tile(k * U + i, i, 2, False)
                for i in range(REST):
                    tile(TF - REST + i, i, 2, i == REST - 1)
                inner_low(TF - 1, REST - 1)
                output(TF - 2, REST - 2)
                output(TF - 1, REST - 1)

            @block.tensor
            def _(pe):
                def rows_t(t, i, turn):
                    pe.wait_ge(s_xg[i], 16 * turn)
                    for kc in range(KC):
                        mm = pe.transpose(x_ps[:, kc * P:(kc + 1) * P], xg[i][:, kc * P:(kc + 1) * P], ident[:])
                    mm.then_inc(s_gt, 1)

                def product(ps, half, e, i):
                    n = 0
                    for kc in range(KC):
                        for xh, w in ((xg_hi, 0), (xg_lo, 0), (xg_hi, 1)):
                            mm = pe.matmul(ps[:, 0:F], xh[i % 2][:, kc, :], w_gu[:, e, kc, w, half * F:(half + 1) * F].rearrange("p a f -> p (a f)"),
                                           start=(n == 0), stop=(n == 3 * KC - 1))
                            n += 1
                    return mm

                def inner_t(t):
                    pe.wait_ge(s_in, t + 1)
                    for c in range(NF):
                        mm = pe.transpose(i_ps[:, c * P:(c + 1) * P], inter[:, c * P:(c + 1) * P], ident[:])
                    mm.then_inc(s_it, 1)

                def down(t, i, e, first):
                    pe.wait_ge(s_itl, t + 1)
                    if not first:
                        pe.wait_ge(s_ys, t)
                    n = 0
                    for c in range(NF):
                        for ih, w in ((it_hi, 0), (it_lo, 0), (it_hi, 1)):
                            mm = pe.matmul(y_ps[:, 0:D], ih[i % 2][:, c, :], w_dn[:, e, w, c, :].rearrange("p a d -> p (a d)"),
                                           start=(n == 0), stop=(n == 3 * NF - 1))
                            n += 1
                    mm.then_inc(s_dn, 1)

                def expert_of(t):
                    return bass.ds(pe.value_load(t_e_i[0:1, bass.ds(t, 1)], min_val=0, max_val=E - 1), 1)

                def tiles(t0, turn, first, last):
                    e = {}
                    e[0] = expert_of(t0)
                    many = REST if last else U
                    for i in range(many):
                        t = t0 + i
                        pe.wait_ge(s_gtl, t + 1)
                        product(g_ps, 0, e[i], i).then_inc(s_gate, 1)
                        if not (first and i == 0):
                            inner_t(t - 1)
                        if not (last and i == many - 1):
                            rows_t(t + 1, (i + 1) % U, turn + (i + 1) // U)
                        if i < 2 and not first:
                            e[i - 2] = expert_of(t - 2)
                        product(u_ps, 1, e[i], i).then_inc(s_up, 1)
                        if i < many - 1:
                            e[i + 1] = expert_of(t + 1)
                        if not (first and i < 2):
                            down(t - 2, i, e[i - 2], first and i == 2)
                    if last:
                        inner_t(TF - 1)
                        down(TF - 2, many - 2, e[many - 2], False)
                        down(TF - 1, many - 1, e[many - 1], False)

                rows_t(0, 0, 1)
                tiles(0, 1, True, False)
                with nc.tensor.Fori(1, TF // U) as k:
                    tiles(k * U, k + 1, False, False)
                tiles(TF - REST, TF // U + 1, False, True)

        with nc.Block() as block:

            def load_outputs(eng, c):
                for g in range(G):
                    eng.dma_start(fin[g][:, c], y_tiles[g, :, c]).then_inc(s_fin[g], 16)

            def store_out(eng, groups):
                for g in groups:
                    eng.wait_ge(s_sum, g + 1)
                    eng.dma_start(out_tiles[g], x_res[:, g * J:(g + 1) * J, :]).then_inc(s_out, 16)

            @block.sync
            def _(sp):
                load_outputs(sp, 0)
                store_out(sp, range(0, G, 2))

            @block.scalar
            def _(act):
                load_outputs(act, 1)
                store_out(act, range(1, G, 2))
                act.wait_ge(s_out, 16 * G)

            @block.vector
            def _(dve):
                for g in range(G):
                    dve.wait_ge(s_fin[g], 32)
                    t = slice(g * J, (g + 1) * J)
                    dve.tensor_tensor(fin[g][:, 0], fin[g][:, 0], fin[g][:, 1], ALU.add).then_inc(s_add, 1)
                    dve.wait_ge(s_add, g + 1)
                    dve.tensor_tensor(x_res[:, t, :], x_res[:, t, :], fin[g][:, 0], ALU.add).then_inc(s_sum, 1)


def kernel(**inputs):
    import numpy as _np
    import concourse.bacc as _bacc
    from concourse import mybir as _mybir
    from concourse.bass_utils import run_bass_kernel_spmd as _run

    a = {k: _np.asarray(v) for k, v in inputs.items()}
    vision = a["ctx_1024"]
    arrays = {
        "x": a["x"],
        "ctx": vision,
        "ctx_t": vision.reshape(-1, vision.shape[-1]).T,
        "mask": a["mask_BxS2_bf1"].view(_np.uint8),
        "g_xattn": a["g_xattn"],
        "g_ffn": a["g_ffn"],
        "wq_t": a["L0_xattn_Wq"].T,
        "wk_t": a["L0_xattn_Wk"].T,
        "wv_t": a["L0_xattn_Wv"].T,
        "wo": a["L0_xattn_Wo"],
        "gate_w_t": a["L0_ffn_gate_w"].T,
        "gate_b": a["L0_ffn_gate_b"],
        "expert_bias": a["L0_ffn_expert_bias"],
        "w_gu_t": a["L0_ffn_w_gate_up"].transpose(0, 2, 1),
        "w_down_t": a["L0_ffn_w_down"].transpose(0, 2, 1),
    }
    arrays = {f"in_{k}": _np.ascontiguousarray(v) for k, v in arrays.items()}
    nc = _bacc.Bacc("TRN2", target_bir_lowering=False, num_devices=1)
    args = [nc.dram_tensor(k, v.shape, _mybir.dt.from_np(v.dtype), kind="ExternalInput").ap() for k, v in arrays.items()]
    args.append(nc.dram_tensor("out_0", a["x"].shape, _mybir.dt.float32, kind="ExternalOutput").ap())
    bass_flamingo_gated_block(nc, *args)
    return _run(nc, [arrays], core_ids=[0]).results[0]["out_0"]
```
